# Optimizing a Trainium2 kernel written in Bass

```python
import numpy as np
import jax
import jax.numpy as jnp

def _softmax(x, axis=-1):
    return jax.nn.softmax(x, axis=axis)

def _gelu(x):
    return jax.nn.gelu(x, approximate=True)

def _silu(x):
    return jax.nn.silu(x)

def _sigmoid(x):
    return jax.nn.sigmoid(x)

def _layernorm(x, axis=-1, eps=1e-05):
    m = jnp.mean(x, axis=axis, keepdims=True)
    v = jnp.var(x, axis=axis, keepdims=True)
    return (x - m) / jnp.sqrt(v + eps)

def _scatter_add(tgt, idx, src, axis=0):
    return tgt.at[idx].add(src)

def _segment_sum(src, seg, n):
    return jax.ops.segment_sum(src, seg, n)
kernel_name = 'mk_vit_tower_cls_d1_tok_img256_r4_2c8682'

def setup_inputs(seed: int=0):
    np.random.seed(seed)
    _w = jnp.asarray

    def _rec_inputs():
        import jax
        import jax.numpy as jnp
        _rk = jax.random.key(seed)
        x = -0.000202321 + 1.00025 * jax.random.normal(jax.random.fold_in(_rk, 1), (16, 64, 56, 56), jnp.float32)
        cls_tok = 0.02 * jax.random.normal(jax.random.fold_in(_rk, 5), (1, 1, 64), jnp.float32)
        return (x, cls_tok)
    x, cls_tok = _rec_inputs()

    def _L0_tok_setup():
        import jax, jax.numpy as jnp
        import numpy as np
        B, C, H, W = (8, 64, 56, 56)
        K = 3

        def _unfold3x3(x):
            b, c, h, w = x.shape
            xp = jnp.pad(x, ((0, 0), (0, 0), (1, 1), (1, 1)))
            patches = jnp.stack([xp[:, :, i:i + h, j:j + w] for i in range(K) for j in range(K)], axis=2)
            return patches.reshape(b, c * K * K, h * w).transpose(0, 2, 1)
        key = jax.random.key(seed)
        ks = jax.random.split(key, 8)
        d = C * K * K
        s1 = 1.0 / np.sqrt(d)
        s2 = 1.0 / np.sqrt(C)
        return {'x': jax.random.normal(ks[0], (B, C, H, W), jnp.float32), 'W1': jax.random.uniform(ks[1], (d, C), jnp.float32, -s1, s1), 'b1': jax.random.uniform(ks[2], (C,), jnp.float32, -s1, s1), 'W2': jax.random.uniform(ks[3], (C, d), jnp.float32, -s2, s2), 'b2': jax.random.uniform(ks[4], (d,), jnp.float32, -s2, s2), 'W3': jax.random.uniform(ks[5], (d, C), jnp.float32, -s1, s1), 'b3': jax.random.uniform(ks[6], (C,), jnp.float32, -s1, s1)}
    _L0_tok_all = _L0_tok_setup()
    _L0_tok_in = {k: v for k, v in _L0_tok_all.items() if k in ('W1', 'b1', 'W2', 'b2', 'W3', 'b3')}
    del _L0_tok_all

    def _L0_attn_setup():
        import jax, jax.numpy as jnp
        import numpy as np
        P = 64
        H = 64
        L = 1024
        BATCH = 4
        A_MAX = 1.0

        def _binary_op(q_i, q_j):
            A_i, b_i = q_i
            A_j, b_j = q_j
            iA, iB, iC, iD = jnp.split(A_i, 4, axis=-1)
            jA, jB, jC, jD = jnp.split(A_j, 4, axis=-1)
            A_new = jnp.concatenate([jA * iA + jB * iC, jA * iB + jB * iD, jC * iA + jD * iC, jC * iB + jD * iD], axis=-1)
            b1, b2 = jnp.split(b_i, 2, axis=-1)
            b_new = jnp.concatenate([jA * b1 + jB * b2, jC * b1 + jD * b2], axis=-1)
            return (A_new, b_new + b_j)
        key = jax.random.key(seed)
        k_u, k_a, k_b, k_c, k_d, k_dt = jax.random.split(key, 6)
        inv_sqrt_h = 1.0 / np.sqrt(H)
        inv_sqrt_p = 1.0 / np.sqrt(P)
        return {'input_sequence': jax.random.normal(k_u, (BATCH, L, H), dtype=jnp.float32), 'A_diag': jax.random.uniform(k_a, (P,), dtype=jnp.float32) * A_MAX, 'B': jax.random.uniform(k_b, (P, H, 2), minval=-inv_sqrt_h, maxval=inv_sqrt_h, dtype=jnp.float32), 'C': jax.random.uniform(k_c, (H, P, 2), minval=-inv_sqrt_p, maxval=inv_sqrt_p, dtype=jnp.float32), 'D': jax.random.normal(k_d, (H,), dtype=jnp.float32), 'dt': jax.random.normal(k_dt, (P,), dtype=jnp.float32) * 0.5}
    _L0_attn_all = _L0_attn_setup()
    _L0_attn_in = {k: v for k, v in _L0_attn_all.items() if k in ('A_diag', 'B', 'C', 'D', 'dt')}
    del _L0_attn_all

    def _L0_ffn_setup():
        import jax, jax.numpy as jnp
        import numpy as np
        B, N, D = (16, 1024, 64)
        NUM_EXPERTS, TOP_K, HEADS = (4, 2, 4)
        N_EDGES = 262144
        LN_EPS = 1e-05

        def _layernorm(x, g, b):
            mu = x.mean(-1, keepdims=True)
            var = ((x - mu) ** 2).mean(-1, keepdims=True)
            return (x - mu) * jax.lax.rsqrt(var + LN_EPS) * g + b

        def _forward(x, edge_index, W_gat, att_src, att_dst, b_gat, ln_gamma, ln_beta, W1, b1, W2, b2):
            Bc, Nc, Dc = x.shape
            M = Bc * Nc
            x_flat = x.reshape(M, Dc)
            h = (x_flat @ W_gat).reshape(M, HEADS, NUM_EXPERTS)
            loops = jnp.arange(M, dtype=edge_index.dtype)
            src = jnp.concatenate([edge_index[0], loops])
            dst = jnp.concatenate([edge_index[1], loops])
            a_src = (h * att_src).sum(-1)
            a_dst = (h * att_dst).sum(-1)
            e = jax.nn.leaky_relu(a_src[src] + a_dst[dst], negative_slope=0.2)
            e_max = jax.ops.segment_max(e, dst, num_segments=M)
            ee = jnp.exp(e - e_max[dst])
            denom = jax.ops.segment_sum(ee, dst, num_segments=M)
            alpha = ee / (denom[dst] + 1e-16)
            msg = h[src] * alpha[:, :, None]
            agg = jax.ops.segment_sum(msg, dst, num_segments=M).reshape(M, HEADS * NUM_EXPERTS) + b_gat
            scores = _layernorm(agg, ln_gamma, ln_beta).reshape(M, HEADS, NUM_EXPERTS).mean(1)
            scores = scores.reshape(Bc, Nc, NUM_EXPERTS)
            topk_s, topk_i = jax.lax.top_k(scores, TOP_K)
            w = jax.nn.softmax(topk_s, axis=-1)
            out = jnp.zeros_like(x)
            for ei in range(NUM_EXPERTS):
                g = jnp.where(topk_i == ei, w, 0.0).sum(-1)
                hh = jax.nn.gelu(x @ W1[ei] + b1[ei], approximate=False)
                out = out + g[..., None] * (hh @ W2[ei] + b2[ei])
            return out
        key = jax.random.key(seed)
        ks = jax.random.split(key, 8)
        s = 0.05
        return {'x': jax.random.normal(ks[0], (B, N, D), jnp.float32), 'W_gat': jax.random.normal(ks[1], (D, HEADS * NUM_EXPERTS), jnp.float32) * s, 'att_src': jax.random.normal(ks[2], (HEADS, NUM_EXPERTS), jnp.float32) * s, 'att_dst': jax.random.normal(ks[3], (HEADS, NUM_EXPERTS), jnp.float32) * s, 'b_gat': jnp.zeros((HEADS * NUM_EXPERTS,), jnp.float32), 'ln_gamma': jnp.ones((HEADS * NUM_EXPERTS,), jnp.float32), 'ln_beta': jnp.zeros((HEADS * NUM_EXPERTS,), jnp.float32), 'W1': jax.random.normal(ks[4], (NUM_EXPERTS, D, 2 * D), jnp.float32) * s, 'b1': jnp.zeros((NUM_EXPERTS, 2 * D), jnp.float32), 'W2': jax.random.normal(ks[5], (NUM_EXPERTS, 2 * D, D), jnp.float32) * s, 'b2': jnp.zeros((NUM_EXPERTS, D), jnp.float32), 'edge_index': jax.random.randint(ks[6], (2, N_EDGES), 0, B * N, jnp.int32)}
    _L0_ffn_all = _L0_ffn_setup()
    _L0_ffn_in = {k: v for k, v in _L0_ffn_all.items() if k in ('W_gat', 'att_src', 'att_dst', 'b_gat', 'ln_gamma', 'ln_beta', 'W1', 'b1', 'W2', 'b2', 'edge_index')}
    del _L0_ffn_all
    return {'x': x, 'cls_tok': cls_tok, 'L0_tok_W1': _L0_tok_in['W1'], 'L0_tok_b1': _L0_tok_in['b1'], 'L0_tok_W2': _L0_tok_in['W2'], 'L0_tok_b2': _L0_tok_in['b2'], 'L0_tok_W3': _L0_tok_in['W3'], 'L0_tok_b3': _L0_tok_in['b3'], 'L0_attn_A_diag': _L0_attn_in['A_diag'], 'L0_attn_B': _L0_attn_in['B'], 'L0_attn_C': _L0_attn_in['C'], 'L0_attn_D': _L0_attn_in['D'], 'L0_attn_dt': _L0_attn_in['dt'], 'L0_ffn_W_gat': _L0_ffn_in['W_gat'], 'L0_ffn_att_src': _L0_ffn_in['att_src'], 'L0_ffn_att_dst': _L0_ffn_in['att_dst'], 'L0_ffn_b_gat': _L0_ffn_in['b_gat'], 'L0_ffn_ln_gamma': _L0_ffn_in['ln_gamma'], 'L0_ffn_ln_beta': _L0_ffn_in['ln_beta'], 'L0_ffn_W1': _L0_ffn_in['W1'], 'L0_ffn_b1': _L0_ffn_in['b1'], 'L0_ffn_W2': _L0_ffn_in['W2'], 'L0_ffn_b2': _L0_ffn_in['b2'], 'L0_ffn_edge_index': _L0_ffn_in['edge_index']}

def reference(x, cls_tok, L0_tok_W1, L0_tok_b1, L0_tok_W2, L0_tok_b2, L0_tok_W3, L0_tok_b3, L0_attn_A_diag, L0_attn_B, L0_attn_C, L0_attn_D, L0_attn_dt, L0_ffn_W_gat, L0_ffn_att_src, L0_ffn_att_dst, L0_ffn_b_gat, L0_ffn_ln_gamma, L0_ffn_ln_beta, L0_ffn_W1, L0_ffn_b1, L0_ffn_W2, L0_ffn_b2, L0_ffn_edge_index):
    import jax
    import jax.numpy as jnp

    def _L0_tok_ref(x, W1, b1, W2, b2, W3, b3):
        import jax, jax.numpy as jnp
        import numpy as np
        B, C, H, W = (8, 64, 56, 56)
        K = 3

        def _unfold3x3(x):
            b, c, h, w = x.shape
            xp = jnp.pad(x, ((0, 0), (0, 0), (1, 1), (1, 1)))
            patches = jnp.stack([xp[:, :, i:i + h, j:j + w] for i in range(K) for j in range(K)], axis=2)
            return patches.reshape(b, c * K * K, h * w).transpose(0, 2, 1)
        t = _unfold3x3(x)
        h1 = jax.nn.relu(jnp.einsum('bld,dc->blc', t, W1) + b1)
        s = jax.nn.sigmoid(jnp.einsum('blc,cd->bld', h1, W2) + b2)
        out = jnp.einsum('bld,dc->blc', t * s, W3) + b3
        return out

    def _L0_attn_ref(input_sequence, A_diag, B, C, D, dt):
        import jax, jax.numpy as jnp
        import numpy as np
        P = 64
        H = 64
        L = 1024
        BATCH = 4
        A_MAX = 1.0

        def _binary_op(q_i, q_j):
            A_i, b_i = q_i
            A_j, b_j = q_j
            iA, iB, iC, iD = jnp.split(A_i, 4, axis=-1)
            jA, jB, jC, jD = jnp.split(A_j, 4, axis=-1)
            A_new = jnp.concatenate([jA * iA + jB * iC, jA * iB + jB * iD, jC * iA + jD * iC, jC * iB + jD * iD], axis=-1)
            b1, b2 = jnp.split(b_i, 2, axis=-1)
            b_new = jnp.concatenate([jA * b1 + jB * b2, jC * b1 + jD * b2], axis=-1)
            return (A_new, b_new + b_j)
        B_c = B[..., 0] + 1j * B[..., 1]
        C_c = C[..., 0] + 1j * C[..., 1]
        dts = jax.nn.sigmoid(dt)
        Ad = jax.nn.relu(A_diag)
        S = 1.0 + dts ** 2 * Ad
        M11 = 1.0 - dts ** 2 * Ad / S
        M12 = -dts * Ad / S
        M21 = dts / S
        M22 = 1.0 / S
        M = jnp.concatenate([M11, M12, M21, M22])

        def single(u):
            Bu = u.astype(B_c.dtype) @ B_c.T
            M_el = jnp.broadcast_to(M, (u.shape[0], 4 * Ad.shape[0]))
            F = jnp.concatenate([M11 * Bu * dts, M21 * Bu * dts], axis=-1)
            _, xs = jax.lax.associative_scan(_binary_op, (M_el, F))
            ys = xs[:, Ad.shape[0]:]
            return (ys @ C_c.T).real + D * u
        return jax.vmap(single)(input_sequence)

    def _L0_ffn_ref(x, W_gat, att_src, att_dst, b_gat, ln_gamma, ln_beta, W1, b1, W2, b2, edge_index):
        import jax, jax.numpy as jnp
        import numpy as np
        B, N, D = (16, 1024, 64)
        NUM_EXPERTS, TOP_K, HEADS = (4, 2, 4)
        N_EDGES = 262144
        LN_EPS = 1e-05

        def _layernorm(x, g, b):
            mu = x.mean(-1, keepdims=True)
            var = ((x - mu) ** 2).mean(-1, keepdims=True)
            return (x - mu) * jax.lax.rsqrt(var + LN_EPS) * g + b

        def _forward(x, edge_index, W_gat, att_src, att_dst, b_gat, ln_gamma, ln_beta, W1, b1, W2, b2):
            Bc, Nc, Dc = x.shape
            M = Bc * Nc
            x_flat = x.reshape(M, Dc)
            h = (x_flat @ W_gat).reshape(M, HEADS, NUM_EXPERTS)
            loops = jnp.arange(M, dtype=edge_index.dtype)
            src = jnp.concatenate([edge_index[0], loops])
            dst = jnp.concatenate([edge_index[1], loops])
            a_src = (h * att_src).sum(-1)
            a_dst = (h * att_dst).sum(-1)
            e = jax.nn.leaky_relu(a_src[src] + a_dst[dst], negative_slope=0.2)
            e_max = jax.ops.segment_max(e, dst, num_segments=M)
            ee = jnp.exp(e - e_max[dst])
            denom = jax.ops.segment_sum(ee, dst, num_segments=M)
            alpha = ee / (denom[dst] + 1e-16)
            msg = h[src] * alpha[:, :, None]
            agg = jax.ops.segment_sum(msg, dst, num_segments=M).reshape(M, HEADS * NUM_EXPERTS) + b_gat
            scores = _layernorm(agg, ln_gamma, ln_beta).reshape(M, HEADS, NUM_EXPERTS).mean(1)
            scores = scores.reshape(Bc, Nc, NUM_EXPERTS)
            topk_s, topk_i = jax.lax.top_k(scores, TOP_K)
            w = jax.nn.softmax(topk_s, axis=-1)
            out = jnp.zeros_like(x)
            for ei in range(NUM_EXPERTS):
                g = jnp.where(topk_i == ei, w, 0.0).sum(-1)
                hh = jax.nn.gelu(x @ W1[ei] + b1[ei], approximate=False)
                out = out + g[..., None] * (hh @ W2[ei] + b2[ei])
            return out
        return _forward(x, edge_index, W_gat, att_src, att_dst, b_gat, ln_gamma, ln_beta, W1, b1, W2, b2)
    h = _L0_tok_ref(x, L0_tok_W1, L0_tok_b1, L0_tok_W2, L0_tok_b2, L0_tok_W3, L0_tok_b3)
    h = jnp.concatenate([jnp.broadcast_to(cls_tok, (h.shape[0], 1, h.shape[2])), h], axis=1)
    h = h + _L0_attn_ref(_layernorm(h, axis=-1), L0_attn_A_diag, L0_attn_B, L0_attn_C, L0_attn_D, L0_attn_dt)
    h = h + _L0_ffn_ref(_layernorm(h, axis=-1), L0_ffn_W_gat, L0_ffn_att_src, L0_ffn_att_dst, L0_ffn_b_gat, L0_ffn_ln_gamma, L0_ffn_ln_beta, L0_ffn_W1, L0_ffn_b1, L0_ffn_W2, L0_ffn_b2, L0_ffn_edge_index)
    return h

_drawn_inputs = setup_inputs


def setup_inputs(seed=0):
    import zlib

    import numpy as np

    out = dict(_drawn_inputs(seed))
    spreads = {'L0_ffn_b_gat': (0.0, 0.8),
     'L0_ffn_ln_gamma': (1.0, 0.6),
     'L0_ffn_ln_beta': (0.0, 0.8),
     'L0_ffn_b1': (0.0, 0.8),
     'L0_ffn_b2': (0.0, 0.8)}
    factors = {'L0_tok_b1': 8.0,
     'L0_ffn_W_gat': 6.455,
     'L0_ffn_att_src': 8.0,
     'L0_ffn_att_dst': 8.0,
     'L0_ffn_W1': 5.213,
     'L0_ffn_W2': 4.894}
    for name, (base, spread) in spreads.items():
        noise = np.random.default_rng([zlib.crc32(name.encode()), seed]).standard_normal(out[name].shape)
        drawn = base * np.exp(spread * noise) if base else spread * noise
        out[name] = jnp.asarray(drawn.astype(out[name].dtype))
    for name, factor in factors.items():
        out[name] = (out[name] * factor).astype(out[name].dtype)
    return out
```

```python
import concourse.bass as bass
from concourse import mybir
from contextlib import ExitStack

f32 = mybir.dt.float32
i32 = mybir.dt.int32
bf16 = mybir.dt.bfloat16
ALU = mybir.AluOpType
ACT = mybir.ActivationFunctionType
AX = mybir.AxisListType

IMAGES, CH, SIDE = 16, 64, 56
TOKENS = SIDE * SIDE
SEQ = TOKENS + 1
NODES = IMAGES * SEQ
ROWS = 8
CHUNK = ROWS * SIDE
CHUNKS = TOKENS // CHUNK
STEPS = CHUNK + 1
PAD = SIDE + 2
TAPS = 9
TAP_TILES = [(0, 1), (3, 4), (6, 7), (2, 5), (8,)]
FOLD = 4
FP = CHUNK // FOLD
HEADS, EXPERTS = 4, 4
HE = HEADS * EXPERTS
HIDDEN = 128
TW = HE + 2 * HEADS
GRAPH_NODES = 16 * 1024
EDGES = 262144
P = 128
LO = P
ETILES = EDGES // P
SORTED = EDGES + GRAPH_NODES
SCOLS = SORTED // P
HALF = 16
EROUNDS = ETILES // (2 * HALF)
SROUNDS = LO // (2 * HALF)
GROUP = 4
FLAG = 65536
BIG = 1.0e30
EPS = 1e-5
DENOM_EPS = 1e-16
GRAPH_IMAGES = -(-GRAPH_NODES // SEQ)
NT = 512
NCH = NODES // NT


def build(nc, x, cls_tok, tokW1, tokb1, tokW2, tokb2, tokW3, tokb3, A_diag, Bmat, Cmat, Dvec, dtv,
          W_gat, att_src, att_dst, b_gat, ln_gamma, ln_beta, W1, b1, W2, b2, edges, out):
    sorted_rec = nc.dram_tensor("sorted_rec", [SORTED, 2], i32, kind="Internal").ap()
    gathered = nc.dram_tensor("gathered", [P, SCOLS * TW], f32, kind="Internal").ap()
    table = nc.dram_tensor("table", [NODES, TW], f32, kind="Internal").ap()
    h_tok = nc.dram_tensor("h_tok", [NODES, CH], f32, kind="Internal").ap()
    xnT = nc.dram_tensor("xnT", [CH, NODES], f32, kind="Internal").ap()
    seg_scratch = nc.dram_tensor("seg_scratch", [2, P, P], i32, kind="Internal").ap()

    front(nc, x, cls_tok, tokW1, tokb1, tokW2, tokb2, tokW3, tokb3, A_diag, Bmat, Cmat, Dvec, dtv,
          W_gat, att_src, att_dst, edges, sorted_rec, gathered, table, h_tok, xnT, seg_scratch)
    back(nc, table, gathered, sorted_rec, seg_scratch, h_tok, xnT, b_gat, ln_gamma, ln_beta,
         W1, b1, W2, b2, out)


def front(nc, x, cls_tok, tokW1, tokb1, tokW2, tokb2, tokW3, tokb3, A_diag, Bmat, Cmat, Dvec, dtv,
          W_gat, att_src, att_dst, edges, sorted_rec, gathered, table, h_tok, xnT, seg_scratch):
    ctx = ExitStack()
    with ctx:
        def sb(name, shape, dt=f32):
            return ctx.enter_context(nc.sbuf_tensor(name, shape, dt))

        def pb(name, shape, dt=f32):
            return ctx.enter_context(nc.psum_tensor(name, shape, dt))

        def sem(name):
            return ctx.enter_context(nc.semaphore(name))

        ident = sb("ident", [P, P])
        ident_b = sb("ident_b", [P, P], bf16)
        before = sb("before", [P, P])
        above = sb("above", [P, P])
        iota_i = sb("iota_i", [P, P], i32)
        iota_f = sb("iota_f", [P, P])
        iota_b = sb("iota_b", [P, P], bf16)
        part_i = sb("part_i", [P, 1], i32)
        part_f = sb("part_f", [P, 1])
        zero_b = sb("zero_b", [P, NT], bf16)
        zero_f = sb("zero_f", [P, P])
        center = sb("center", [CH, CH])
        mean = sb("mean", [CH, CH])
        eps_c = sb("eps_c", [P, 1])

        arena = sb("arena", [P, ETILES * 9 // 2])
        at = [0]

        def carve(n, dt=f32):
            words = n if dt != bf16 else n // 2
            v = arena[:, at[0]:at[0] + words]
            at[0] += words
            return v if dt == f32 else v.bitcast(dt)

        src_i = carve(ETILES, i32)
        dst_f = carve(ETILES)
        lo_f = carve(ETILES)
        lo_b = carve(ETILES, bf16)
        hi_b = carve(ETILES, bf16)
        hi128_b = carve(ETILES, bf16)
        tabs = [arena[:, n * STEPS:(n + 1) * STEPS] for n in range(4)]
        tab_a, tab_b, tab_k, tab_c = tabs

        xa = [sb(f"xa{n}", [P, PAD * PAD]) for n in range(2)]
        xb = [sb(f"xb{n}", [P, PAD * PAD]) for n in range(2)]
        dst_i = xa[0][:, 0:ETILES].bitcast(i32)
        tmp_i = xb[0][:, 0:ETILES].bitcast(i32)
        oh_hi = sb("oh_hi", [P, GROUP * P], bf16)
        oh_lo = sb("oh_lo", [P, GROUP * P], bf16)
        hiT = sb("hiT", [P, GROUP * P])
        hist = sb("hist", [P, GROUP * P])
        sort_junk = sb("sort_junk", [P, P])
        rank = sb("rank", [P, HALF])
        first = sb("first", [P, HALF])
        pos = [sb(f"pos{n}", [P, HALF], i32) for n in range(2)]
        rec = [sb(f"rec{n}", [P, HALF, 2], i32) for n in range(2)]
        counts = sb("counts", [P, GROUP * P])
        deg = sb("deg", [P, P])
        incl = sb("incl", [P, P])
        base = sb("base", [P, P])
        rowbase = sb("rowbase", [P, 1])
        seg_i = sb("seg_i", [P, 2, P], i32)
        node_f = sb("node_f", [P, P])
        node_flag = sb("node_flag", [P, P])
        base_i = seg_i[:, 0, :]
        pick = [sb(f"pick{n}", [P, HALF, 2], i32) for n in range(2)]
        ring = [sb(f"ring{n}", [P, HALF, TW]) for n in range(2)]

        NTT = len(TAP_TILES)
        w1 = sb("w1", [P, NTT, CH])
        w2 = sb("w2", [CH, TAPS * CH])
        w3 = sb("w3", [P, NTT, CH])
        tb1 = sb("tb1", [CH, 1])
        tb2 = sb("tb2", [P, NTT])
        tb3 = sb("tb3", [CH, 1])
        b_sb = sb("b_sb", [CH, 2 * CH])
        c_sb = sb("c_sb", [2 * CH, CH])
        d_sb = sb("d_sb", [CH, 1])
        cls_c = sb("cls_c", [CH, 1])
        adiag = sb("adiag", [P, 1])
        dts = sb("dts", [P, 1])
        wproj = sb("wproj", [CH, TW])
        att_bc = sb("att_bc", [CH, 2, HE])
        wtmp = sb("wtmp", [CH, 2, HE])
        par = sb("par", [P, 16])

        h1 = sb("h1", [CH, CHUNK])
        gate = [sb(f"gate{n}", [P, CHUNK]) for n in range(2)]
        prod = sb("prod", [P, NTT, CHUNK])
        hT = [sb(f"hT{n}", [CH, TOKENS]) for n in range(2)]
        sq = [sb(f"sq{n}", [CH, CHUNK]) for n in range(2)]
        std = [sb(f"std{n}", [CH, CHUNK]) for n in range(2)]
        u = [sb(f"u{n}", [CH, CHUNK]) for n in range(2)]
        fin = [sb(f"fin{n}", [P, CHUNK]) for n in range(2)]
        wst = [sb(f"wst{n}", [P, CHUNK]) for n in range(2)]
        y = sb("y", [P, CHUNK])
        carry = sb("carry", [P, 2])
        start = sb("start", [P, 2])
        h2 = [sb(f"h2{n}", [CH, CHUNK]) for n in range(2)]
        xn = [sb(f"xn{n}", [CH, CHUNK]) for n in range(2)]
        t_out = [sb(f"t_out{n}", [P, FOLD, TW]) for n in range(2)]
        h_out = [sb(f"h_out{n}", [P, FOLD, CH]) for n in range(2)]

        bank = [pb(f"bank{n}", [P, 512]) for n in range(8)]
        p_hi, p_dst, p_hist, p_first = bank[0:4]

        names = """consts weights_in edges_in ids_ready groups_oh hist_added counts_done totals_ready
            rowbase_done base_ready ids_bcast hiT_ready hist_copied first_done first_read
            oh_used group_pos pos_ready rec_ready scat0 scat1 sorted_done tabs_ready pads_zero
            x_in conv_done h1_done s_ps gate_done prod_done tok_done hT_done cent_done sq_done
            var_done std_done u_done bu_done y_done co_done h2_done cent2_done sq2_done var2_done
            std2_done xn_done tm_done tm_copied fin_read
            tm_st0 tm_st1 pick0 pick1 gath0 gath1 ring_st0 ring_st1 seg_st cls_in cls_ps cls_sb
            cls_st wp1 par_act par_dve waited""".split()
        S = {n: sem(n) for n in names}
        scat = [S["scat0"], S["scat1"]]
        pick_in = [S["pick0"], S["pick1"]]
        gath = [S["gath0"], S["gath1"]]
        ring_st = [S["ring_st0"], S["ring_st1"]]
        tm_st = [S["tm_st0"], S["tm_st1"]]

        src_v = edges[0, :].rearrange("(p t) -> p t", t=ETILES)
        dst_v = edges[1, :].rearrange("(p t) -> p t", t=ETILES)
        sorted_v = sorted_rec.rearrange("(p c) w -> p c w", c=SCOLS)

        def tile_rows(t):
            return CH * len(TAP_TILES[t])

        def taps_view(buf, c, t):
            src = xa if t < 3 else xb
            row, col = [(0, 0), (1, 0), (2, 0), (0, 2), (2, 2)][t]
            v = src[buf][0:tile_rows(t), :].rearrange("p (r q) -> p r q", q=PAD)
            return v[:, ROWS * c + row:ROWS * c + row + ROWS, col:col + SIDE]

        def r3(ap):
            return ap.rearrange("p (r q) -> p r q", q=SIDE)

        WEIGHT_LOADS = 3 * NTT + 14

        def steps(eng, step):
            step(0, 0, None, None)
            with eng.Fori(0, IMAGES // 2 - 1) as i:
                step(2 * i + 1, 1, 2 * i, 0)
                step(2 * i + 2, 0, 2 * i + 1, 1)
            step(IMAGES - 1, 1, IMAGES - 2, 0)
            step(None, None, IMAGES - 1, 1)

        block = ctx.enter_context(nc.Block())

        @block.sync
        def _(sp):
            sp.dma_start(dst_i, dst_v).then_inc(S["edges_in"], 16)
            sp.dma_start(src_i, src_v).then_inc(S["edges_in"], 16)
            n = [0]

            def w(dst, src):
                n[0] += 1
                sp.dma_start(dst, src).then_inc(S["weights_in"], 16)

            row = 0
            for t in range(NTT):
                k = tile_rows(t)
                w(w1[0:k, t, :], tokW1[row:row + k, :])
                w(w3[0:k, t, :], tokW3[row:row + k, :])
                row += k
            w(w2[:, :], tokW2)
            w(tb1[:, :], tokb1)
            for t in range(NTT):
                w(tb2[0:tile_rows(t), t:t + 1], tokb2[t * P:t * P + tile_rows(t), :])
            w(tb3[:, :], tokb3)
            w(b_sb[:, :], Bmat)
            w(c_sb[:, :], Cmat)
            w(d_sb[:, :], Dvec)
            for g in range(2):
                w(adiag[g * CH:(g + 1) * CH, :], A_diag)
                w(dts[g * CH:(g + 1) * CH, :], dtv)
            w(wproj[:, 0:HE], W_gat)
            w(att_bc[:, 0, :], att_src.partition_broadcast(CH))
            w(att_bc[:, 1, :], att_dst.partition_broadcast(CH))
            w(cls_c[:, :], cls_tok)
            assert n[0] == WEIGHT_LOADS

            sp.wait_ge(S["base_ready"], 1)
            sp.dma_start(seg_scratch.rearrange("a p q -> p a q"), seg_i[:, :, :]).then_inc(S["seg_st"], 16)
            sp.wait_ge(S["cls_sb"], 8)
            for dst, s in ((table.rearrange("(b s) w -> b s w", s=SEQ)[:, 0, :], t_out[0][0:IMAGES, 0, :]),
                           (h_tok.rearrange("(b s) w -> b s w", s=SEQ)[:, 0, :], h_out[0][0:IMAGES, 0, :]),
                           (xnT.rearrange("c (b s) -> c b s", s=SEQ)[:, :, 0:1], xn[0][:, 0:IMAGES].unsqueeze(2))):
                sp.dma_start(dst, s, allow_slow_non_contiguous=True).then_inc(S["cls_st"], 16)
            sp.wait_ge(S["cls_st"], 48)

            def load_image(b, buf):
                src = x[b, :, :, :]
                va = xa[buf][:, :].rearrange("p (r q) -> p r q", q=PAD)
                vb = xb[buf][:, :].rearrange("p (r q) -> p r q", q=PAD)
                sp.dma_start(va[0:CH, 1:1 + SIDE, 1:1 + SIDE], src).then_inc(S["x_in"], 16)
                sp.dma_start(va[CH:P, 1:1 + SIDE, 0:SIDE], src).then_inc(S["x_in"], 16)
                sp.dma_start(vb[0:CH, 1:1 + SIDE, 1:1 + SIDE], src).then_inc(S["x_in"], 16)
                sp.dma_start(vb[CH:P, 0:SIDE, 1:1 + SIDE], src).then_inc(S["x_in"], 16)

            def store_chunk(b, c, par_b):
                q = (par_b * CHUNKS + c) % 2
                sp.wait_ge(S["tm_copied"], 2 * (b * CHUNKS + c) + 2)
                sp.sem_inc(S["waited"], 1)
                node = b * SEQ + 1 + c * CHUNK
                sp.dma_start(table[bass.ds(node, CHUNK), :].rearrange("(p j) w -> p j w", j=FOLD),
                             t_out[q][0:FP, :, :]).then_inc(tm_st[q], 16)
                sp.dma_start(h_tok[bass.ds(node, CHUNK), :].rearrange("(p j) w -> p j w", j=FOLD),
                             h_out[q][0:FP, :, :]).then_inc(tm_st[q], 16)
                sp.dma_start(xnT[:, bass.ds(node, CHUNK)], xn[q][:, :]).then_inc(tm_st[q], 16)

            sp.wait_ge(S["pads_zero"], 1)
            load_image(0, 0)

            def loads_and_stores(b_tok, tok_par, b_att, att_par):
                if b_tok is not None and not (isinstance(b_tok, int) and b_tok == IMAGES - 1):
                    sp.wait_ge(S["x_in"], 64 * (b_tok + 1))
                    sp.sem_inc(S["waited"], 1)
                    if not (isinstance(b_tok, int) and b_tok == 0):
                        sp.wait_ge(S["prod_done"], 5 * CHUNKS * b_tok)
                        sp.sem_inc(S["waited"], 1)
                        sp.wait_ge(S["conv_done"], CHUNKS * b_tok)
                    sp.sem_inc(S["waited"], 1)
                    load_image(b_tok + 1, 1 - tok_par)
                if b_att is not None:
                    for c in range(CHUNKS):
                        store_chunk(b_att, c, att_par)

            steps(sp, loads_and_stores)
            sp.wait_ge(S["seg_st"], 16)
            for q in range(2):
                sp.wait_ge(tm_st[q], 48 * CHUNKS * IMAGES // 2)

        @block.gpsimd
        def _(pool):
            g = nc.gpsimd
            g.memset(ident[:, :], 0.0)
            g.memset(before[:, :], 1.0)
            g.memset(above[:, :], 1.0)
            g.memset(zero_f[:, :], 0.0)
            g.memset(zero_b[:, :], 0.0)
            g.memset(mean[:, :], 1.0 / CH)
            g.memset(center[:, :], -1.0 / CH)
            g.memset(eps_c[:, :], EPS)
            g.iota(iota_i[:, :], pattern=[[1, P]], base=0, channel_multiplier=0)
            g.iota(part_i[:, :], pattern=[[1, 1]], base=0, channel_multiplier=1)
            g.drain()
            g.affine_select(out=ident[:, :], in_=ident[:, :], compare_op=ALU.not_equal, fill=1.0, base=0,
                            pattern=[[-1, P]], channel_multiplier=1)
            g.affine_select(out=before[:, :], in_=before[:, :], compare_op=ALU.is_gt, fill=0.0, base=0,
                            pattern=[[-1, P]], channel_multiplier=1)
            g.affine_select(out=above[:, :], in_=above[:, :], compare_op=ALU.is_gt, fill=0.0, base=0,
                            pattern=[[1, P]], channel_multiplier=-1)
            g.affine_select(out=center[:, :], in_=center[:, :], compare_op=ALU.not_equal,
                            fill=1.0 - 1.0 / CH, base=0, pattern=[[-1, CH]], channel_multiplier=1)
            g.drain()
            g.nop().then_inc(S["consts"], 1)

            with pool.Fori(0, EROUNDS + SROUNDS) as i:
                for h in range(2):
                    pool.wait_ge(S["pos_ready"], 2 * i + h + 1)
                    pool.wait_ge(S["rec_ready"], 2 * i + h + 1)
                    pool.sem_inc(S["waited"], 1)
                    for j in range(HALF):
                        g.indirect_dma_start(
                            out=sorted_rec, out_offset=bass.IndirectOffsetOnAxis(ap=pos[h][:, j:j + 1], axis=0),
                            in_=rec[h][:, j, :], in_offset=None).then_inc(scat[h], 16)
            for h in range(2):
                pool.wait_ge(scat[h], 16 * HALF * (EROUNDS + SROUNDS))
            pool.wait_ge(S["cls_st"], 48)
            for q in range(2):
                pool.wait_ge(tm_st[q], 48 * CHUNKS * GRAPH_IMAGES // 2)

            ROUNDS = SCOLS // (2 * HALF)

            def load_pick(col, h):
                g.dma_start(pick[h][:, :, :], sorted_v[:, bass.ds(col, HALF), :]).then_inc(pick_in[h], 16)

            def gather_half(i, h):
                pool.wait_ge(pick_in[h], 16 * (i + 1))
                pool.sem_inc(S["waited"], 1)
                for j in range(HALF):
                    g.indirect_dma_start(
                        out=ring[h][:, j, :], out_offset=None, in_=table[0:GRAPH_NODES, :],
                        in_offset=bass.IndirectOffsetOnAxis(ap=pick[h][:, j, 0:1], axis=0)).then_inc(gath[h], 16)

            def store_half(i, h):
                pool.wait_ge(gath[h], 16 * HALF * (i + 1))
                g.dma_start(gathered[:, bass.ds((i * 2 + h) * HALF * TW, HALF * TW)],
                            ring[h][:, :, :].rearrange("p a b -> p (a b)")).then_inc(ring_st[h], 16)

            load_pick(0, 0)
            load_pick(HALF, 1)
            gather_half(0, 0)
            gather_half(0, 1)
            with pool.Fori(1, ROUNDS) as i:
                for h in range(2):
                    store_half(i - 1, h)
                    load_pick((i * 2 + h) * HALF, h)
                    pool.wait_ge(ring_st[h], 16 * i)
                    gather_half(i, h)
            for h in range(2):
                store_half(ROUNDS - 1, h)
            for h in range(2):
                pool.wait_ge(ring_st[h], 16 * ROUNDS)

        @block.tensor
        def _(pe):
            mm = nc.tensor.matmul
            pe.wait_ge(S["ids_ready"], 1)
            mm(p_hist[:, :], zero_b[:, 0:P], zero_b[:, :], start=True, stop=False)
            with pe.Fori(0, ETILES // GROUP) as q:
                pe.wait_ge(S["groups_oh"], q + 1)
                for j in range(GROUP):
                    m = mm(p_hist[:, j * P:(j + 1) * P], oh_hi[:, j * P:(j + 1) * P],
                           oh_lo[:, j * P:(j + 1) * P], start=False, stop=False)
                m.then_inc(S["hist_added"], 1)
            mm(p_hist[:, :], zero_b[:, 0:P], zero_b[:, :], start=False, stop=True).then_inc(S["counts_done"], 1)
            pe.wait_ge(S["totals_ready"], 1)
            mm(p_hi[:, 0:1], above[:, :], incl[:, P - 1:P], start=True, stop=True).then_inc(S["rowbase_done"], 1)
            pe.wait_ge(S["base_ready"], 1)
            with pe.Fori(0, EROUNDS) as i:
                for h in range(2):
                    for gi in range(HALF // GROUP):
                        q = i * (2 * HALF // GROUP) + h * (HALF // GROUP) + gi
                        t0 = i * 2 * HALF + h * HALF + gi * GROUP
                        pe.wait_ge(S["group_pos"], q)
                        for j in range(GROUP):
                            mm(p_hi[:, j * P:(j + 1) * P], hi_b[:, bass.ds(t0 + j, 1)].broadcast_to([P, P]),
                               ident_b[:, :], start=True, stop=True)
                        for j in range(GROUP):
                            o = p_dst[:, j * P:(j + 1) * P]
                            mm(o, hi128_b[:, bass.ds(t0 + j, 1)].broadcast_to([P, P]), ident_b[:, :],
                               start=True, stop=False)
                            m = mm(o, lo_b[:, bass.ds(t0 + j, 1)].broadcast_to([P, P]), ident_b[:, :],
                                   start=False, stop=True)
                        m.then_inc(S["ids_bcast"], 1)
                        pe.wait_ge(S["hiT_ready"], q + 1)
                        pe.wait_ge(S["hist_copied"], q)
                        for j in range(GROUP):
                            m = mm(p_first[:, j * P:(j + 1) * P], hiT[:, j * P:(j + 1) * P],
                                   hist[:, j * P:(j + 1) * P], start=True, stop=True)
                        m.then_inc(S["first_done"], 1)
                        pe.wait_ge(S["groups_oh"], ETILES // GROUP + q + 1)
                        mm(p_hist[:, :], ident[:, :], hist[:, :], start=True, stop=False)
                        for j in range(GROUP):
                            m = mm(p_hist[:, j * P:(j + 1) * P], oh_hi[:, j * P:(j + 1) * P],
                                   oh_lo[:, j * P:(j + 1) * P], start=False, stop=j == GROUP - 1)
                        m.then_inc(S["hist_added"], 1)

            pe.wait_ge(S["wp1"], 1)
            pe.wait_ge(S["tabs_ready"], 1)
            N = IMAGES
            mm(bank[4][0:CH, 0:N], center[:, :], hT[0][:, 0:N], start=True, stop=True).then_inc(S["cls_ps"], 1)
            pe.wait_ge(S["cls_sb"], 1)
            mm(bank[5][0:CH, 0:N], mean[:, :], sq[0][:, 0:N], start=True, stop=True).then_inc(S["cls_ps"], 1)
            pe.wait_ge(S["cls_sb"], 2)
            mm(bank[6][:, 0:N], b_sb[:, :], u[0][:, 0:N], start=True, stop=True).then_inc(S["cls_ps"], 1)
            pe.wait_ge(S["cls_sb"], 3)
            mm(bank[7][0:CH, 0:N], c_sb[:, :], y[:, 0:N], start=True, stop=True).then_inc(S["cls_ps"], 1)
            pe.wait_ge(S["cls_sb"], 4)
            mm(bank[4][0:CH, 0:N], center[:, :], h2[0][:, 0:N], start=True, stop=True).then_inc(S["cls_ps"], 1)
            pe.wait_ge(S["cls_sb"], 5)
            mm(bank[5][0:CH, 0:N], mean[:, :], sq[1][:, 0:N], start=True, stop=True).then_inc(S["cls_ps"], 1)
            pe.wait_ge(S["cls_sb"], 6)
            mm(bank[6][0:N, 0:TW], xn[0][:, 0:N], wproj[:, :], start=True, stop=True)
            mm(bank[6][0:N, 128:128 + CH], h2[0][:, 0:N], ident[0:CH, 0:CH], start=True, stop=True)\
                .then_inc(S["cls_ps"], 1)
            pe.wait_ge(S["cls_sb"], 8)

            def step(bt, tp, ba, ap):
                nt = bt * CHUNKS if bt is not None else None
                na = ba * CHUNKS if ba is not None else None
                zero = isinstance(bt, int) and bt == 0
                zero_a = isinstance(ba, int) and ba == 0

                def conv(c):
                    k = nt + c
                    if c == 0:
                        pe.wait_ge(S["x_in"], 64 * (bt + 1))
                    if not (zero and c == 0):
                        pe.wait_ge(S["h1_done"], k)
                    for t in range(NTT):
                        n = tile_rows(t)
                        m = mm(bank[0][0:CH, 0:CHUNK], w1[0:n, t, :], taps_view(tp, c, t),
                               start=t == 0, stop=t == NTT - 1)
                    m.then_inc(S["conv_done"], 1)

                def gates(c, t):
                    k = 5 * (nt + c) + t
                    if t == 0:
                        pe.wait_ge(S["h1_done"], nt + c + 1)
                    if not (zero and c == 0 and t < 2):
                        pe.wait_ge(S["gate_done"], k - 1)
                        if t == NTT - 1:
                            pe.sem_inc(S["waited"], 1)
                    n = tile_rows(t)
                    o = (5 * (tp * CHUNKS + c) + t) % 2
                    mm(bank[1 + o][0:n, 0:CHUNK], w2[:, 128 * t:128 * t + n], h1[:, :],
                       start=True, stop=True).then_inc(S["s_ps"], 1)

                def project(c, t):
                    k = 5 * (nt + c) + t
                    n = tile_rows(t)
                    pe.wait_ge(S["prod_done"], k + 1)
                    if t == 0 and not (zero and c == 0):
                        pe.wait_ge(S["hT_done"], nt + c)
                    pe.sem_inc(S["waited"], 1)
                    m = mm(bank[3][0:CH, 0:CHUNK], w3[0:n, t, :], prod[0:n, t, :], start=t == 0, stop=t == NTT - 1)
                    if t == NTT - 1:
                        m.then_inc(S["tok_done"], 1)

                tok = bt is not None
                att = ba is not None
                if tok:
                    conv(0)
                for c in range(CHUNKS + 2 if att else CHUNKS):
                    tc = tok and c < CHUNKS
                    a0 = att and c < CHUNKS
                    a1 = att and 1 <= c <= CHUNKS
                    a2 = att and c >= 2
                    if a1:
                        pe.wait_ge(S["y_done"], na + c)
                        if c > 1 or not zero_a:
                            pe.wait_ge(S["xn_done"], na + c - 1)
                        mm(bank[7][0:CH, 0:CHUNK], c_sb[:, :], y[:, :], start=True, stop=True)\
                            .then_inc(S["co_done"], 1)
                    if tc:
                        gates(c, 0)
                    if a2:
                        q = (ap * CHUNKS + c - 2) % 2
                        pe.wait_ge(S["xn_done"], na + c - 1)
                        pe.wait_ge(S["fin_read"], na + min(c, CHUNKS))
                        for j in range(FOLD):
                            mm(bank[6][0:FP, j * P:j * P + TW], xn[q][:, j:CHUNK:FOLD], wproj[:, :],
                               start=True, stop=True)
                            m = mm(bank[6][0:FP, j * P + 32:j * P + 32 + CH], h2[q][:, j:CHUNK:FOLD],
                                   ident[0:CH, 0:CH], start=True, stop=True)
                        m.then_inc(S["tm_done"], 1)
                    if tc:
                        gates(c, 1)
                    if a0:
                        pe.wait_ge(S["hT_done"], na + CHUNKS)
                        if not (zero_a and c == 0):
                            pe.wait_ge(S["u_done"], na + c)
                        pe.sem_inc(S["waited"], 1)
                        mm(bank[4][0:CH, 0:CHUNK], center[:, :], hT[ap][:, c * CHUNK:(c + 1) * CHUNK],
                           start=True, stop=True).then_inc(S["cent_done"], 1)
                    if a1:
                        pe.wait_ge(S["h2_done"], na + c)
                        pe.sem_inc(S["waited"], 1)
                        mm(bank[7][0:CH, 0:CHUNK], center[:, :], h2[(ap * CHUNKS + c - 1) % 2][:, :],
                           start=True, stop=True).then_inc(S["cent2_done"], 1)
                    if tc:
                        gates(c, 2)
                        gates(c, 3)
                    if a0:
                        pe.wait_ge(S["sq_done"], na + c + 1)
                        pe.sem_inc(S["waited"], 1)
                        mm(bank[5][0:CH, 0:CHUNK], mean[:, :], sq[0][:, :], start=True, stop=True)\
                            .then_inc(S["var_done"], 1)
                    if a1:
                        pe.wait_ge(S["sq2_done"], na + c)
                        if a2:
                            pe.wait_ge(S["tm_copied"], 2 * (na + c - 1))
                        pe.sem_inc(S["waited"], 1)
                        mm(bank[6][0:CH, 0:CHUNK], mean[:, :], sq[1][:, :], start=True, stop=True)\
                            .then_inc(S["var2_done"], 1)
                    if tc:
                        gates(c, 4)
                        if c + 1 < CHUNKS:
                            conv(c + 1)
                        project(c, 0)
                        project(c, 1)
                        project(c, 2)
                    if a0:
                        pe.wait_ge(S["u_done"], na + c + 1)
                        if a1:
                            pe.wait_ge(S["std2_done"], na + c)
                        elif not zero_a:
                            pe.wait_ge(S["tm_copied"], 2 * na)
                        mm(bank[6][:, 0:CHUNK], b_sb[:, :], u[(ap * CHUNKS + c) % 2][:, :], start=True, stop=True)\
                            .then_inc(S["bu_done"], 1)
                    if tc:
                        project(c, 3)
                        project(c, 4)

            steps(pe, step)

        @block.scalar
        def _(act):
            a = nc.scalar.activation
            act.wait_ge(S["base_ready"], 1)
            with act.Fori(0, EROUNDS) as i:
                for h in range(2):
                    act.wait_ge(scat[h], 16 * HALF * i)
                    a(rec[h][:, :, 0], src_i[:, bass.ds((2 * i + h) * HALF, HALF)], ACT.Copy)
                    a(rec[h][:, :, 1], dst_f[:, bass.ds((2 * i + h) * HALF, HALF)], ACT.Copy)\
                        .then_inc(S["rec_ready"], 1)
                    for gi in range(HALF // GROUP):
                        q = i * (2 * HALF // GROUP) + h * (HALF // GROUP) + gi
                        act.wait_ge(S["hist_added"], ETILES // GROUP + q + 1)
                        a(hist[:, :], p_hist[:, :], ACT.Copy).then_inc(S["hist_copied"], 1)
            with act.Fori(0, SROUNDS) as i:
                for h in range(2):
                    act.wait_ge(scat[h], 16 * HALF * (EROUNDS + i))
                    a(rec[h][:, :, 0], node_f[:, bass.ds((2 * i + h) * HALF, HALF)], ACT.Copy)
                    a(rec[h][:, :, 1], node_flag[:, bass.ds((2 * i + h) * HALF, HALF)], ACT.Copy)\
                        .then_inc(S["rec_ready"], 1)

            act.wait_ge(S["weights_in"], 16 * WEIGHT_LOADS)
            a(par[:, 0:1], dts[:, :], ACT.Sigmoid).then_inc(S["par_act"], 1)
            act.wait_ge(S["par_dve"], 1)
            a(par[:, 3:4], par[:, 2:3], ACT.Sqrt).then_inc(S["par_act"], 1)

            N = IMAGES
            act.wait_ge(S["cls_ps"], 1)
            a(sq[0][:, 0:N], bank[4][0:CH, 0:N], ACT.Square).then_inc(S["cls_sb"], 1)
            act.wait_ge(S["cls_ps"], 2)
            a(std[0][:, 0:N], bank[5][0:CH, 0:N], ACT.Sqrt, bias=eps_c[0:CH, :]).then_inc(S["cls_in"], 1)
            act.wait_ge(S["cls_ps"], 5)
            a(sq[1][:, 0:N], bank[4][0:CH, 0:N], ACT.Square).then_inc(S["cls_sb"], 1)
            act.wait_ge(S["cls_ps"], 6)
            a(std[1][:, 0:N], bank[5][0:CH, 0:N], ACT.Sqrt, bias=eps_c[0:CH, :]).then_inc(S["cls_in"], 1)
            act.wait_ge(S["cls_ps"], 7)
            a(t_out[0][0:N, 0, :], bank[6][0:N, 0:TW], ACT.Copy).then_inc(S["cls_sb"], 1)
            a(h_out[0][0:N, 0, :], bank[6][0:N, 128:128 + CH], ACT.Copy).then_inc(S["cls_sb"], 1)

            def step(bt, tp, ba, ap):
                nt = bt * CHUNKS if bt is not None else None
                na = ba * CHUNKS if ba is not None else None
                tok = bt is not None
                att = ba is not None
                zero = isinstance(bt, int) and bt == 0
                zero_a = isinstance(ba, int) and ba == 0

                def relu(c):
                    act.wait_ge(S["conv_done"], nt + c + 1)
                    if not (zero and c == 0):
                        act.wait_ge(S["s_ps"], 5 * (nt + c))
                    a(h1[:, :], bank[0][0:CH, 0:CHUNK], ACT.Relu, bias=tb1[:, :]).then_inc(S["h1_done"], 1)

                def gate_(c, t):
                    k = 5 * (nt + c) + t
                    o = (5 * (tp * CHUNKS + c) + t) % 2
                    n = tile_rows(t)
                    act.wait_ge(S["s_ps"], k + 1)
                    if not (zero and c == 0 and t < 2):
                        act.wait_ge(S["prod_done"], k - 1)
                    a(gate[o][0:n, :], bank[1 + o][0:n, 0:CHUNK], ACT.Sigmoid, bias=tb2[0:n, t:t + 1])\
                        .then_inc(S["gate_done"], 1)

                if tok:
                    relu(0)
                for c in range(CHUNKS + 2 if att else CHUNKS):
                    tc = tok and c < CHUNKS
                    a0 = att and c < CHUNKS
                    a1 = att and 1 <= c <= CHUNKS
                    a2 = att and c >= 2
                    if tc:
                        gate_(c, 0)
                    if a2:
                        q = (ap * CHUNKS + c - 2) % 2
                        act.wait_ge(S["tm_done"], na + c - 1)
                        if not (zero_a and c - 2 < 2):
                            act.wait_ge(tm_st[q], 24 * (na + c - 2 - q))
                        v = bank[6][0:FP, :].rearrange("p (j w) -> p j w", w=P)
                        a(t_out[q][0:FP, :, :], v[:, :, 0:TW], ACT.Copy).then_inc(S["tm_copied"], 1)
                        a(h_out[q][0:FP, :, :], v[:, :, 32:32 + CH], ACT.Copy).then_inc(S["tm_copied"], 1)
                    if tc:
                        gate_(c, 1)
                        gate_(c, 2)
                    if a0:
                        act.wait_ge(S["cent_done"], na + c + 1)
                        if not (zero_a and c == 0):
                            act.wait_ge(S["var_done"], na + c)
                        a(sq[0][:, :], bank[4][0:CH, 0:CHUNK], ACT.Square).then_inc(S["sq_done"], 1)
                    if a1:
                        act.wait_ge(S["cent2_done"], na + c)
                        if not (zero_a and c == 1):
                            act.wait_ge(S["var2_done"], na + c - 1)
                        a(sq[1][:, :], bank[7][0:CH, 0:CHUNK], ACT.Square).then_inc(S["sq2_done"], 1)
                    if tc:
                        gate_(c, 3)
                        gate_(c, 4)
                    if a0:
                        act.wait_ge(S["var_done"], na + c + 1)
                        if not (zero_a and c == 0):
                            act.wait_ge(S["u_done"], na + c)
                        a(std[0][:, :], bank[5][0:CH, 0:CHUNK], ACT.Sqrt, bias=eps_c[0:CH, :])\
                            .then_inc(S["std_done"], 1)
                    if a1:
                        act.wait_ge(S["var2_done"], na + c)
                        if not (zero_a and c == 1):
                            act.wait_ge(S["xn_done"], na + c - 1)
                        a(std[1][:, :], bank[6][0:CH, 0:CHUNK], ACT.Sqrt, bias=eps_c[0:CH, :])\
                            .then_inc(S["std2_done"], 1)
                    if tc:
                        if c + 1 < CHUNKS:
                            relu(c + 1)
                        act.wait_ge(S["tok_done"], nt + c + 1)
                        if c == 0 and not zero:
                            act.wait_ge(S["h2_done"], nt - CHUNKS)
                        a(hT[tp][:, c * CHUNK:(c + 1) * CHUNK], bank[3][0:CH, 0:CHUNK], ACT.Identity,
                          bias=tb3[:, :]).then_inc(S["hT_done"], 1)

            steps(act, step)

        @block.vector
        def _(dve):
            v = nc.vector
            dve.wait_ge(S["consts"], 1)
            dve.wait_ge(S["edges_in"], 32)
            v.tensor_copy(ident_b[:, :], ident[:, :])
            v.tensor_copy(iota_f[:, :], iota_i[:, :])
            v.tensor_copy(iota_b[:, :], iota_i[:, :])
            v.tensor_copy(part_f[:, :], part_i[:, :])
            v.tensor_single_scalar(tmp_i, dst_i, 7, ALU.arith_shift_right)
            v.tensor_copy(dst_f, dst_i)
            v.drain()
            v.tensor_copy(hi_b, tmp_i)
            v.tensor_scalar(hi128_b, tmp_i, float(LO), None, ALU.mult)
            v.tensor_scalar(node_f[:, :], part_f[:, 0:1].broadcast_to([P, P]), float(LO), None, ALU.mult)
            v.drain()
            v.tensor_tensor(lo_f, dst_f, hi128_b, ALU.subtract)
            v.tensor_tensor(node_f[:, :], node_f[:, :], iota_f[:, :], ALU.add)
            v.drain()
            v.tensor_copy(lo_b, lo_f)
            v.tensor_scalar(node_flag[:, :], node_f[:, :], float(FLAG), None, ALU.add)
            v.drain()
            v.nop().then_inc(S["ids_ready"], 1)

            def one_hots(t0):
                ib = iota_b[:, :].unsqueeze(1).broadcast_to([P, GROUP, P])
                for o, ids in ((oh_hi, hi_b), (oh_lo, lo_b)):
                    last = v.tensor_tensor(o[:, :].rearrange("p (j n) -> p j n", n=P),
                                           ids[:, bass.ds(t0, GROUP)].unsqueeze(2).broadcast_to([P, GROUP, P]),
                                           ib, ALU.is_equal)
                last.then_inc(S["groups_oh"], 1)

            with dve.Fori(0, ETILES // GROUP) as q:
                dve.wait_ge(S["hist_added"], q)
                one_hots(q * GROUP)
            dve.wait_ge(S["counts_done"], 1)
            v.tensor_copy(counts[:, :], p_hist[:, :])
            v.drain()
            v.tensor_tensor(deg[:, :], counts[:, 0:P], counts[:, P:2 * P], ALU.add)
            v.drain()
            for j in (2, 3):
                v.tensor_tensor(deg[:, :], deg[:, :], counts[:, j * P:(j + 1) * P], ALU.add)
                v.drain()
            v.tensor_scalar(deg[:, :], deg[:, :], 1.0, None, ALU.add)
            v.drain()
            v.tensor_tensor_scan(incl[:, :], deg[:, :], zero_f[:, :], 0.0, ALU.add, ALU.add)
            v.drain()
            v.nop().then_inc(S["totals_ready"], 1)
            dve.wait_ge(S["rowbase_done"], 1)
            v.tensor_copy(rowbase[:, :], p_hi[:, 0:1])
            v.tensor_tensor(base[:, :], incl[:, :], deg[:, :], ALU.subtract)
            v.drain()
            v.tensor_scalar(base[:, :], base[:, :], rowbase[:, 0:1], None, ALU.add)
            v.drain()
            v.tensor_copy(seg_i[:, 0, :], base[:, :])
            v.tensor_tensor(incl[:, :], base[:, :], deg[:, :], ALU.add)
            v.drain()
            v.tensor_scalar(seg_i[:, 1, :], incl[:, :], -1.0, None, ALU.add)
            v.tensor_scalar(hist[:, 0:P], base[:, :], 1.0, None, ALU.add)
            v.drain()
            for j in (1, 2, 3):
                v.tensor_tensor(hist[:, j * P:(j + 1) * P], hist[:, (j - 1) * P:j * P],
                                counts[:, (j - 1) * P:j * P], ALU.add)
                v.drain()
            v.nop().then_inc(S["base_ready"], 1)

            with dve.Fori(0, EROUNDS) as i:
                for h in range(2):
                    for gi in range(HALF // GROUP):
                        q = i * (2 * HALF // GROUP) + h * (HALF // GROUP) + gi
                        t0 = i * 2 * HALF + h * HALF + gi * GROUP
                        dve.wait_ge(S["ids_bcast"], q + 1)
                        dve.wait_ge(S["first_done"], q)
                        v.tensor_scalar(hiT[:, :], p_hi[:, :], part_f[:, 0:1], None, ALU.is_equal)\
                            .then_inc(S["hiT_ready"], 1)
                        for j in range(GROUP):
                            v.scalar_tensor_tensor(out=sort_junk[:, :], in0=p_dst[:, j * P:(j + 1) * P],
                                                   scalar=dst_f[:, bass.ds(t0 + j, 1)], in1=before[:, :],
                                                   op0=ALU.is_equal, op1=ALU.mult,
                                                   accum_out=rank[:, gi * GROUP + j:gi * GROUP + j + 1])
                            v.drain()
                        dve.wait_ge(S["hist_added"], ETILES // GROUP + q)
                        one_hots(t0)
                        dve.wait_ge(S["first_done"], q + 1)
                        for j in range(GROUP):
                            last = v.scalar_tensor_tensor(
                                out=sort_junk[:, :], in0=iota_f[:, :], scalar=lo_f[:, bass.ds(t0 + j, 1)],
                                in1=p_first[:, j * P:(j + 1) * P], op0=ALU.is_equal, op1=ALU.mult,
                                accum_out=first[:, gi * GROUP + j:gi * GROUP + j + 1])
                            v.drain()
                        v.nop().then_inc(S["group_pos"], 1)
                    dve.wait_ge(scat[h], 16 * HALF * i)
                    v.tensor_tensor(pos[h][:, :], rank[:, :], first[:, :], ALU.add)
                    v.drain()
                    v.nop().then_inc(S["pos_ready"], 1)
            with dve.Fori(0, SROUNDS) as i:
                for h in range(2):
                    dve.wait_ge(scat[h], 16 * HALF * (EROUNDS + i))
                    v.tensor_copy(pos[h][:, :], base[:, bass.ds((2 * i + h) * HALF, HALF)])\
                        .then_inc(S["pos_ready"], 1)

            for t in (*xa, *xb):
                v.memset(t[:, :], 0.0)
            v.drain()
            v.nop().then_inc(S["pads_zero"], 1)
            dve.wait_ge(S["weights_in"], 16 * WEIGHT_LOADS)
            wh = wproj[:, 0:HE].unsqueeze(1).broadcast_to([CH, 2, HE])
            v.tensor_tensor(wtmp[:, :, :], wh, att_bc[:, :, :], ALU.mult)
            v.drain()
            v.tensor_reduce(wproj[:, HE:TW], wtmp[:, :, :].rearrange("p a (h e) -> p (a h) e", e=EXPERTS),
                            AX.X, ALU.add)
            v.tensor_scalar(c_sb[CH:P, :], c_sb[CH:P, :], -1.0, None, ALU.mult)
            v.tensor_copy(hT[0][:, 0:IMAGES], cls_c[:, 0:1].broadcast_to([CH, IMAGES]))
            v.drain()
            v.nop().then_inc(S["wp1"], 1)

            def p_(n):
                return par[:, n:n + 1]

            def seq(*ops):
                for op in ops:
                    op()
                    v.drain()

            dve.wait_ge(S["par_act"], 1)
            seq(lambda: v.tensor_scalar(p_(1), adiag[:, :], 0.0, None, ALU.max),
                lambda: v.tensor_tensor(p_(7), p_(0), p_(0), ALU.mult),
                lambda: v.tensor_tensor(p_(7), p_(7), p_(1), ALU.mult),
                lambda: v.tensor_scalar(p_(7), p_(7), 1.0, None, ALU.add),
                lambda: v.reciprocal(p_(2), p_(7)))
            v.nop().then_inc(S["par_dve"], 1)
            dve.wait_ge(S["par_act"], 2)
            seq(lambda: v.reciprocal(p_(7), p_(3)),
                lambda: v.tensor_tensor(p_(7), p_(7), p_(2), ALU.mult),
                lambda: v.tensor_tensor(p_(7), p_(7), p_(3), ALU.add),
                lambda: v.tensor_scalar(p_(3), p_(7), 0.5, None, ALU.mult),
                lambda: v.reciprocal(p_(7), p_(3)),
                lambda: v.tensor_tensor(p_(4), p_(7), p_(2), ALU.mult),
                lambda: v.tensor_tensor(p_(5), p_(4), p_(0), ALU.mult))
            dve.wait_ge(S["rec_ready"], 2 * EROUNDS)
            dve.wait_ge(S["hist_added"], 2 * ETILES // GROUP)
            v.memset(tab_c[:, 0:1], 1.0)
            v.memset(tab_k[:, 0:1], 0.0)
            v.drain()
            n = 1
            while n < STEPS:
                m = min(2 * n, STEPS) - n
                seq(lambda: v.tensor_tensor(p_(6), p_(1), p_(5), ALU.mult),
                    lambda: v.tensor_scalar(p_(6), p_(6), -1.0, None, ALU.mult))
                v.tensor_scalar(tab_a[:, 0:m], tab_k[:, 0:m], p_(6), None, ALU.mult)
                v.tensor_scalar(tab_b[:, 0:m], tab_k[:, 0:m], p_(4), None, ALU.mult)
                v.drain()
                v.scalar_tensor_tensor(out=tab_c[:, n:n + m], in0=tab_c[:, 0:m], scalar=p_(4), in1=tab_a[:, 0:m],
                                       op0=ALU.mult, op1=ALU.add)
                v.scalar_tensor_tensor(out=tab_k[:, n:n + m], in0=tab_c[:, 0:m], scalar=p_(5), in1=tab_b[:, 0:m],
                                       op0=ALU.mult, op1=ALU.add)
                v.drain()
                seq(lambda: v.tensor_tensor(p_(6), p_(6), p_(5), ALU.mult),
                    lambda: v.tensor_tensor(p_(5), p_(5), p_(4), ALU.mult),
                    lambda: v.tensor_scalar(p_(5), p_(5), 2.0, None, ALU.mult),
                    lambda: v.tensor_tensor(p_(4), p_(4), p_(4), ALU.mult),
                    lambda: v.tensor_tensor(p_(4), p_(4), p_(6), ALU.add))
                n *= 2
            seq(lambda: v.tensor_tensor(p_(8), p_(1), tab_k[:, CHUNK:STEPS], ALU.mult),
                lambda: v.tensor_scalar(p_(8), p_(8), -1.0, None, ALU.mult))
            seq(lambda: v.tensor_tensor(p_(6), p_(1), p_(0), ALU.mult),
                lambda: v.tensor_tensor(p_(7), p_(2), p_(0), ALU.mult),
                lambda: v.scalar_tensor_tensor(out=tab_a, in0=tab_k, scalar=p_(6), in1=tab_c, op0=ALU.mult, op1=ALU.add),
                lambda: v.tensor_scalar(tab_a, tab_a, p_(7), None, ALU.mult),
                lambda: v.scalar_tensor_tensor(out=tab_b, in0=tab_c, scalar=p_(0), in1=tab_k, op0=ALU.mult, op1=ALU.subtract),
                lambda: v.tensor_scalar(tab_b, tab_b, p_(7), None, ALU.mult))
            v.nop().then_inc(S["tabs_ready"], 1)

            N = IMAGES
            dve.wait_ge(S["cls_in"], 1)
            seq(lambda: v.reciprocal(std[0][:, 0:N], std[0][:, 0:N]))
            v.tensor_tensor(u[0][:, 0:N], bank[4][0:CH, 0:N], std[0][:, 0:N], ALU.mult).then_inc(S["cls_sb"], 1)
            dve.wait_ge(S["cls_ps"], 3)
            v.tensor_tensor(start[:, 0:1], bank[6][:, 0:1], tab_a[:, 0:1], ALU.mult)
            v.tensor_tensor(start[:, 1:2], bank[6][:, 0:1], tab_b[:, 0:1], ALU.mult)
            v.tensor_scalar(y[:, 0:N], bank[6][:, 0:N], tab_b[:, 0:1], None, ALU.mult).then_inc(S["cls_sb"], 1)
            dve.wait_ge(S["cls_ps"], 4)
            v.scalar_tensor_tensor(out=h2[0][:, 0:N], in0=u[0][:, 0:N], scalar=d_sb[:, :],
                                   in1=bank[7][0:CH, 0:N], op0=ALU.mult, op1=ALU.add)
            v.drain()
            v.tensor_tensor(h2[0][:, 0:N], h2[0][:, 0:N], hT[0][:, 0:N], ALU.add).then_inc(S["cls_sb"], 1)
            dve.wait_ge(S["cls_in"], 2)
            seq(lambda: v.reciprocal(std[1][:, 0:N], std[1][:, 0:N]))
            v.tensor_tensor(xn[0][:, 0:N], bank[4][0:CH, 0:N], std[1][:, 0:N], ALU.mult).then_inc(S["cls_sb"], 1)
            dve.wait_ge(S["cls_st"], 48)

            def step(bt, tp, ba, ap):
                nt = bt * CHUNKS if bt is not None else None
                na = ba * CHUNKS if ba is not None else None
                tok = bt is not None
                att = ba is not None
                zero = isinstance(bt, int) and bt == 0
                zero_a = isinstance(ba, int) and ba == 0
                for c in range(CHUNKS + 2 if att else CHUNKS):
                    tc = tok and c < CHUNKS
                    a0 = att and c < CHUNKS
                    a1 = att and 1 <= c <= CHUNKS
                    q = (ap * CHUNKS + c) % 2 if att else 0
                    if a1:
                        dve.wait_ge(S["co_done"], na + c)
                        dve.wait_ge(S["tm_done"], na + max(c - 2, 0))
                        v.scalar_tensor_tensor(out=h2[1 - q][:, :], in0=u[1 - q][:, :], scalar=d_sb[:, :],
                                               in1=bank[7][0:CH, 0:CHUNK], op0=ALU.mult, op1=ALU.add)
                        v.drain()
                        v.tensor_tensor(h2[1 - q][:, :], h2[1 - q][:, :],
                                        hT[ap][:, (c - 1) * CHUNK:c * CHUNK], ALU.add).then_inc(S["h2_done"], 1)
                    if tc:
                        if not (zero and c == 0):
                            dve.wait_ge(S["tok_done"], nt + c)
                        for t in range(NTT):
                            k = 5 * (nt + c) + t
                            o = (5 * (tp * CHUNKS + c) + t) % 2
                            n = tile_rows(t)
                            dve.wait_ge(S["gate_done"], k + 1)
                            v.tensor_tensor(r3(prod[0:n, t, :]), taps_view(tp, c, t), r3(gate[o][0:n, :]),
                                            ALU.mult).then_inc(S["prod_done"], 1)
                    if a0:
                        dve.wait_ge(S["std_done"], na + c + 1)
                        v.reciprocal(std[0][:, :], std[0][:, :])
                        v.drain()
                        v.tensor_tensor(u[q][:, :], bank[4][0:CH, 0:CHUNK], std[0][:, :], ALU.mult)\
                            .then_inc(S["u_done"], 1)
                    if a1:
                        dve.wait_ge(S["std2_done"], na + c)
                        v.reciprocal(std[1][:, :], std[1][:, :])
                        v.drain()
                        if not (zero_a and c - 1 < 2):
                            dve.wait_ge(tm_st[1 - q], 24 * (na + c - 1 - (1 - q)))
                        v.tensor_tensor(xn[1 - q][:, :], bank[7][0:CH, 0:CHUNK], std[1][:, :], ALU.mult)\
                            .then_inc(S["xn_done"], 1)
                    if a0:
                        dve.wait_ge(S["bu_done"], na + c + 1)
                        tt = slice(1, STEPS)
                        v.tensor_tensor(fin[0][:, :], bank[6][:, 0:CHUNK], tab_a[:, tt], ALU.mult)
                        v.tensor_tensor(fin[1][:, :], bank[6][:, 0:CHUNK], tab_b[:, tt], ALU.mult)
                        v.drain()
                        v.nop().then_inc(S["fin_read"], 1)
                        init = carry if c else start
                        for n in range(2):
                            v.tensor_tensor_scan(wst[n][:, :], p_(3).broadcast_to([P, CHUNK]), fin[n][:, :],
                                                 init[:, n:n + 1], ALU.mult, ALU.add)
                        v.drain()
                        v.tensor_tensor(fin[0][:, :], wst[0][:, :], tab_k[:, tt], ALU.mult)
                        v.tensor_tensor(fin[1][:, :], wst[1][:, :], tab_c[:, tt], ALU.mult)
                        v.drain()
                        if not (zero_a and c == 0):
                            dve.wait_ge(S["co_done"], na + c)
                        v.tensor_tensor(y[:, :], fin[0][:, :], fin[1][:, :], ALU.add).then_inc(S["y_done"], 1)
                        last = slice(CHUNK - 1, CHUNK)
                        v.tensor_scalar(carry[:, 1:2], wst[0][:, last], tab_c[:, CHUNK:STEPS], None, ALU.mult)
                        v.drain()
                        v.scalar_tensor_tensor(out=carry[:, 0:1], in0=wst[1][:, last], scalar=p_(8),
                                               in1=carry[:, 1:2], op0=ALU.mult, op1=ALU.add)
                        v.drain()
                        v.tensor_copy(carry[:, 1:2], y[:, last])

            steps(dve, step)


SC = 136
SCHUNKS = SCOLS // SC
RW = 2 * HEADS + HE
VW = HEADS + HE
GK = 89
GATE_BATCHES = [GRAPH_NODES, GRAPH_NODES + P * GK, NODES - P * GK]
FF = NT // P


def back(nc, table, gathered, sorted_rec, seg_scratch, h_tok, xnT, b_gat, ln_gamma, ln_beta,
         W1, b1, W2, b2, out):
    partial = nc.dram_tensor("partial", [SORTED + P, RW], f32, kind="Internal").ap()
    gates = nc.dram_tensor("gates", [NODES, EXPERTS], f32, kind="Internal").ap()
    ctx = ExitStack()
    with ctx:
        def sb(name, shape, dt=f32):
            return ctx.enter_context(nc.sbuf_tensor(name, shape, dt))

        def pb(name, shape, dt=f32):
            return ctx.enter_context(nc.psum_tensor(name, shape, dt))

        def sem(name):
            return ctx.enter_context(nc.semaphore(name))

        ident = sb("ident2", [P, P])
        big = sb("big", [P, 2 * SCOLS])
        recs = big[:, :].bitcast(i32).rearrange("p (c w) -> p c w", w=2)
        st = sb("st", [P, SCOLS])
        ns = sb("ns", [P, SCOLS])
        nb = sb("nb", [P, SCOLS])
        rows = [sb(f"rows{n}", [P, SC, TW]) for n in range(2)]
        res = [sb(f"res{n}", [P, SC, RW]) for n in range(2)]
        sd = sb("sd", [P, HEADS, SC])
        ad = sb("ad", [P, HEADS, SC])
        e = sb("e", [P, HEADS, SC])
        mx = sb("mx", [P, HEADS, SC + 1])
        ex = sb("ex", [P, 2, HEADS, SC])
        msg = sb("msg", [P, HE, SC])
        cad = sb("cad", [P, HEADS])
        car = sb("car", [P, RW])
        key = sb("key", [P, SCOLS])
        cols = msg[:, :, :].rearrange("p a c -> p (a c)").bitcast(i32)
        fs = sb("fs", [P, 1])
        hs = sb("hs", [P, 1])
        partf = sb("partf", [P, 1])
        part = sb("part", [P, 1], i32)
        idx = sb("idx", [P, 4], i32)
        idxf = sb("idxf", [P, 4])
        arow = sb("arow", [P, TW])
        ends = sb("ends", [P, 3, VW])
        endsT = sb("endsT", [VW, 3, P])
        nbT = sb("nbT", [VW, P])
        mcT = sb("mcT", [VW, P + 1])
        vcT = sb("vcT", [VW, P + 1])
        exT = sb("exT", [VW, 2, P])
        cin = sb("cin", [P, 2, VW])
        fix = sb("fix", [P, RW])
        fm = sb("fm", [P, 3, VW])
        fixed = sb("fixed", [P, RW])
        seg = sb("seg", [P, P], i32)
        nidx = [sb(f"nidx{n}", [P, HALF], i32) for n in range(2)]
        nrow = [sb(f"nrow{n}", [P, HALF, RW]) for n in range(2)]
        node = sb("node", [P, P, RW])
        th = sb("th", [P, P, HE])
        gt = sb("gt", [P, P, HE])
        g1 = sb("g1", [P, P, HEADS])
        g2 = sb("g2", [P, P, HEADS])
        g3 = sb("g3", [P, P, HEADS])
        r1 = sb("r1", [P, P])
        r2 = sb("r2", [P, P])
        bgat = sb("bgat", [P, HE])
        gam = sb("gam", [P, HE])
        bet = sb("bet", [P, HE])
        eps2 = sb("eps2", [P, 1])
        w1 = sb("fw1", [CH, EXPERTS, HIDDEN])
        w2 = sb("fw2", [HIDDEN, EXPERTS, CH])
        fb1 = sb("fb1", [HIDDEN, EXPERTS])
        fb2 = sb("fb2", [P, EXPERTS * CH])
        xf = [sb(f"xf{n}", [CH, NT]) for n in range(2)]
        hr = [sb(f"hr{n}", [P, FF, CH]) for n in range(2)]
        gf = [sb(f"gf{n}", [P, FF, EXPERTS]) for n in range(2)]
        hh = [big[:, n * EXPERTS * NT:(n + 1) * EXPERTS * NT].rearrange("p (e n) -> p e n", n=NT)
              for n in range(2)]
        yb = sb("yb", [P, FF, EXPERTS, CH])
        yc = sb("yc", [P, FF, 2, CH])
        yo = [sb(f"yo{n}", [P, FF, CH]) for n in range(2)]

        hid = [pb(f"hid{n}", [P, 512]) for n in range(2)]
        ybank = [pb(f"ybank{n}", [P, 1024]) for n in range(2)]
        tp = pb("tp", [P, 512])

        names = """consts in0 wts idx_ready arow_in rows0 rows1 res0 res1 ex_in ex_done ends_ready endsT_done
            cin_ready exT_in exT_done cin_done fix_idx fix_in fix_ex fix_exd fixed_ready fixed_st nstage
            ngath0 ngath1 ybank_free node_ready th_in g_sq g_std g_e g_ex gt_ready gt_st ff0 ff1 hid_done hh_done y_done
            yo_done out0 out1 scan_used waited""".split()
        S = {n: sem("b_" + n) for n in names}
        block = ctx.enter_context(nc.Block())
        sorted_v = sorted_rec.rearrange("(p c) w -> p c w", c=SCOLS)
        partial_v = partial[0:SORTED, :].rearrange("(p c) w -> p (c w)", c=SCOLS)
        rows_s = [S["rows0"], S["rows1"]]
        res_s = [S["res0"], S["res1"]]
        ff = [S["ff0"], S["ff1"]]
        ost = [S["out0"], S["out1"]]
        WTS = 9

        def chunks(eng, step):
            outside = (NODES - GRAPH_NODES) // NT
            lo = GRAPH_NODES
            with eng.Fori(0, outside // 2) as i:
                for q in range(2):
                    step(2 * i + q, lo + (2 * i + q) * NT, q)
            k = outside
            step(k, NODES - NT, 0)
            step(k + 1, 0, 1)
            k += 2
            inside = GRAPH_NODES // NT - 1
            with eng.Fori(0, inside // 2) as i:
                for q in range(2):
                    step(k + 2 * i + q, (1 + 2 * i + q) * NT, q)
            step(k + inside - 1, inside * NT, 0)

        assert (NODES - GRAPH_NODES) // NT % 2 == 0 and (GRAPH_NODES // NT - 1) % 2 == 1
        TOTAL = (NODES - GRAPH_NODES) // NT + 1 + GRAPH_NODES // NT
        OUTSIDE = (NODES - GRAPH_NODES) // NT + 1

        @block.sync
        def _(sp):
            sp.dma_start(recs, sorted_v).then_inc(S["in0"], 16)
            sp.dma_start(seg[:, :], seg_scratch[1, :, :]).then_inc(S["in0"], 16)
            for dst, src in ((bgat[:, :], b_gat.partition_broadcast(P)), (gam[:, :], ln_gamma.partition_broadcast(P)),
                             (bet[:, :], ln_beta.partition_broadcast(P)), (fb2[:, :], b2.partition_broadcast(P)),
                             (w1[:, :, :], W1.rearrange("e c h -> c e h")), (w2[:, :, :], W2.rearrange("e h c -> h e c")),
                             (fb1[:, :], b1)):
                sp.dma_start(dst, src).then_inc(S["wts"], 16)

            def load_rows(k, q):
                sp.dma_start(rows[q][:, :, :].rearrange("p c w -> p (c w)"),
                             gathered[:, bass.ds(k * SC * TW, SC * TW)]).then_inc(rows_s[q], 16)

            load_rows(0, 0)
            load_rows(1, 1)

            def store_res(k, q):
                sp.wait_ge(S["scan_used"], k + 1)
                sp.sem_inc(S["waited"], 1)
                sp.dma_start(partial_v[:, bass.ds(k * SC * RW, SC * RW)],
                             res[q][:, :, :].rearrange("p c w -> p (c w)")).then_inc(res_s[q], 16)

            with sp.Fori(0, SCHUNKS // 2 - 1) as i:
                for q in range(2):
                    store_res(2 * i + q, q)
                    load_rows(2 * i + q + 2, q)
            for q in range(2):
                store_res(SCHUNKS - 2 + q, q)

            for n, g0 in enumerate(GATE_BATCHES):
                if n:
                    sp.wait_ge(S["gt_st"], 16 * n)
                sp.dma_start(th[:, 0:GK, :], table[g0:g0 + P * GK, 0:HE].rearrange("(p k) w -> p k w", k=GK))\
                    .then_inc(S["th_in"], 16)
                sp.wait_ge(S["gt_ready"], n + 1)
                sp.dma_start(gates[g0:g0 + P * GK, :].rearrange("(p k) w -> p k w", k=GK), g1[:, 0:GK, :])\
                    .then_inc(S["gt_st"], 16)
            sp.wait_ge(S["gt_st"], 16 * len(GATE_BATCHES))

            def load_ff(k, n0, q):
                sp.dma_start(xf[q][:, :], xnT[:, bass.ds(n0, NT)]).then_inc(ff[q], 16)
                sp.dma_start(hr[q][:, :, :], h_tok[bass.ds(n0, NT), :].rearrange("(p j) c -> p j c", j=FF))\
                    .then_inc(ff[q], 16)
                sp.dma_start(gf[q][:, :, :], gates[bass.ds(n0, NT), :].rearrange("(p j) c -> p j c", j=FF))\
                    .then_inc(ff[q], 16)

            def store_ff(k, n0, q):
                sp.wait_ge(S["yo_done"], k + 1)
                sp.sem_inc(S["waited"], 1)
                sp.dma_start(out[bass.ds(n0, NT), :].rearrange("(p j) c -> p j c", j=FF), yo[q][:, :, :])\
                    .then_inc(ost[q], 16)

            def node0(k):
                return (GRAPH_NODES + k * NT if k < OUTSIDE - 1 else
                        NODES - NT if k == OUTSIDE - 1 else (k - OUTSIDE) * NT)

            load_ff(0, node0(0), 0)
            load_ff(1, node0(1), 1)
            with sp.Fori(0, (OUTSIDE - 3) // 2) as i:
                for q in range(2):
                    store_ff(2 * i + q, GRAPH_NODES + (2 * i + q) * NT, q)
                    load_ff(2 * i + q + 2, GRAPH_NODES + (2 * i + q + 2) * NT, q)
            for k in range(OUTSIDE - 3, OUTSIDE + 1):
                if k == OUTSIDE - 1:
                    for z in range(2):
                        sp.wait_ge(ost[z], 16 * (OUTSIDE // 2))
                store_ff(k, node0(k), k % 2)
                if k == OUTSIDE - 2:
                    sp.wait_ge(S["gt_ready"], len(GATE_BATCHES) + 1)
                    sp.dma_start(gates[0:GRAPH_NODES, :].rearrange("(p k) w -> p k w", k=P), g1[:, :, :])\
                        .then_inc(S["gt_st"], 16)
                    sp.wait_ge(S["gt_st"], 16 * (len(GATE_BATCHES) + 1))
                load_ff(k + 2, node0(k + 2), k % 2)
            with sp.Fori(0, (TOTAL - OUTSIDE - 4) // 2) as i:
                for z in range(2):
                    m = 2 * i + z + 1
                    store_ff(OUTSIDE + m, m * NT, z)
                    load_ff(OUTSIDE + m + 2, (m + 2) * NT, z)
            for k in range(TOTAL - 3, TOTAL):
                store_ff(k, node0(k), k % 2)
                if k + 2 < TOTAL:
                    load_ff(k + 2, node0(k + 2), k % 2)
            sp.wait_ge(ost[0], 16 * ((TOTAL + 1) // 2))
            sp.wait_ge(ost[1], 16 * (TOTAL // 2))

        @block.gpsimd
        def _(pool):
            g = nc.gpsimd
            g.memset(ident[:, :], 0.0)
            g.memset(eps2[:, :], EPS)
            g.iota(cols, pattern=[[1, SCOLS]], base=0, channel_multiplier=0)
            g.iota(part[:, :], pattern=[[1, 1]], base=0, channel_multiplier=1)
            g.drain()
            g.affine_select(out=ident[:, :], in_=ident[:, :], compare_op=ALU.not_equal, fill=1.0, base=0,
                            pattern=[[-1, P]], channel_multiplier=1)
            g.drain()
            g.nop().then_inc(S["consts"], 1)
            off = bass.IndirectOffsetOnAxis
            pool.wait_ge(S["idx_ready"], 1)
            g.indirect_dma_start(out=arow[:, :], out_offset=None, in_=table[0:GRAPH_NODES, :],
                                 in_offset=off(ap=idx[:, 0:1], axis=0)).then_inc(S["arow_in"], 16)
            for q in range(2):
                pool.wait_ge(res_s[q], 16 * SCHUNKS // 2)
            g.indirect_dma_start(out=fix[:, :], out_offset=None, in_=partial[0:SORTED, :],
                                 in_offset=off(ap=idx[:, 1:2], axis=0)).then_inc(S["fix_in"], 16)
            pool.wait_ge(S["fixed_ready"], 1)
            g.indirect_dma_start(out=partial, out_offset=off(ap=idx[:, 2:3], axis=0), in_=fixed[:, :],
                                 in_offset=None).then_inc(S["fixed_st"], 16)
            pool.wait_ge(S["fixed_st"], 16)
            with pool.Fori(0, SROUNDS) as i:
                for h in range(2):
                    g.tensor_copy(nidx[h][:, :], seg[:, bass.ds((2 * i + h) * HALF, HALF)])
                g.drain()
                for h in range(2):
                    for j in range(HALF):
                        g.indirect_dma_start(out=nrow[h][:, j, :], out_offset=None, in_=partial[0:SORTED, :],
                                             in_offset=off(ap=nidx[h][:, j:j + 1], axis=0))\
                            .then_inc([S["ngath0"], S["ngath1"]][h], 16)
                for h in range(2):
                    pool.wait_ge([S["ngath0"], S["ngath1"]][h], 16 * HALF * (i + 1))
                    g.tensor_copy(node[:, bass.ds((2 * i + h) * HALF, HALF), :], nrow[h][:, :, :])
                g.drain()
            g.nop().then_inc(S["node_ready"], 1)

        @block.tensor
        def _(pe):
            mm = nc.tensor.matmul
            pe.wait_ge(S["ends_ready"], 1)
            for n in range(3):
                m = mm(tp[0:VW, n * P:(n + 1) * P], ends[:, n, :], ident[:, :], start=True, stop=True)
            m.then_inc(S["endsT_done"], 1)
            pe.wait_ge(S["cin_ready"], 1)
            mm(tp[:, 0:VW], mcT[:, 0:P], ident[0:VW, 0:VW], start=True, stop=True)
            mm(tp[:, VW:2 * VW], vcT[:, 0:P], ident[0:VW, 0:VW], start=True, stop=True).then_inc(S["cin_done"], 1)
            pe.wait_ge(S["wts"], 16 * 7)

            def step(k, n0, q):
                pe.wait_ge(ff[q], 24 * (k - q) + 48)
                for ee in range(EXPERTS):
                    if ee >= 2:
                        pe.wait_ge(S["hh_done"], EXPERTS * k + ee - 1)
                    mm(hid[ee % 2][:, :], w1[:, ee, :], xf[q][:, :], start=True, stop=True).then_inc(S["hid_done"], 1)
                pe.wait_ge(S["hh_done"], EXPERTS * k + EXPERTS)
                pe.wait_ge(S["ybank_free"], k + 1)
                for j in range(FF):
                    for ee in range(EXPERTS):
                        o = (j * EXPERTS + ee) * CH
                        m = mm(ybank[q][:, o:o + CH], hh[q][:, ee, j:NT:FF], w2[:, ee, :], start=True, stop=True)
                m.then_inc(S["y_done"], 1)

            chunks(pe, step)

        @block.scalar
        def _(act):
            a = nc.scalar.activation
            with act.Fori(0, SCHUNKS) as k:
                act.wait_ge(S["ex_in"], k + 1)
                a(ex[:, :, :, :], ex[:, :, :, :], ACT.Exp).then_inc(S["ex_done"], 1)
            act.wait_ge(S["exT_in"], 1)
            a(exT[:, :, :], exT[:, :, :], ACT.Exp).then_inc(S["exT_done"], 1)
            act.wait_ge(S["fix_ex"], 1)
            a(fm[:, 0:2, :], fm[:, 0:2, :], ACT.Exp).then_inc(S["fix_exd"], 1)

            def gate_fn(n, K):
                act.wait_ge(S["g_sq"], n + 1)
                a(r1[:, 0:K], r1[:, 0:K], ACT.Sqrt, scale=1.0 / HE, bias=eps2[:, :]).then_inc(S["g_std"], 1)
                act.wait_ge(S["g_e"], n + 1)
                a(g1[:, 0:K, :], g1[:, 0:K, :], ACT.Exp).then_inc(S["g_ex"], 1)

            for n in range(len(GATE_BATCHES)):
                gate_fn(n, GK)

            act.wait_ge(S["wts"], 16 * 7)

            def step(k, n0, q):
                if isinstance(k, int) and k == OUTSIDE:
                    gate_fn(len(GATE_BATCHES), P)
                for ee in range(EXPERTS):
                    act.wait_ge(S["hid_done"], EXPERTS * k + ee + 1)
                    a(hh[q][:, ee, :], hid[ee % 2][:, :], ACT.Gelu, bias=fb1[:, ee:ee + 1]).then_inc(S["hh_done"], 1)

            chunks(act, step)

        @block.vector
        def _(dve):
            v = nc.vector

            def seq(*ops):
                for op in ops:
                    op()
                    v.drain()

            dve.wait_ge(S["consts"], 1)
            v.nop().then_inc(S["ybank_free"], 2)
            dve.wait_ge(S["in0"], 32)
            seq(lambda: v.tensor_copy(key[:, :], recs[:, :, 1]),
                lambda: v.tensor_scalar(st[:, :], key[:, :], float(FLAG), None, ALU.is_ge))
            v.tensor_scalar(ns[:, :], st[:, :], -1.0, 1.0, ALU.mult, ALU.add)
            v.tensor_scalar(nb[:, :], st[:, :], -BIG, None, ALU.mult)
            v.scalar_tensor_tensor(out=idx[:, 0:1], in0=st[:, 0:1], scalar=-float(FLAG), in1=key[:, 0:1],
                                   op0=ALU.mult, op1=ALU.add)
            v.tensor_copy(partf[:, :], part[:, :])
            v.tensor_reduce(hs[:, :], st[:, :], AX.X, ALU.max)
            v.drain()
            v.nop().then_inc(S["idx_ready"], 1)
            seq(lambda: v.tensor_copy(key[:, :], cols),
                lambda: v.scalar_tensor_tensor(out=key[:, :], in0=ns[:, :], scalar=float(SCOLS), in1=key[:, :],
                                               op0=ALU.mult, op1=ALU.add),
                lambda: v.tensor_reduce(fs[:, :], key[:, :], AX.X, ALU.min),
                lambda: v.tensor_scalar(idxf[:, 3:4], fs[:, :], 0.0, None, ALU.is_equal),
                lambda: v.scalar_tensor_tensor(out=idxf[:, 0:1], in0=partf[:, :], scalar=float(SCOLS), in1=fs[:, :],
                                               op0=ALU.mult, op1=ALU.add),
                lambda: v.tensor_tensor(idxf[:, 1:2], idxf[:, 0:1], idxf[:, 3:4], ALU.add),
                lambda: v.tensor_scalar(idxf[:, 1:2], idxf[:, 1:2], -1.0, None, ALU.add),
                lambda: v.tensor_scalar(idxf[:, 2:3], partf[:, :], float(SORTED), None, ALU.add),
                lambda: v.tensor_tensor(idxf[:, 2:3], idxf[:, 2:3], idxf[:, 1:2], ALU.subtract),
                lambda: v.scalar_tensor_tensor(out=idxf[:, 2:3], in0=idxf[:, 2:3], scalar=idxf[:, 3:4],
                                               in1=idxf[:, 1:2], op0=ALU.mult, op1=ALU.add),
                lambda: v.tensor_copy(idx[:, 1:3], idxf[:, 1:3]),
                lambda: v.memset(car[:, :], 0.0),
                lambda: v.memset(car[:, 0:HEADS], -BIG))
            dve.wait_ge(S["arow_in"], 16)
            seq(lambda: v.tensor_copy(cad[:, :], arow[:, HE + HEADS:TW]))

            with dve.Fori(0, SCHUNKS // 2) as i:
                for q in range(2):
                    k = 2 * i + q
                    dve.wait_ge(rows_s[q], 16 * (i + 1))
                    rv = rows[q][:, :, :].rearrange("p c w -> p w c")
                    ov = res[q][:, :, :].rearrange("p c w -> p w c")
                    cs = bass.ds(k * SC, SC)

                    def flag(t, n=HEADS):
                        return t[:, cs].unsqueeze(1).broadcast_to([P, n, SC])

                    seq(lambda: v.tensor_tensor(sd[:, :, :], rv[:, HE + HEADS:TW, :], flag(st), ALU.mult))
                    for h in range(HEADS):
                        v.tensor_tensor_scan(ad[:, h, :], ns[:, cs], sd[:, h, :], cad[:, h:h + 1], ALU.mult, ALU.add)
                    v.tensor_copy(mx[:, :, 0], car[:, 0:HEADS])
                    v.drain()
                    v.tensor_copy(cad[:, :], ad[:, :, SC - 1])
                    seq(lambda: v.tensor_tensor(e[:, :, :], rv[:, HE:HE + HEADS, :], ad[:, :, :], ALU.add),
                        lambda: v.scalar_tensor_tensor(out=e[:, :, :], in0=e[:, :, :], scalar=0.2, in1=e[:, :, :],
                                                       op0=ALU.mult, op1=ALU.max))
                    for h in range(HEADS):
                        v.tensor_tensor_scan(mx[:, h, 1:SC + 1], nb[:, cs], e[:, h, :], car[:, h:h + 1],
                                             ALU.add, ALU.max)
                    v.drain()
                    v.tensor_tensor(ex[:, 0, :, :], mx[:, :, 0:SC], mx[:, :, 1:SC + 1], ALU.subtract)
                    v.tensor_tensor(ex[:, 1, :, :], e[:, :, :], mx[:, :, 1:SC + 1], ALU.subtract)
                    v.drain()
                    v.tensor_scalar(ex[:, 0, :, :], ex[:, 0, :, :], 0.0, None, ALU.min).then_inc(S["ex_in"], 1)
                    dve.wait_ge(S["ex_done"], k + 1)
                    v.tensor_tensor(ex[:, 0, :, :], ex[:, 0, :, :], flag(ns), ALU.mult)
                    for h in range(HEADS):
                        v.tensor_tensor(msg[:, h * EXPERTS:(h + 1) * EXPERTS, :],
                                        rv[:, h * EXPERTS:(h + 1) * EXPERTS, :],
                                        ex[:, 1, h, :].unsqueeze(1).broadcast_to([P, EXPERTS, SC]), ALU.mult)
                    v.drain()
                    dve.wait_ge(res_s[q], 16 * i)
                    v.tensor_copy(ov[:, 0:HEADS, :], mx[:, :, 1:SC + 1])
                    for h in range(HEADS):
                        v.tensor_tensor_scan(ov[:, HEADS + h, :], ex[:, 0, h, :], ex[:, 1, h, :],
                                             car[:, HEADS + h:HEADS + h + 1], ALU.mult, ALU.add)
                        for x_ in range(EXPERTS):
                            w = h * EXPERTS + x_
                            v.tensor_tensor_scan(ov[:, 2 * HEADS + w, :], ex[:, 0, h, :], msg[:, w, :],
                                                 car[:, 2 * HEADS + w:2 * HEADS + w + 1], ALU.mult, ALU.add)
                    v.drain()
                    v.tensor_copy(car[:, :], res[q][:, SC - 1, :])
                    v.drain()
                    v.nop().then_inc(S["scan_used"], 1)

            v.tensor_copy(ends[:, 0, 0:HEADS], car[:, 0:HEADS])
            v.tensor_copy(ends[:, 0, HEADS:VW].rearrange("p (h x) -> p h x", x=EXPERTS),
                          car[:, 0:HEADS].unsqueeze(2).broadcast_to([P, HEADS, EXPERTS]))
            v.tensor_copy(ends[:, 1, :], car[:, HEADS:RW])
            v.tensor_scalar(ends[:, 2, :], hs[:, 0:1].broadcast_to([P, VW]), -1.0, 1.0, ALU.mult, ALU.add)
            v.drain()
            v.nop().then_inc(S["ends_ready"], 1)
            dve.wait_ge(S["endsT_done"], 1)
            v.tensor_copy(endsT[:, :, :].rearrange("p a b -> p (a b)"), tp[0:VW, 0:3 * P])
            v.memset(mcT[:, 0:1], -BIG)
            v.memset(vcT[:, 0:1], 0.0)
            v.drain()
            seq(lambda: v.tensor_scalar(nbT[:, :], endsT[:, 2, :], 1.0, BIG, ALU.subtract, ALU.mult),
                lambda: v.tensor_tensor_scan(mcT[:, 1:P + 1], nbT[:, :], endsT[:, 0, :], -BIG, ALU.add, ALU.max),
                lambda: v.tensor_tensor(exT[:, 0, :], mcT[:, 0:P], mcT[:, 1:P + 1], ALU.subtract),
                lambda: v.tensor_scalar(exT[:, 0, :], exT[:, 0, :], 0.0, None, ALU.min),
                lambda: v.tensor_tensor(exT[:, 1, :], endsT[:, 0, :], mcT[:, 1:P + 1], ALU.subtract))
            v.nop().then_inc(S["exT_in"], 1)
            dve.wait_ge(S["exT_done"], 1)
            seq(lambda: v.tensor_tensor(exT[:, 0, :], exT[:, 0, :], endsT[:, 2, :], ALU.mult),
                lambda: v.tensor_tensor(endsT[:, 1, :], exT[:, 1, :], endsT[:, 1, :], ALU.mult),
                lambda: v.tensor_tensor_scan(vcT[:, 1:P + 1], exT[:, 0, :], endsT[:, 1, :], 0.0, ALU.mult, ALU.add))
            v.nop().then_inc(S["cin_ready"], 1)
            dve.wait_ge(S["cin_done"], 1)
            seq(lambda: v.tensor_copy(cin[:, :, :].rearrange("p a b -> p (a b)"), tp[:, 0:2 * VW]))
            dve.wait_ge(S["fix_in"], 16)
            v.tensor_copy(fm[:, 0, 0:HEADS], fix[:, 0:HEADS])
            v.tensor_copy(fm[:, 0, HEADS:VW].rearrange("p (h x) -> p h x", x=EXPERTS),
                          fix[:, 0:HEADS].unsqueeze(2).broadcast_to([P, HEADS, EXPERTS]))
            v.drain()
            seq(lambda: v.tensor_tensor(fm[:, 2, :], fm[:, 0, :], cin[:, 0, :], ALU.max),
                lambda: v.tensor_copy(fixed[:, 0:HEADS], fm[:, 2, 0:HEADS]),
                lambda: v.tensor_tensor(fm[:, 0, :], fm[:, 0, :], fm[:, 2, :], ALU.subtract),
                lambda: v.tensor_tensor(fm[:, 1, :], cin[:, 0, :], fm[:, 2, :], ALU.subtract))
            v.nop().then_inc(S["fix_ex"], 1)
            dve.wait_ge(S["fix_exd"], 1)
            seq(lambda: v.tensor_tensor(fm[:, 0, :], fm[:, 0, :], fix[:, HEADS:RW], ALU.mult),
                lambda: v.tensor_tensor(fm[:, 1, :], fm[:, 1, :], cin[:, 1, :], ALU.mult),
                lambda: v.tensor_tensor(fixed[:, HEADS:RW], fm[:, 0, :], fm[:, 1, :], ALU.add))
            v.nop().then_inc(S["fixed_ready"], 1)

            def bc(t, K):
                return t[:, :].unsqueeze(1).broadcast_to([P, K, HE])

            def gate_fn(n, K):
                T = th[:, 0:K, :]
                G = gt[:, 0:K, :]
                R = r1[:, 0:K]
                W = r2[:, 0:K]
                A1, A2, A3 = g1[:, 0:K, :], g2[:, 0:K, :], g3[:, 0:K, :]
                seq(lambda: v.tensor_tensor(T, T, bc(bgat, K), ALU.add),
                    lambda: v.tensor_reduce(R, T, AX.X, ALU.add),
                    lambda: v.tensor_scalar(R, R, 1.0 / HE, None, ALU.mult),
                    lambda: v.tensor_tensor(T, T, R.unsqueeze(2).broadcast_to([P, K, HE]), ALU.subtract),
                    lambda: v.tensor_tensor(G, T, T, ALU.mult),
                    lambda: v.tensor_reduce(R, G, AX.X, ALU.add))
                v.nop().then_inc(S["g_sq"], 1)
                dve.wait_ge(S["g_std"], n + 1)
                seq(lambda: v.reciprocal(R, R),
                    lambda: v.tensor_tensor(T, T, R.unsqueeze(2).broadcast_to([P, K, HE]), ALU.mult),
                    lambda: v.tensor_tensor(T, T, bc(gam, K), ALU.mult),
                    lambda: v.tensor_tensor(T, T, bc(bet, K), ALU.add),
                    lambda: v.tensor_tensor(A2, T[:, :, 0:4], T[:, :, 4:8], ALU.add),
                    lambda: v.tensor_tensor(A2, A2, T[:, :, 8:12], ALU.add),
                    lambda: v.tensor_tensor(A2, A2, T[:, :, 12:16], ALU.add),
                    lambda: v.tensor_scalar(A2, A2, 1.0 / HEADS, None, ALU.mult),
                    lambda: v.memset(A3, 0.0))
                for i in range(EXPERTS):
                    for j in range(i + 1, EXPERTS):
                        seq(lambda: v.tensor_tensor(W, A2[:, :, i], A2[:, :, j], ALU.is_ge),
                            lambda: v.tensor_tensor(A3[:, :, j], A3[:, :, j], W, ALU.add),
                            lambda: v.tensor_scalar(W, W, -1.0, 1.0, ALU.mult, ALU.add),
                            lambda: v.tensor_tensor(A3[:, :, i], A3[:, :, i], W, ALU.add))
                seq(lambda: v.tensor_scalar(A3, A3, 2.0, None, ALU.is_lt),
                    lambda: v.tensor_reduce(R, A2, AX.X, ALU.max))
                if n:
                    dve.wait_ge(S["gt_st"], 16 * n)
                seq(lambda: v.tensor_tensor(A1, A2, R.unsqueeze(2).broadcast_to([P, K, EXPERTS]), ALU.subtract))
                v.nop().then_inc(S["g_e"], 1)
                dve.wait_ge(S["g_ex"], n + 1)
                seq(lambda: v.tensor_tensor(A1, A1, A3, ALU.mult),
                    lambda: v.tensor_reduce(R, A1, AX.X, ALU.add),
                    lambda: v.reciprocal(R, R),
                    lambda: v.tensor_tensor(A1, A1, R.unsqueeze(2).broadcast_to([P, K, EXPERTS]), ALU.mult))
                v.nop().then_inc(S["gt_ready"], 1)

            dve.wait_ge(S["wts"], 16 * 7)
            for n in range(len(GATE_BATCHES)):
                dve.wait_ge(S["th_in"], 16 * (n + 1))
                gate_fn(n, GK)

            def step(k, n0, q):
                if isinstance(k, int) and k == OUTSIDE:
                    dve.wait_ge(S["node_ready"], 1)
                    seq(lambda: v.tensor_scalar(g2[:, :, :], node[:, :, HEADS:2 * HEADS], DENOM_EPS, None, ALU.add),
                        lambda: v.reciprocal(g2[:, :, :], g2[:, :, :]))
                    for h in range(HEADS):
                        v.tensor_tensor(th[:, :, h * EXPERTS:(h + 1) * EXPERTS],
                                        node[:, :, 2 * HEADS + h * EXPERTS:2 * HEADS + (h + 1) * EXPERTS],
                                        g2[:, :, h:h + 1].broadcast_to([P, P, EXPERTS]), ALU.mult)
                    v.drain()
                    gate_fn(len(GATE_BATCHES), P)
                dve.wait_ge(S["y_done"], k + 1)
                dve.wait_ge(ff[q], 24 * (k - q) + 48)
                Y = yb[:, :, :, :].rearrange("p j e c -> p j (e c)")
                v.tensor_tensor(Y, ybank[q][:, :].rearrange("p (j n) -> p j n", j=FF),
                                fb2[:, :].unsqueeze(1).broadcast_to([P, FF, EXPERTS * CH]), ALU.add)\
                    .then_inc(S["ybank_free"], 1)
                v.drain()
                v.tensor_tensor(yb[:, :, :, :].rearrange("p j e c -> p (j e) c"),
                                yb[:, :, :, :].rearrange("p j e c -> p (j e) c"),
                                gf[q][:, :, :].rearrange("p j e -> p (j e)").unsqueeze(2)
                                .broadcast_to([P, FF * EXPERTS, CH]), ALU.mult)
                v.drain()
                v.tensor_tensor(yc[:, :, :, :], yb[:, :, 0:2, :], yb[:, :, 2:4, :], ALU.add)
                v.drain()
                v.tensor_tensor(yc[:, :, 0, :], yc[:, :, 0, :], yc[:, :, 1, :], ALU.add)
                v.drain()
                dve.wait_ge(ost[q], 8 * (k - q))
                v.tensor_tensor(yo[q][:, :, :], yc[:, :, 0, :], hr[q][:, :, :], ALU.add).then_inc(S["yo_done"], 1)

            chunks(dve, step)


_TAP_ORDER = [t for ts in TAP_TILES for t in ts]


def kernel(**inputs):
    import numpy as np
    import concourse.bacc as bacc
    from concourse.bass_utils import run_bass_kernel_spmd

    g = {k: np.asarray(v) for k, v in inputs.items()}

    def by_tap(w):
        r = w.reshape(CH, TAPS, -1).transpose(1, 0, 2)[_TAP_ORDER]
        return np.ascontiguousarray(r.reshape(TAPS * CH, -1))

    col = lambda a: np.ascontiguousarray(a.reshape(-1, 1))
    row = lambda a: np.ascontiguousarray(a.reshape(1, -1))
    arrays = {
        "x": g["x"], "cls_tok": col(g["cls_tok"]),
        "tok_W1": by_tap(g["L0_tok_W1"]), "tok_b1": col(g["L0_tok_b1"]),
        "tok_W2": np.ascontiguousarray(by_tap(np.ascontiguousarray(g["L0_tok_W2"].T)).T),
        "tok_b2": by_tap(col(g["L0_tok_b2"])),
        "tok_W3": by_tap(g["L0_tok_W3"]), "tok_b3": col(g["L0_tok_b3"]),
        "A_diag": col(g["L0_attn_A_diag"]),
        "B": np.ascontiguousarray(g["L0_attn_B"].transpose(1, 2, 0).reshape(CH, 2 * CH)),
        "C": np.ascontiguousarray(g["L0_attn_C"].transpose(2, 1, 0).reshape(2 * CH, CH)),
        "D": col(g["L0_attn_D"]), "dt": col(g["L0_attn_dt"]),
        "W_gat": g["L0_ffn_W_gat"], "att_src": row(g["L0_ffn_att_src"]), "att_dst": row(g["L0_ffn_att_dst"]),
        "b_gat": row(g["L0_ffn_b_gat"]), "ln_gamma": row(g["L0_ffn_ln_gamma"]),
        "ln_beta": row(g["L0_ffn_ln_beta"]), "W1": g["L0_ffn_W1"],
        "b1": np.ascontiguousarray(g["L0_ffn_b1"].T), "W2": g["L0_ffn_W2"], "b2": row(g["L0_ffn_b2"]),
        "edges": g["L0_ffn_edge_index"],
    }
    nc = bacc.Bacc("TRN2", target_bir_lowering=False, num_devices=1)
    args = [nc.dram_tensor("in_" + k, a.shape, mybir.dt.from_np(a.dtype), kind="ExternalInput").ap()
            for k, a in arrays.items()]
    args.append(nc.dram_tensor("out", [NODES, CH], f32, kind="ExternalOutput").ap())
    build(nc, *args)
    r = run_bass_kernel_spmd(nc, [{"in_" + k: a for k, a in arrays.items()}], core_ids=[0])
    return r.results[0]["out"].reshape(IMAGES, SEQ, CH)
```

```python
import concourse.bass as bass
from concourse import mybir
from contextlib import ExitStack

f32 = mybir.dt.float32
i32 = mybir.dt.int32
bf16 = mybir.dt.bfloat16
ALU = mybir.AluOpType
ACT = mybir.ActivationFunctionType
AX = mybir.AxisListType

IMAGES, CH, SIDE = 16, 64, 56
TOKENS = SIDE * SIDE
SEQ = TOKENS + 1
NODES = IMAGES * SEQ
ROWS = 8
CHUNK = ROWS * SIDE
CHUNKS = TOKENS // CHUNK
STEPS = CHUNK + 1
PAD = SIDE + 2
TAPS = 9
TAP_TILES = [(0, 1), (3, 4), (6, 7), (2, 5), (8,)]
FOLD = 4
FP = CHUNK // FOLD
HEADS, EXPERTS = 4, 4
HE = HEADS * EXPERTS
HIDDEN = 128
TW = HE + 2 * HEADS
GRAPH_NODES = 16 * 1024
EDGES = 262144
P = 128
LO = P
ETILES = EDGES // P
SORTED = EDGES + GRAPH_NODES
SCOLS = SORTED // P
HALF = 16
RING = 64
EROUNDS = ETILES // (2 * HALF)
GROUPS = ETILES // 4
SROUNDS = LO // (2 * HALF)
GROUP = 4
RG = 2 * HALF // GROUP
FLAG = 65536
BIG = 1.0e30
EPS = 1e-5
DENOM_EPS = 1e-16
GRAPH_IMAGES = -(-GRAPH_NODES // SEQ)
NT = 512
NCH = NODES // NT


def wait(eng, sem, value):
    if not (isinstance(value, int) and value <= 0):
        eng.wait_ge(sem, value)


def build(nc, x, cls_tok, tokW1, tokb1, tokW2, tokb2, tokW3, tokb3, A_diag, Bmat, Cmat, Dvec, dtv,
          W_gat, att_src, att_dst, b_gat, ln_gamma, ln_beta, W1, b1, W2, b2, edges, out):
    sorted_rec = nc.dram_tensor("sorted_rec", [SORTED, 2], i32, kind="Internal").ap()
    gathered = nc.dram_tensor("gathered", [P, SCOLS * TW], f32, kind="Internal").ap()
    table = nc.dram_tensor("table", [NODES, TW], f32, kind="Internal").ap()
    h_tok = nc.dram_tensor("h_tok", [NODES, CH], f32, kind="Internal").ap()
    xnT = nc.dram_tensor("xnT", [CH, NODES], f32, kind="Internal").ap()
    seg_scratch = nc.dram_tensor("seg_scratch", [2, P, P], i32, kind="Internal").ap()

    front(nc, x, cls_tok, tokW1, tokb1, tokW2, tokb2, tokW3, tokb3, A_diag, Bmat, Cmat, Dvec, dtv,
          W_gat, att_src, att_dst, edges, sorted_rec, gathered, table, h_tok, xnT, seg_scratch)
    back(nc, table, gathered, sorted_rec, seg_scratch, h_tok, xnT, b_gat, ln_gamma, ln_beta,
         W1, b1, W2, b2, out)


def front(nc, x, cls_tok, tokW1, tokb1, tokW2, tokb2, tokW3, tokb3, A_diag, Bmat, Cmat, Dvec, dtv,
          W_gat, att_src, att_dst, edges, sorted_rec, gathered, table, h_tok, xnT, seg_scratch):
    ctx = ExitStack()
    with ctx:
        def sb(name, shape, dt=f32):
            return ctx.enter_context(nc.sbuf_tensor(name, shape, dt))

        def pb(name, shape, dt=f32):
            return ctx.enter_context(nc.psum_tensor(name, shape, dt))

        def sem(name):
            return ctx.enter_context(nc.semaphore(name))

        ident = sb("ident", [P, P])
        ident_b = sb("ident_b", [P, P], bf16)
        before = sb("before", [P, P])
        above = sb("above", [P, P])
        iota_i = sb("iota_i", [P, P], i32)
        iota_f = sb("iota_f", [P, P])
        part_i = sb("part_i", [P, 1], i32)
        part_f = sb("part_f", [P, 1])
        zero_b = sb("zero_b", [P, NT], bf16)
        zero_f = sb("zero_f", [P, P])
        center = sb("center", [CH, CH])
        mean = sb("mean", [CH, CH])
        eps_c = sb("eps_c", [P, 1])

        src_i = sb("src_i", [P, ETILES], i32)[:, :]
        dst_f = sb("dst_f", [P, ETILES])[:, :]
        pos_all = sb("pos_all", [P, ETILES], i32)
        arena = sb("arena", [P, ETILES * 5 // 2 + 3 * GROUP // 2])
        at = [0]

        def carve(n, dt=f32):
            words = n if dt != bf16 else n // 2
            v = arena[:, at[0]:at[0] + words]
            at[0] += words
            return v if dt == f32 else v.bitcast(dt)

        IDS = ETILES + GROUP
        lo_f = carve(ETILES)
        lo_b = carve(IDS, bf16)
        hi_b = carve(IDS, bf16)
        hi128_b = carve(IDS, bf16)
        tabs = [arena[:, n * STEPS:(n + 1) * STEPS] for n in range(4)]
        tab_a, tab_b, tab_k, tab_c = tabs

        xa = [sb(f"xa{n}", [P, PAD * PAD]) for n in range(2)]
        xb = [sb(f"xb{n}", [P, PAD * PAD]) for n in range(2)]
        dst_i = xa[0][:, 0:ETILES].bitcast(i32)
        tmp_i = xb[0][:, 0:ETILES].bitcast(i32)
        oh_hi = [sb(f"oh_hi{n}", [P, P, GROUP], bf16) for n in range(2)]
        oh_lo = [sb(f"oh_lo{n}", [P, P, GROUP], bf16) for n in range(2)]
        iota_g = sb("iota_g", [P, P, GROUP], bf16)
        hiT = [sb(f"hiT{n}", [P, GROUP * P]) for n in range(2)]
        neg_part = sb("neg_part", [P, 1])
        hist = sb("hist", [P, GROUP * P])
        rank = sb("rank", [P, HALF])
        first = sb("first", [P, HALF])
        pos = [sb(f"pos{n}", [P, HALF], i32) for n in range(2)]
        rec = [sb(f"rec{n}", [P, HALF, 2], i32) for n in range(2)]
        counts = sb("counts", [P, GROUP * P])
        deg = sb("deg", [P, P])
        incl = sb("incl", [P, P])
        base = sb("base", [P, P])
        rowbase = sb("rowbase", [P, 1])
        seg_i = sb("seg_i", [P, 2, P], i32)
        node_f = sb("node_f", [P, P])
        node_flag = sb("node_flag", [P, P])
        base_i = seg_i[:, 0, :]
        pick = [sb(f"pick{n}", [P, RING, 2], i32) for n in range(2)]
        ring = [sb(f"ring{n}", [P, RING, TW]) for n in range(2)]

        NTT = len(TAP_TILES)
        w1 = sb("w1", [P, NTT, CH])
        w2 = sb("w2", [CH, TAPS * CH])
        w3 = sb("w3", [P, NTT, CH])
        tb1 = sb("tb1", [CH, 1])
        tb2 = sb("tb2", [P, NTT])
        tb3 = sb("tb3", [CH, 1])
        b_sb = sb("b_sb", [CH, 2 * CH])
        c_sb = sb("c_sb", [2 * CH, CH])
        d_sb = sb("d_sb", [CH, 1])
        cls_c = sb("cls_c", [CH, 1])
        adiag = sb("adiag", [P, 1])
        dts = sb("dts", [P, 1])
        wproj = sb("wproj", [CH, TW])
        att_bc = sb("att_bc", [CH, 2, HE])
        wtmp = sb("wtmp", [CH, 2, HE])
        par = sb("par", [P, 16])

        h1 = sb("h1", [CH, CHUNK])
        gate = [sb(f"gate{n}", [P, CHUNK]) for n in range(2)]
        prod = sb("prod", [P, NTT, CHUNK])
        sort_junk = prod[:, 0:2, :].rearrange("p a b -> p (a b)")[:, 0:GROUP * P].rearrange("p (j n) -> p j n", n=P)
        first_junk = prod[:, 2:4, :].rearrange("p a b -> p (a b)")[:, 0:GROUP * P].rearrange("p (j n) -> p j n", n=P)
        hT = [sb(f"hT{n}", [CH, TOKENS]) for n in range(2)]
        sq = [sb(f"sq{n}", [CH, CHUNK]) for n in range(2)]
        std = [sb(f"std{n}", [CH, CHUNK]) for n in range(2)]
        u = [sb(f"u{n}", [CH, CHUNK]) for n in range(2)]
        fin = [sb(f"fin{n}", [P, CHUNK]) for n in range(2)]
        wst = [sb(f"wst{n}", [P, CHUNK]) for n in range(2)]
        y = sb("y", [P, CHUNK])
        carry = sb("carry", [P, 2])
        start = sb("start", [P, 2])
        h2 = [sb(f"h2{n}", [CH, CHUNK]) for n in range(2)]
        xn = [sb(f"xn{n}", [CH, CHUNK]) for n in range(2)]
        t_out = [sb(f"t_out{n}", [P, FOLD, TW]) for n in range(2)]
        h_out = [sb(f"h_out{n}", [P, FOLD, CH]) for n in range(2)]

        bank = [pb(f"bank{n}", [P, 512]) for n in range(8)]
        p_hi, p_dst, p_first, p_hist = bank[0:2], bank[2:4], bank[4:6], bank[6]

        names = """consts weights_in edges_in ids_ready groups_oh hist_added counts_done totals_ready
            rowbase_done base_ready ids_bcast hiT_ready hist_copied first_done first_read
            ranked group_pos pos_ready staged scat0 scat1 sorted_done tabs_ready pads_zero
            x_in conv_done h1_done s_ps gate_done prod_done tok_done hT_done cent_done sq_done
            var_done std_done u_done bu_done y_done co_done h2_done cent2_done sq2_done var2_done
            std2_done xn_done tm_done tm_copied fin_read
            tm_st0 tm_st1 pick0 pick1 gath0 gath1 ring_st0 ring_st1 seg_st cls_in cls_ps cls_sb
            cls_st wp1 par_act par_dve waited""".split()
        S = {n: sem(n) for n in names}
        scat = [S["scat0"], S["scat1"]]
        pick_in = [S["pick0"], S["pick1"]]
        gath = [S["gath0"], S["gath1"]]
        ring_st = [S["ring_st0"], S["ring_st1"]]
        tm_st = [S["tm_st0"], S["tm_st1"]]

        src_v = edges[0, :].rearrange("(p t) -> p t", t=ETILES)
        dst_v = edges[1, :].rearrange("(p t) -> p t", t=ETILES)
        sorted_v = sorted_rec.rearrange("(p c) w -> p c w", c=SCOLS)

        def tile_rows(t):
            return CH * len(TAP_TILES[t])

        def taps_view(buf, c, t):
            src = xa if t < 3 else xb
            row, col = [(0, 0), (1, 0), (2, 0), (0, 2), (2, 2)][t]
            v = src[buf][0:tile_rows(t), :].rearrange("p (r q) -> p r q", q=PAD)
            return v[:, ROWS * c + row:ROWS * c + row + ROWS, col:col + SIDE]

        def r3(ap):
            return ap.rearrange("p (r q) -> p r q", q=SIDE)

        WEIGHT_LOADS = 3 * NTT + 14

        def slots(ba):
            return range(CHUNKS + 2 if isinstance(ba, int) and ba == IMAGES - 1 else CHUNKS)

        def active(bt, ba, c):
            first = isinstance(ba, int) and ba == 0
            att = ba is not None
            return (bt is not None and c < CHUNKS, att and c < CHUNKS, att and (not first or c >= 1)
                    and c <= CHUNKS, att and (not first or c >= 2))

        def steps(eng, step, last_apart=False):
            step(0, 0, None, None)
            step(1, 1, 0, 0)
            with eng.Fori(1, IMAGES // 2 - last_apart) as i:
                step(2 * i, 0, 2 * i - 1, 1)
                step(2 * i + 1, 1, 2 * i, 0)
            if last_apart:
                step(IMAGES - 2, 0, IMAGES - 3, 1)
                step(IMAGES - 1, 1, IMAGES - 2, 0)
            step(None, None, IMAGES - 1, 1)

        block = ctx.enter_context(nc.Block())

        @block.sync
        def _(sp):
            sp.dma_start(dst_i, dst_v).then_inc(S["edges_in"], 16)
            sp.dma_start(src_i, src_v).then_inc(S["edges_in"], 16)
            n = [0]

            def w(dst, src):
                n[0] += 1
                sp.dma_start(dst, src).then_inc(S["weights_in"], 16)

            row = 0
            for t in range(NTT):
                k = tile_rows(t)
                w(w1[0:k, t, :], tokW1[row:row + k, :])
                w(w3[0:k, t, :], tokW3[row:row + k, :])
                row += k
            w(w2[:, :], tokW2)
            w(tb1[:, :], tokb1)
            for t in range(NTT):
                w(tb2[0:tile_rows(t), t:t + 1], tokb2[t * P:t * P + tile_rows(t), :])
            w(tb3[:, :], tokb3)
            w(b_sb[:, :], Bmat)
            w(c_sb[:, :], Cmat)
            w(d_sb[:, :], Dvec)
            for g in range(2):
                w(adiag[g * CH:(g + 1) * CH, :], A_diag)
                w(dts[g * CH:(g + 1) * CH, :], dtv)
            w(wproj[:, 0:HE], W_gat)
            w(att_bc[:, 0, :], att_src.partition_broadcast(CH))
            w(att_bc[:, 1, :], att_dst.partition_broadcast(CH))
            w(cls_c[:, :], cls_tok)
            assert n[0] == WEIGHT_LOADS

            sp.wait_ge(S["base_ready"], 1)
            sp.dma_start(seg_scratch.rearrange("a p q -> p a q"), seg_i[:, :, :]).then_inc(S["seg_st"], 16)
            sp.wait_ge(S["cls_sb"], 8)
            for dst, s in ((table.rearrange("(b s) w -> b s w", s=SEQ)[:, 0, :], t_out[0][0:IMAGES, 0, :]),
                           (h_tok.rearrange("(b s) w -> b s w", s=SEQ)[:, 0, :], h_out[0][0:IMAGES, 0, :]),
                           (xnT.rearrange("c (b s) -> c b s", s=SEQ)[:, :, 0:1], xn[0][:, 0:IMAGES].unsqueeze(2))):
                sp.dma_start(dst, s, allow_slow_non_contiguous=True).then_inc(S["cls_st"], 16)
            sp.wait_ge(S["cls_st"], 48)

            def load_image(b, buf):
                src = x[b, :, :, :]
                va = xa[buf][:, :].rearrange("p (r q) -> p r q", q=PAD)
                vb = xb[buf][:, :].rearrange("p (r q) -> p r q", q=PAD)
                sp.dma_start(va[0:CH, 1:1 + SIDE, 1:1 + SIDE], src).then_inc(S["x_in"], 16)
                sp.dma_start(va[CH:P, 1:1 + SIDE, 0:SIDE], src).then_inc(S["x_in"], 16)
                sp.dma_start(vb[0:CH, 1:1 + SIDE, 1:1 + SIDE], src).then_inc(S["x_in"], 16)
                sp.dma_start(vb[CH:P, 0:SIDE, 1:1 + SIDE], src).then_inc(S["x_in"], 16)

            def store_chunk(b, c, q):
                sp.wait_ge(S["tm_copied"], 2 * (b * CHUNKS + c) + 2)
                sp.sem_inc(S["waited"], 1)
                node = b * SEQ + 1 + c * CHUNK
                sp.dma_start(table[bass.ds(node, CHUNK), :].rearrange("(p j) w -> p j w", j=FOLD),
                             t_out[q][0:FP, :, :]).then_inc(tm_st[q], 16)
                sp.dma_start(h_tok[bass.ds(node, CHUNK), :].rearrange("(p j) w -> p j w", j=FOLD),
                             h_out[q][0:FP, :, :]).then_inc(tm_st[q], 16)
                sp.dma_start(xnT[:, bass.ds(node, CHUNK)], xn[q][:, :]).then_inc(tm_st[q], 16)

            sp.wait_ge(S["pads_zero"], 1)
            load_image(0, 0)

            def loads_and_stores(b_tok, tok_par, b_att, att_par):
                if b_tok is not None and not (isinstance(b_tok, int) and b_tok == IMAGES - 1):
                    sp.wait_ge(S["x_in"], 64 * (b_tok + 1))
                    sp.sem_inc(S["waited"], 1)
                    if not (isinstance(b_tok, int) and b_tok == 0):
                        sp.wait_ge(S["prod_done"], 5 * CHUNKS * b_tok)
                        sp.sem_inc(S["waited"], 1)
                        sp.wait_ge(S["conv_done"], CHUNKS * b_tok)
                    sp.sem_inc(S["waited"], 1)
                    load_image(b_tok + 1, 1 - tok_par)
                for c in slots(b_att):
                    if active(b_tok, b_att, c)[3]:
                        q = (att_par * CHUNKS + c) % 2
                        if c >= 2:
                            store_chunk(b_att, c - 2, q)
                        else:
                            store_chunk(b_att - 1, c + CHUNKS - 2, q)

            steps(sp, loads_and_stores, last_apart=True)
            sp.wait_ge(S["seg_st"], 16)
            for q in range(2):
                sp.wait_ge(tm_st[q], 48 * CHUNKS * IMAGES // 2)

        @block.gpsimd
        def _(pool):
            g = nc.gpsimd
            g.memset(ident[:, :], 0.0)
            g.memset(before[:, :], 1.0)
            g.memset(above[:, :], 1.0)
            g.memset(zero_f[:, :], 0.0)
            g.memset(zero_b[:, :], 0.0)
            g.memset(mean[:, :], 1.0 / CH)
            g.memset(center[:, :], -1.0 / CH)
            g.memset(eps_c[:, :], EPS)
            g.iota(iota_i[:, :], pattern=[[1, P]], base=0, channel_multiplier=0)
            g.iota(part_i[:, :], pattern=[[1, 1]], base=0, channel_multiplier=1)
            g.drain()
            g.affine_select(out=ident[:, :], in_=ident[:, :], compare_op=ALU.not_equal, fill=1.0, base=0,
                            pattern=[[-1, P]], channel_multiplier=1)
            g.affine_select(out=before[:, :], in_=before[:, :], compare_op=ALU.is_gt, fill=0.0, base=0,
                            pattern=[[-1, P]], channel_multiplier=1)
            g.affine_select(out=above[:, :], in_=above[:, :], compare_op=ALU.is_gt, fill=0.0, base=0,
                            pattern=[[1, P]], channel_multiplier=-1)
            g.affine_select(out=center[:, :], in_=center[:, :], compare_op=ALU.not_equal,
                            fill=1.0 - 1.0 / CH, base=0, pattern=[[-1, CH]], channel_multiplier=1)
            g.drain()
            g.nop().then_inc(S["consts"], 1)

            pool.wait_ge(S["ids_ready"], 1)
            for t in (*xa, *xb):
                g.memset(t[:, :], 0.0)
            g.drain()
            g.nop().then_inc(S["pads_zero"], 1)

            def scatter_half(k, h, places, sources, targets):
                g.tensor_copy(pos[h][:, :], places)
                g.tensor_copy(rec[h][:, :, 0], sources)
                g.tensor_copy(rec[h][:, :, 1], targets).then_inc(S["staged"], 1)
                pool.wait_ge(S["staged"], k + 1)
                pool.sem_inc(S["waited"], 1)
                for j in range(HALF):
                    g.indirect_dma_start(
                        out=sorted_rec, out_offset=bass.IndirectOffsetOnAxis(ap=pos[h][:, j:j + 1], axis=0),
                        in_=rec[h][:, j, :], in_offset=None).then_inc(scat[h], 16)

            def scatter_edges(i):
                for h in range(2):
                    cols = bass.ds((2 * i + h) * HALF, HALF)
                    pool.wait_ge(S["pos_ready"], 2 * i + h + 1)
                    wait(pool, scat[h], 16 * HALF * i)
                    pool.sem_inc(S["waited"], 1)
                    scatter_half(2 * i + h, h, pos_all[:, cols], src_i[:, cols], dst_f[:, cols])

            scatter_edges(0)
            with pool.Fori(1, EROUNDS) as i:
                scatter_edges(i)
            for i in range(SROUNDS):
                for h in range(2):
                    cols = slice((2 * i + h) * HALF, (2 * i + h + 1) * HALF)
                    pool.wait_ge(scat[h], 16 * HALF * (EROUNDS + i))
                    scatter_half(2 * (EROUNDS + i) + h, h, base_i[:, cols], node_f[:, cols], node_flag[:, cols])
            for h in range(2):
                pool.wait_ge(scat[h], 16 * HALF * (EROUNDS + SROUNDS))
            pool.wait_ge(S["cls_st"], 48)
            for q in range(2):
                pool.wait_ge(tm_st[q], 48 * CHUNKS * GRAPH_IMAGES // 2)

            BLOCKS = SCOLS // RING

            def load_pick(k, h):
                g.dma_start(pick[h][:, :, :], sorted_v[:, bass.ds(k * RING, RING), :]).then_inc(pick_in[h], 16)

            def gather_block(i, h, first=False, last=False):
                k = 2 * i + h
                pool.wait_ge(pick_in[h], 16 * (i + 1))
                wait(pool, ring_st[h], 16 * i)
                pool.sem_inc(S["waited"], 1)
                for j in range(RING):
                    if j == 8 and not first:
                        pool.wait_ge(gath[1 - h], 16 * RING * (i + h))
                        store_block(k - 1, 1 - h)
                        if not last:
                            load_pick(k + 1, 1 - h)
                    g.indirect_dma_start(
                        out=ring[h][:, j, :], out_offset=None, in_=table[0:GRAPH_NODES, :],
                        in_offset=bass.IndirectOffsetOnAxis(ap=pick[h][:, j, 0:1], axis=0)).then_inc(gath[h], 16)

            def store_block(k, h):
                g.dma_start(gathered[:, bass.ds(k * RING * TW, RING * TW)],
                            ring[h][:, :, :].rearrange("p a b -> p (a b)")).then_inc(ring_st[h], 16)

            load_pick(0, 0)
            load_pick(1, 1)
            gather_block(0, 0, first=True)
            gather_block(0, 1)
            with pool.Fori(1, BLOCKS // 2 - 1) as i:
                for h in range(2):
                    gather_block(i, h)
            gather_block(BLOCKS // 2 - 1, 0)
            gather_block(BLOCKS // 2 - 1, 1, last=True)
            pool.wait_ge(gath[1], 16 * RING * (BLOCKS // 2))
            store_block(BLOCKS - 1, 1)
            for h in range(2):
                pool.wait_ge(ring_st[h], 16 * (BLOCKS // 2))

        @block.tensor
        def _(pe):
            mm = nc.tensor.matmul
            pe.wait_ge(S["ids_ready"], 1)
            mm(p_hist[:, :], zero_b[:, 0:P], zero_b[:, :], start=True, stop=False)
            def count(buf, last=False):
                for j in range(GROUP):
                    m = mm(p_hist[:, j * P:(j + 1) * P], oh_hi[buf][:, :, j], oh_lo[buf][:, :, j],
                           start=False, stop=last and j == GROUP - 1)
                m.then_inc(S["hist_added"], 1)

            def count_pair(q):
                for n in range(2):
                    pe.wait_ge(S["groups_oh"], q + n + 1)
                    count(n)

            count_pair(0)
            with pe.Fori(1, GROUPS // 2) as i:
                count_pair(2 * i)
            mm(p_hist[:, :], zero_b[:, 0:P], zero_b[:, :], start=False, stop=True).then_inc(S["counts_done"], 1)
            pe.wait_ge(S["totals_ready"], 1)
            mm(p_hi[0][:, 0:1], above[:, :], incl[:, P - 1:P], start=True, stop=True).then_inc(S["rowbase_done"], 1)
            pe.wait_ge(S["base_ready"], 1)

            def broadcast_ids(q, t0, b):
                wait(pe, S["hiT_ready"], q - 1)
                wait(pe, S["ranked"], q - 1)
                for j in range(GROUP):
                    mm(p_hi[b][:, j * P:(j + 1) * P], hi_b[:, bass.ds(t0 + j, 1)].broadcast_to([P, P]),
                       ident_b[:, :], start=True, stop=True)
                for j in range(GROUP):
                    o = p_dst[b][:, j * P:(j + 1) * P]
                    mm(o, hi128_b[:, bass.ds(t0 + j, 1)].broadcast_to([P, P]), ident_b[:, :],
                       start=True, stop=False)
                    m = mm(o, lo_b[:, bass.ds(t0 + j, 1)].broadcast_to([P, P]), ident_b[:, :],
                           start=False, stop=True)
                m.then_inc(S["ids_bcast"], 1)

            def sort_round(i):
                for gi in range(RG):
                    q = i * RG + gi
                    b = gi % 2
                    broadcast_ids(q + 1, (i * RG + gi + 1) * GROUP, 1 - b)
                    pe.wait_ge(S["hiT_ready"], q + 1)
                    wait(pe, S["hist_copied"], q)
                    wait(pe, S["group_pos"], q - 1)
                    for j in range(GROUP):
                        m = mm(p_first[b][:, j * P:(j + 1) * P], hiT[b][:, j * P:(j + 1) * P],
                               hist[:, j * P:(j + 1) * P], start=True, stop=True)
                    m.then_inc(S["first_done"], 1)
                    pe.wait_ge(S["groups_oh"], GROUPS + q + 1)
                    mm(p_hist[:, :], ident[:, :], hist[:, :], start=True, stop=False)
                    count(b, last=True)

            broadcast_ids(0, 0, 0)
            sort_round(0)
            with pe.Fori(1, EROUNDS) as i:
                sort_round(i)

            pe.wait_ge(S["wp1"], 1)
            pe.wait_ge(S["tabs_ready"], 1)
            N = IMAGES
            mm(bank[4][0:CH, 0:N], center[:, :], hT[0][:, 0:N], start=True, stop=True).then_inc(S["cls_ps"], 1)
            pe.wait_ge(S["cls_sb"], 1)
            mm(bank[5][0:CH, 0:N], mean[:, :], sq[0][:, 0:N], start=True, stop=True).then_inc(S["cls_ps"], 1)
            pe.wait_ge(S["cls_sb"], 2)
            mm(bank[6][:, 0:N], b_sb[:, :], u[0][:, 0:N], start=True, stop=True).then_inc(S["cls_ps"], 1)
            pe.wait_ge(S["cls_sb"], 3)
            mm(bank[7][0:CH, 0:N], c_sb[:, :], y[:, 0:N], start=True, stop=True).then_inc(S["cls_ps"], 1)
            pe.wait_ge(S["cls_sb"], 4)
            mm(bank[4][0:CH, 0:N], center[:, :], h2[0][:, 0:N], start=True, stop=True).then_inc(S["cls_ps"], 1)
            pe.wait_ge(S["cls_sb"], 5)
            mm(bank[5][0:CH, 0:N], mean[:, :], sq[1][:, 0:N], start=True, stop=True).then_inc(S["cls_ps"], 1)
            pe.wait_ge(S["cls_sb"], 6)
            mm(bank[6][0:N, 0:TW], xn[0][:, 0:N], wproj[:, :], start=True, stop=True)
            mm(bank[6][0:N, 128:128 + CH], h2[0][:, 0:N], ident[0:CH, 0:CH], start=True, stop=True)\
                .then_inc(S["cls_ps"], 1)
            pe.wait_ge(S["cls_sb"], 8)

            def step(bt, tp, ba, ap):
                nt = bt * CHUNKS if bt is not None else None
                na = ba * CHUNKS if ba is not None else None
                zero = isinstance(bt, int) and bt == 0
                zero_a = isinstance(ba, int) and ba == 0

                def conv(c):
                    k = nt + c
                    if c == 0:
                        pe.wait_ge(S["x_in"], 64 * (bt + 1))
                    if not (zero and c == 0):
                        pe.wait_ge(S["h1_done"], k)
                    for t in range(NTT):
                        n = tile_rows(t)
                        m = mm(bank[0][0:CH, 0:CHUNK], w1[0:n, t, :], taps_view(tp, c, t),
                               start=t == 0, stop=t == NTT - 1)
                    m.then_inc(S["conv_done"], 1)

                def gates(c, t):
                    k = 5 * (nt + c) + t
                    if t == 0:
                        pe.wait_ge(S["h1_done"], nt + c + 1)
                    if not (zero and c == 0 and t < 2):
                        pe.wait_ge(S["gate_done"], k - 1)
                        if t == NTT - 1:
                            pe.sem_inc(S["waited"], 1)
                    n = tile_rows(t)
                    o = (5 * (tp * CHUNKS + c) + t) % 2
                    mm(bank[1 + o][0:n, 0:CHUNK], w2[:, 128 * t:128 * t + n], h1[:, :],
                       start=True, stop=True).then_inc(S["s_ps"], 1)

                def project(c, t):
                    k = 5 * (nt + c) + t
                    n = tile_rows(t)
                    pe.wait_ge(S["prod_done"], k + 1)
                    if t == 0 and not (zero and c == 0):
                        pe.wait_ge(S["hT_done"], nt + c)
                    pe.sem_inc(S["waited"], 1)
                    m = mm(bank[3][0:CH, 0:CHUNK], w3[0:n, t, :], prod[0:n, t, :], start=t == 0, stop=t == NTT - 1)
                    if t == NTT - 1:
                        m.then_inc(S["tok_done"], 1)

                tok = bt is not None
                att = ba is not None
                if tok:
                    conv(0)
                for c in slots(ba):
                    tc, a0, a1, a2 = active(bt, ba, c)
                    if a0:
                        pe.wait_ge(S["hT_done"], na + CHUNKS)
                        if not (zero_a and c == 0):
                            pe.wait_ge(S["u_done"], na + c)
                        pe.sem_inc(S["waited"], 1)
                        mm(bank[4][0:CH, 0:CHUNK], center[:, :], hT[ap][:, c * CHUNK:(c + 1) * CHUNK],
                           start=True, stop=True).then_inc(S["cent_done"], 1)
                    if tc:
                        gates(c, 0)
                    if a2:
                        q = (ap * CHUNKS + c - 2) % 2
                        pe.wait_ge(S["xn_done"], na + c - 1)
                        pe.wait_ge(S["fin_read"], na + min(c, CHUNKS))
                        for j in range(FOLD):
                            mm(bank[6][0:FP, j * P:j * P + TW], xn[q][:, j:CHUNK:FOLD], wproj[:, :],
                               start=True, stop=True)
                            m = mm(bank[6][0:FP, j * P + 32:j * P + 32 + CH], h2[q][:, j:CHUNK:FOLD],
                                   ident[0:CH, 0:CH], start=True, stop=True)
                        m.then_inc(S["tm_done"], 1)
                    if tc:
                        gates(c, 1)
                    if a1:
                        pe.wait_ge(S["y_done"], na + c)
                        if c > 1 or not zero_a:
                            pe.wait_ge(S["xn_done"], na + c - 1)
                        mm(bank[7][0:CH, 0:CHUNK], c_sb[:, :], y[:, :], start=True, stop=True)\
                            .then_inc(S["co_done"], 1)
                    if tc:
                        gates(c, 2)
                    if a0:
                        pe.wait_ge(S["sq_done"], na + c + 1)
                        pe.sem_inc(S["waited"], 1)
                        mm(bank[5][0:CH, 0:CHUNK], mean[:, :], sq[0][:, :], start=True, stop=True)\
                            .then_inc(S["var_done"], 1)
                    if tc:
                        gates(c, 3)
                    if a1:
                        pe.wait_ge(S["h2_done"], na + c)
                        pe.sem_inc(S["waited"], 1)
                        mm(bank[7][0:CH, 0:CHUNK], center[:, :], h2[(ap * CHUNKS + c - 1) % 2][:, :],
                           start=True, stop=True).then_inc(S["cent2_done"], 1)
                    if tc:
                        gates(c, 4)
                        project(c, 0)
                    if a1:
                        pe.wait_ge(S["sq2_done"], na + c)
                        if a2:
                            pe.wait_ge(S["tm_copied"], 2 * (na + c - 1))
                        pe.sem_inc(S["waited"], 1)
                        mm(bank[6][0:CH, 0:CHUNK], mean[:, :], sq[1][:, :], start=True, stop=True)\
                            .then_inc(S["var2_done"], 1)
                    if tc:
                        if c + 1 < CHUNKS:
                            conv(c + 1)
                        project(c, 1)
                    if a0:
                        pe.wait_ge(S["u_done"], na + c + 1)
                        if a1:
                            pe.wait_ge(S["std2_done"], na + c)
                        elif not zero_a:
                            pe.wait_ge(S["tm_copied"], 2 * na)
                        mm(bank[6][:, 0:CHUNK], b_sb[:, :], u[(ap * CHUNKS + c) % 2][:, :], start=True, stop=True)\
                            .then_inc(S["bu_done"], 1)
                    if tc:
                        project(c, 2)
                        project(c, 3)
                        project(c, 4)

            steps(pe, step)

        @block.scalar
        def _(act):
            a = nc.scalar.activation
            act.wait_ge(S["base_ready"], 1)

            def hi_one_hot(q, b):
                act.wait_ge(S["ids_bcast"], q + 1)
                wait(act, S["first_done"], q - 1)
                a(hiT[b][:, :], p_hi[b][:, :], ACT.Abs, bias=neg_part[:, :])
                nc.scalar.drain()
                a(hiT[b][:, :], hiT[b][:, :], ACT.Relu, scale=-1.0, bias=1.0).then_inc(S["hiT_ready"], 1)

            def sort_round(i):
                for h in range(2):
                    for g in range(RG // 2):
                        gi = h * (RG // 2) + g
                        q = i * RG + gi
                        hi_one_hot(q + 1, 1 - gi % 2)
                        act.wait_ge(S["hist_added"], GROUPS + q + 1)
                        a(hist[:, :], p_hist[:, :], ACT.Copy).then_inc(S["hist_copied"], 1)

            hi_one_hot(0, 0)
            sort_round(0)
            with act.Fori(1, EROUNDS) as i:
                sort_round(i)

            act.wait_ge(S["weights_in"], 16 * WEIGHT_LOADS)
            a(par[:, 0:1], dts[:, :], ACT.Sigmoid).then_inc(S["par_act"], 1)
            act.wait_ge(S["par_dve"], 1)
            a(par[:, 3:4], par[:, 2:3], ACT.Sqrt).then_inc(S["par_act"], 1)

            N = IMAGES
            act.wait_ge(S["cls_ps"], 1)
            a(sq[0][:, 0:N], bank[4][0:CH, 0:N], ACT.Square).then_inc(S["cls_sb"], 1)
            act.wait_ge(S["cls_ps"], 2)
            a(std[0][:, 0:N], bank[5][0:CH, 0:N], ACT.Sqrt, bias=eps_c[0:CH, :]).then_inc(S["cls_in"], 1)
            act.wait_ge(S["cls_ps"], 5)
            a(sq[1][:, 0:N], bank[4][0:CH, 0:N], ACT.Square).then_inc(S["cls_sb"], 1)
            act.wait_ge(S["cls_ps"], 6)
            a(std[1][:, 0:N], bank[5][0:CH, 0:N], ACT.Sqrt, bias=eps_c[0:CH, :]).then_inc(S["cls_in"], 1)
            act.wait_ge(S["cls_ps"], 7)
            a(t_out[0][0:N, 0, :], bank[6][0:N, 0:TW], ACT.Copy).then_inc(S["cls_sb"], 1)
            a(h_out[0][0:N, 0, :], bank[6][0:N, 128:128 + CH], ACT.Copy).then_inc(S["cls_sb"], 1)

            def step(bt, tp, ba, ap):
                nt = bt * CHUNKS if bt is not None else None
                na = ba * CHUNKS if ba is not None else None
                tok = bt is not None
                att = ba is not None
                zero = isinstance(bt, int) and bt == 0
                zero_a = isinstance(ba, int) and ba == 0

                def relu(c):
                    act.wait_ge(S["conv_done"], nt + c + 1)
                    if not (zero and c == 0):
                        act.wait_ge(S["s_ps"], 5 * (nt + c))
                    a(h1[:, :], bank[0][0:CH, 0:CHUNK], ACT.Relu, bias=tb1[:, :]).then_inc(S["h1_done"], 1)

                def gate_(c, t):
                    k = 5 * (nt + c) + t
                    o = (5 * (tp * CHUNKS + c) + t) % 2
                    n = tile_rows(t)
                    act.wait_ge(S["s_ps"], k + 1)
                    if not (zero and c == 0 and t < 2):
                        act.wait_ge(S["prod_done"], k - 1)
                    a(gate[o][0:n, :], bank[1 + o][0:n, 0:CHUNK], ACT.Sigmoid, bias=tb2[0:n, t:t + 1])\
                        .then_inc(S["gate_done"], 1)

                if tok:
                    relu(0)
                for c in slots(ba):
                    tc, a0, a1, a2 = active(bt, ba, c)
                    if a0:
                        act.wait_ge(S["cent_done"], na + c + 1)
                        if not (zero_a and c == 0):
                            act.wait_ge(S["var_done"], na + c)
                        a(sq[0][:, :], bank[4][0:CH, 0:CHUNK], ACT.Square).then_inc(S["sq_done"], 1)
                    if tc:
                        gate_(c, 0)
                    if a2:
                        q = (ap * CHUNKS + c - 2) % 2
                        act.wait_ge(S["tm_done"], na + c - 1)
                        if not (zero_a and c - 2 < 2):
                            act.wait_ge(tm_st[q], 24 * (na + c - 2 - q))
                        v = bank[6][0:FP, :].rearrange("p (j w) -> p j w", w=P)
                        a(t_out[q][0:FP, :, :], v[:, :, 0:TW], ACT.Copy).then_inc(S["tm_copied"], 1)
                        a(h_out[q][0:FP, :, :], v[:, :, 32:32 + CH], ACT.Copy).then_inc(S["tm_copied"], 1)
                    if tc:
                        gate_(c, 1)
                        gate_(c, 2)
                        gate_(c, 3)
                    if a1:
                        act.wait_ge(S["cent2_done"], na + c)
                        if not (zero_a and c == 1):
                            act.wait_ge(S["var2_done"], na + c - 1)
                        a(sq[1][:, :], bank[7][0:CH, 0:CHUNK], ACT.Square).then_inc(S["sq2_done"], 1)
                    if tc:
                        gate_(c, 4)
                    if a0 or a1:
                        nc.scalar.preload_act_table_set("natural_log_exp_and_others")
                    if a0:
                        act.wait_ge(S["var_done"], na + c + 1)
                        wait(act, S["u_done"], na + c)
                        a(std[0][:, :], bank[5][0:CH, 0:CHUNK], ACT.Ln, bias=eps_c[0:CH, :])
                    if a1:
                        act.wait_ge(S["var2_done"], na + c)
                        wait(act, S["xn_done"], na + c - 1)
                        a(std[1][:, :], bank[6][0:CH, 0:CHUNK], ACT.Ln, bias=eps_c[0:CH, :])
                    if a0 or a1:
                        nc.scalar.drain()
                    if a0:
                        a(std[0][:, :], std[0][:, :], ACT.Exp, scale=-0.5).then_inc(S["std_done"], 1)
                    if a1:
                        a(std[1][:, :], std[1][:, :], ACT.Exp, scale=-0.5).then_inc(S["std2_done"], 1)
                    if tc:
                        if c + 1 < CHUNKS:
                            relu(c + 1)
                        act.wait_ge(S["tok_done"], nt + c + 1)
                        if att and not zero_a:
                            act.wait_ge(S["h2_done"], na - CHUNKS + c + 1)
                        a(hT[tp][:, c * CHUNK:(c + 1) * CHUNK], bank[3][0:CH, 0:CHUNK], ACT.Identity,
                          bias=tb3[:, :]).then_inc(S["hT_done"], 1)

            steps(act, step)

        @block.vector
        def _(dve):
            v = nc.vector
            dve.wait_ge(S["consts"], 1)
            dve.wait_ge(S["edges_in"], 32)
            v.tensor_copy(ident_b[:, :], ident[:, :])
            v.tensor_copy(iota_f[:, :], iota_i[:, :])
            v.tensor_copy(iota_g[:, :, :], iota_i[:, :].unsqueeze(2).broadcast_to([P, P, GROUP]))
            v.memset(lo_b[:, ETILES:IDS], 0.0)
            v.memset(hi_b[:, ETILES:IDS], 0.0)
            v.memset(hi128_b[:, ETILES:IDS], 0.0)
            v.tensor_copy(part_f[:, :], part_i[:, :])
            v.tensor_single_scalar(tmp_i, dst_i, 7, ALU.arith_shift_right)
            v.tensor_copy(dst_f, dst_i)
            v.drain()
            v.tensor_copy(hi_b[:, 0:ETILES], tmp_i)
            v.tensor_scalar(neg_part[:, :], part_f[:, :], -1.0, None, ALU.mult)
            v.tensor_scalar(hi128_b[:, 0:ETILES], tmp_i, float(LO), None, ALU.mult)
            v.tensor_scalar(node_f[:, :], part_f[:, 0:1].broadcast_to([P, P]), float(LO), None, ALU.mult)
            v.drain()
            v.tensor_tensor(lo_f, dst_f, hi128_b[:, 0:ETILES], ALU.subtract)
            v.tensor_tensor(node_f[:, :], node_f[:, :], iota_f[:, :], ALU.add)
            v.drain()
            v.tensor_copy(lo_b[:, 0:ETILES], lo_f)
            v.tensor_scalar(node_flag[:, :], node_f[:, :], float(FLAG), None, ALU.add)
            v.drain()
            v.nop().then_inc(S["ids_ready"], 1)

            def one_hots(t0, b):
                for o, ids in ((oh_hi, hi_b), (oh_lo, lo_b)):
                    last = v.tensor_tensor(o[b][:, :, :], ids[:, bass.ds(t0, GROUP)].unsqueeze(1)
                                           .broadcast_to([P, P, GROUP]), iota_g[:, :, :], ALU.is_equal)
                last.then_inc(S["groups_oh"], 1)

            def count_pair(q):
                for n in range(2):
                    wait(dve, S["hist_added"], q + n - 1)
                    one_hots((q + n) * GROUP, n)

            count_pair(0)
            with dve.Fori(1, GROUPS // 2) as i:
                count_pair(2 * i)
            dve.wait_ge(S["counts_done"], 1)
            v.tensor_copy(counts[:, :], p_hist[:, :])
            v.drain()
            v.tensor_tensor(deg[:, :], counts[:, 0:P], counts[:, P:2 * P], ALU.add)
            v.drain()
            for j in (2, 3):
                v.tensor_tensor(deg[:, :], deg[:, :], counts[:, j * P:(j + 1) * P], ALU.add)
                v.drain()
            v.tensor_scalar(deg[:, :], deg[:, :], 1.0, None, ALU.add)
            v.drain()
            v.tensor_tensor_scan(incl[:, :], deg[:, :], zero_f[:, :], 0.0, ALU.add, ALU.add)
            v.drain()
            v.nop().then_inc(S["totals_ready"], 1)
            dve.wait_ge(S["rowbase_done"], 1)
            v.tensor_copy(rowbase[:, :], p_hi[0][:, 0:1])
            v.tensor_tensor(base[:, :], incl[:, :], deg[:, :], ALU.subtract)
            v.drain()
            v.tensor_scalar(base[:, :], base[:, :], rowbase[:, 0:1], None, ALU.add)
            v.drain()
            v.tensor_copy(seg_i[:, 0, :], base[:, :])
            v.tensor_tensor(incl[:, :], base[:, :], deg[:, :], ALU.add)
            v.drain()
            v.tensor_scalar(seg_i[:, 1, :], incl[:, :], -1.0, None, ALU.add)
            v.tensor_scalar(hist[:, 0:P], base[:, :], 1.0, None, ALU.add)
            v.drain()
            for j in (1, 2, 3):
                v.tensor_tensor(hist[:, j * P:(j + 1) * P], hist[:, (j - 1) * P:j * P],
                                counts[:, (j - 1) * P:j * P], ALU.add)
                v.drain()
            v.nop().then_inc(S["base_ready"], 1)

            def sort_round(i):
                for h in range(2):
                    for g in range(RG // 2):
                        gi = h * (RG // 2) + g
                        q = i * RG + gi
                        b = gi % 2
                        t0 = (i * RG + gi) * GROUP
                        dve.wait_ge(S["hist_added"], GROUPS + q - 1)
                        one_hots(t0, b)
                        dve.wait_ge(S["ids_bcast"], q + 1)
                        for j in range(GROUP):
                            last = v.scalar_tensor_tensor(
                                out=sort_junk[:, j, :], in0=p_dst[b][:, j * P:(j + 1) * P],
                                scalar=dst_f[:, bass.ds(t0 + j, 1)], in1=before[:, :], op0=ALU.is_equal,
                                op1=ALU.mult, accum_out=rank[:, g * GROUP + j:g * GROUP + j + 1])
                        last.then_inc(S["ranked"], 1)
                        dve.wait_ge(S["first_done"], q + 1)
                        for j in range(GROUP):
                            v.scalar_tensor_tensor(
                                out=first_junk[:, j, :], in0=iota_f[:, :],
                                scalar=lo_f[:, bass.ds(t0 + j, 1)], in1=p_first[b][:, j * P:(j + 1) * P],
                                op0=ALU.is_equal, op1=ALU.mult,
                                accum_out=first[:, g * GROUP + j:g * GROUP + j + 1])
                        v.drain().then_inc(S["group_pos"], 1)
                    v.tensor_tensor(pos_all[:, bass.ds((2 * i + h) * HALF, HALF)], rank[:, :], first[:, :], ALU.add)
                    v.drain().then_inc(S["pos_ready"], 1)

            sort_round(0)
            with dve.Fori(1, EROUNDS) as i:
                sort_round(i)
            dve.wait_ge(S["weights_in"], 16 * WEIGHT_LOADS)
            wh = wproj[:, 0:HE].unsqueeze(1).broadcast_to([CH, 2, HE])
            v.tensor_tensor(wtmp[:, :, :], wh, att_bc[:, :, :], ALU.mult)
            v.drain()
            v.tensor_reduce(wproj[:, HE:TW], wtmp[:, :, :].rearrange("p a (h e) -> p (a h) e", e=EXPERTS),
                            AX.X, ALU.add)
            v.tensor_scalar(c_sb[CH:P, :], c_sb[CH:P, :], -1.0, None, ALU.mult)
            v.tensor_copy(hT[0][:, 0:IMAGES], cls_c[:, 0:1].broadcast_to([CH, IMAGES]))
            v.drain()
            v.nop().then_inc(S["wp1"], 1)

            def p_(n):
                return par[:, n:n + 1]

            def seq(*ops):
                for op in ops:
                    op()
                    v.drain()

            dve.wait_ge(S["par_act"], 1)
            seq(lambda: v.tensor_scalar(p_(1), adiag[:, :], 0.0, None, ALU.max),
                lambda: v.tensor_tensor(p_(7), p_(0), p_(0), ALU.mult),
                lambda: v.tensor_tensor(p_(7), p_(7), p_(1), ALU.mult),
                lambda: v.tensor_scalar(p_(7), p_(7), 1.0, None, ALU.add),
                lambda: v.reciprocal(p_(2), p_(7)))
            v.nop().then_inc(S["par_dve"], 1)
            dve.wait_ge(S["par_act"], 2)
            seq(lambda: v.reciprocal(p_(7), p_(3)),
                lambda: v.tensor_tensor(p_(7), p_(7), p_(2), ALU.mult),
                lambda: v.tensor_tensor(p_(7), p_(7), p_(3), ALU.add),
                lambda: v.tensor_scalar(p_(3), p_(7), 0.5, None, ALU.mult),
                lambda: v.reciprocal(p_(7), p_(3)),
                lambda: v.tensor_tensor(p_(4), p_(7), p_(2), ALU.mult),
                lambda: v.tensor_tensor(p_(5), p_(4), p_(0), ALU.mult))
            v.memset(tab_c[:, 0:1], 1.0)
            v.memset(tab_k[:, 0:1], 0.0)
            v.drain()
            n = 1
            while n < STEPS:
                m = min(2 * n, STEPS) - n
                seq(lambda: v.tensor_tensor(p_(6), p_(1), p_(5), ALU.mult),
                    lambda: v.tensor_scalar(p_(6), p_(6), -1.0, None, ALU.mult))
                v.tensor_scalar(tab_a[:, 0:m], tab_k[:, 0:m], p_(6), None, ALU.mult)
                v.tensor_scalar(tab_b[:, 0:m], tab_k[:, 0:m], p_(4), None, ALU.mult)
                v.drain()
                v.scalar_tensor_tensor(out=tab_c[:, n:n + m], in0=tab_c[:, 0:m], scalar=p_(4), in1=tab_a[:, 0:m],
                                       op0=ALU.mult, op1=ALU.add)
                v.scalar_tensor_tensor(out=tab_k[:, n:n + m], in0=tab_c[:, 0:m], scalar=p_(5), in1=tab_b[:, 0:m],
                                       op0=ALU.mult, op1=ALU.add)
                v.drain()
                seq(lambda: v.tensor_tensor(p_(6), p_(6), p_(5), ALU.mult),
                    lambda: v.tensor_tensor(p_(5), p_(5), p_(4), ALU.mult),
                    lambda: v.tensor_scalar(p_(5), p_(5), 2.0, None, ALU.mult),
                    lambda: v.tensor_tensor(p_(4), p_(4), p_(4), ALU.mult),
                    lambda: v.tensor_tensor(p_(4), p_(4), p_(6), ALU.add))
                n *= 2
            seq(lambda: v.tensor_tensor(p_(8), p_(1), tab_k[:, CHUNK:STEPS], ALU.mult),
                lambda: v.tensor_scalar(p_(8), p_(8), -1.0, None, ALU.mult))
            seq(lambda: v.tensor_tensor(p_(6), p_(1), p_(0), ALU.mult),
                lambda: v.tensor_tensor(p_(7), p_(2), p_(0), ALU.mult),
                lambda: v.scalar_tensor_tensor(out=tab_a, in0=tab_k, scalar=p_(6), in1=tab_c, op0=ALU.mult, op1=ALU.add),
                lambda: v.tensor_scalar(tab_a, tab_a, p_(7), None, ALU.mult),
                lambda: v.scalar_tensor_tensor(out=tab_b, in0=tab_c, scalar=p_(0), in1=tab_k, op0=ALU.mult, op1=ALU.subtract),
                lambda: v.tensor_scalar(tab_b, tab_b, p_(7), None, ALU.mult))
            v.nop().then_inc(S["tabs_ready"], 1)

            N = IMAGES
            dve.wait_ge(S["cls_in"], 1)
            seq(lambda: v.reciprocal(std[0][:, 0:N], std[0][:, 0:N]))
            v.tensor_tensor(u[0][:, 0:N], bank[4][0:CH, 0:N], std[0][:, 0:N], ALU.mult).then_inc(S["cls_sb"], 1)
            dve.wait_ge(S["cls_ps"], 3)
            v.tensor_tensor(start[:, 0:1], bank[6][:, 0:1], tab_a[:, 0:1], ALU.mult)
            v.tensor_tensor(start[:, 1:2], bank[6][:, 0:1], tab_b[:, 0:1], ALU.mult)
            v.tensor_scalar(y[:, 0:N], bank[6][:, 0:N], tab_b[:, 0:1], None, ALU.mult).then_inc(S["cls_sb"], 1)
            dve.wait_ge(S["cls_ps"], 4)
            v.scalar_tensor_tensor(out=h2[0][:, 0:N], in0=u[0][:, 0:N], scalar=d_sb[:, :],
                                   in1=bank[7][0:CH, 0:N], op0=ALU.mult, op1=ALU.add)
            v.drain()
            v.tensor_tensor(h2[0][:, 0:N], h2[0][:, 0:N], hT[0][:, 0:N], ALU.add).then_inc(S["cls_sb"], 1)
            dve.wait_ge(S["cls_in"], 2)
            seq(lambda: v.reciprocal(std[1][:, 0:N], std[1][:, 0:N]))
            v.tensor_tensor(xn[0][:, 0:N], bank[4][0:CH, 0:N], std[1][:, 0:N], ALU.mult).then_inc(S["cls_sb"], 1)
            dve.wait_ge(S["cls_st"], 48)

            def step(bt, tp, ba, ap):
                nt = bt * CHUNKS if bt is not None else None
                na = ba * CHUNKS if ba is not None else None
                tok = bt is not None
                att = ba is not None
                zero = isinstance(bt, int) and bt == 0
                zero_a = isinstance(ba, int) and ba == 0
                for c in slots(ba):
                    tc, a0, a1, _ = active(bt, ba, c)
                    q = (ap * CHUNKS + c) % 2 if att else 0

                    def gated(*tiles):
                        for t in tiles:
                            k = 5 * (nt + c) + t
                            o = (5 * (tp * CHUNKS + c) + t) % 2
                            n = tile_rows(t)
                            dve.wait_ge(S["gate_done"], k + 1)
                            v.tensor_tensor(r3(prod[0:n, t, :]), taps_view(tp, c, t), r3(gate[o][0:n, :]),
                                            ALU.mult).then_inc(S["prod_done"], 1)

                    if tc:
                        if not (zero and c == 0):
                            dve.wait_ge(S["tok_done"], nt + c)
                        gated(0, 1)
                    if a1:
                        dve.wait_ge(S["co_done"], na + c)
                        wait(dve, S["tm_done"], na + c - 2)
                        v.scalar_tensor_tensor(out=h2[1 - q][:, :], in0=u[1 - q][:, :], scalar=d_sb[:, :],
                                               in1=bank[7][0:CH, 0:CHUNK], op0=ALU.mult, op1=ALU.add)
                        v.drain()
                        before_c = (hT[ap][:, (c - 1) * CHUNK:c * CHUNK] if c else
                                    hT[1 - ap][:, (CHUNKS - 1) * CHUNK:CHUNKS * CHUNK])
                        v.tensor_tensor(h2[1 - q][:, :], h2[1 - q][:, :], before_c, ALU.add)\
                            .then_inc(S["h2_done"], 1)
                    if tc:
                        gated(2, 3, 4)
                    if a0:
                        dve.wait_ge(S["std_done"], na + c + 1)
                        v.tensor_tensor(u[q][:, :], bank[4][0:CH, 0:CHUNK], std[0][:, :], ALU.mult)\
                            .then_inc(S["u_done"], 1)
                    if a1:
                        dve.wait_ge(S["std2_done"], na + c)
                        if not (zero_a and c - 1 < 2):
                            dve.wait_ge(tm_st[1 - q], 24 * (na + c - 1 - (1 - q)))
                        v.tensor_tensor(xn[1 - q][:, :], bank[7][0:CH, 0:CHUNK], std[1][:, :], ALU.mult)\
                            .then_inc(S["xn_done"], 1)
                    if a0:
                        dve.wait_ge(S["bu_done"], na + c + 1)
                        tt = slice(1, STEPS)
                        v.tensor_tensor(fin[0][:, :], bank[6][:, 0:CHUNK], tab_a[:, tt], ALU.mult)
                        v.tensor_tensor(fin[1][:, :], bank[6][:, 0:CHUNK], tab_b[:, tt], ALU.mult)
                        v.drain()
                        v.nop().then_inc(S["fin_read"], 1)
                        init = carry if c else start
                        for n in range(2):
                            v.tensor_tensor_scan(wst[n][:, :], p_(3).broadcast_to([P, CHUNK]), fin[n][:, :],
                                                 init[:, n:n + 1], ALU.mult, ALU.add)
                        v.drain()
                        v.tensor_tensor(fin[0][:, :], wst[0][:, :], tab_k[:, tt], ALU.mult)
                        v.tensor_tensor(fin[1][:, :], wst[1][:, :], tab_c[:, tt], ALU.mult)
                        v.drain()
                        if not (zero_a and c == 0):
                            dve.wait_ge(S["co_done"], na + c)
                        v.tensor_tensor(y[:, :], fin[0][:, :], fin[1][:, :], ALU.add).then_inc(S["y_done"], 1)
                        last = slice(CHUNK - 1, CHUNK)
                        v.tensor_scalar(carry[:, 1:2], wst[0][:, last], tab_c[:, CHUNK:STEPS], None, ALU.mult)
                        v.drain()
                        v.scalar_tensor_tensor(out=carry[:, 0:1], in0=wst[1][:, last], scalar=p_(8),
                                               in1=carry[:, 1:2], op0=ALU.mult, op1=ALU.add)
                        v.drain()
                        v.tensor_copy(carry[:, 1:2], y[:, last])

            steps(dve, step)


SC = 136
SCHUNKS = SCOLS // SC
RW = 2 * HEADS + HE
VW = HEADS + HE
GK = 89
GATE_BATCHES = [GRAPH_NODES, GRAPH_NODES + P * GK, NODES - P * GK]
FF = NT // P


def back(nc, table, gathered, sorted_rec, seg_scratch, h_tok, xnT, b_gat, ln_gamma, ln_beta,
         W1, b1, W2, b2, out):
    partial = nc.dram_tensor("partial", [SORTED + P, RW], f32, kind="Internal").ap()
    gates = nc.dram_tensor("gates", [NODES, EXPERTS], f32, kind="Internal").ap()
    ctx = ExitStack()
    with ctx:
        def sb(name, shape, dt=f32):
            return ctx.enter_context(nc.sbuf_tensor(name, shape, dt))

        def pb(name, shape, dt=f32):
            return ctx.enter_context(nc.psum_tensor(name, shape, dt))

        def sem(name):
            return ctx.enter_context(nc.semaphore(name))

        ident = sb("ident2", [P, P])
        big = sb("big", [P, 2 * SCOLS])
        recs = big[:, :].bitcast(i32).rearrange("p (c w) -> p c w", w=2)
        st = sb("st", [P, SCOLS])
        ns = sb("ns", [P, SCOLS])
        nb = sb("nb", [P, SCOLS])
        rows = [sb(f"rows{n}", [P, SC, TW]) for n in range(2)]
        res = [sb(f"res{n}", [P, SC, RW]) for n in range(2)]
        sd = sb("sd", [P, HEADS, SC])
        ad = sb("ad", [P, HEADS, SC])
        e = sb("e", [P, HEADS, SC])
        mx = sb("mx", [P, HEADS, SC + 1])
        ex = sb("ex", [P, 2, HEADS, SC])
        msg = sb("msg", [P, HE, SC])
        cad = sb("cad", [P, HEADS])
        car = sb("car", [P, RW])
        key = sb("key", [P, SCOLS])
        cols = msg[:, :, :].rearrange("p a c -> p (a c)").bitcast(i32)
        fs = sb("fs", [P, 1])
        hs = sb("hs", [P, 1])
        partf = sb("partf", [P, 1])
        part = sb("part", [P, 1], i32)
        idx = sb("idx", [P, 4], i32)
        idxf = sb("idxf", [P, 4])
        arow = sb("arow", [P, TW])
        ends = sb("ends", [P, 3, VW])
        endsT = sb("endsT", [VW, 3, P])
        nbT = sb("nbT", [VW, P])
        mcT = sb("mcT", [VW, P + 1])
        vcT = sb("vcT", [VW, P + 1])
        exT = sb("exT", [VW, 2, P])
        cin = sb("cin", [P, 2, VW])
        fix = sb("fix", [P, RW])
        fm = sb("fm", [P, 3, VW])
        fixed = sb("fixed", [P, RW])
        seg = sb("seg", [P, P], i32)
        nidx = [sb(f"nidx{n}", [P, HALF], i32) for n in range(2)]
        nrow = [sb(f"nrow{n}", [P, HALF, RW]) for n in range(2)]
        node = sb("node", [P, P, RW])
        th = sb("th", [P, P, HE])
        gt = sb("gt", [P, P, HE])
        g1 = sb("g1", [P, P, HEADS])
        g2 = sb("g2", [P, P, HEADS])
        g3 = sb("g3", [P, P, HEADS])
        r1 = sb("r1", [P, P])
        r2 = sb("r2", [P, P])
        bgat = sb("bgat", [P, HE])
        gam = sb("gam", [P, HE])
        bet = sb("bet", [P, HE])
        eps2 = sb("eps2", [P, 1])
        w1 = sb("fw1", [CH, EXPERTS, HIDDEN])
        w2 = sb("fw2", [HIDDEN, EXPERTS, CH])
        fb1 = sb("fb1", [HIDDEN, EXPERTS])
        fb2 = sb("fb2", [P, EXPERTS * CH])
        xf = [sb(f"xf{n}", [CH, NT]) for n in range(2)]
        hr = [sb(f"hr{n}", [P, FF, CH]) for n in range(2)]
        gf = [sb(f"gf{n}", [P, FF, EXPERTS]) for n in range(2)]
        hh = [big[:, n * EXPERTS * NT:(n + 1) * EXPERTS * NT].rearrange("p (e n) -> p e n", n=NT)
              for n in range(2)]
        yb = sb("yb", [P, FF, EXPERTS, CH])
        yc = sb("yc", [P, FF, 2, CH])
        yo = [sb(f"yo{n}", [P, FF, CH]) for n in range(2)]

        hid = [pb(f"hid{n}", [P, 512]) for n in range(2)]
        ybank = [pb(f"ybank{n}", [P, 1024]) for n in range(2)]
        tp = pb("tp", [P, 512])

        names = """consts in0 wts idx_ready arow_in rows0 rows1 res0 res1 ex_in ex_done ends_ready endsT_done
            cin_ready exT_in exT_done cin_done fix_idx fix_in fix_ex fix_exd fixed_ready fixed_st nstage
            ngath0 ngath1 ybank_free node_ready th_in g_sq g_std g_e g_ex gt_ready gt_st ff0 ff1 hid_done hh_done y_done
            yo_done out0 out1 scan_used waited""".split()
        S = {n: sem("b_" + n) for n in names}
        block = ctx.enter_context(nc.Block())
        sorted_v = sorted_rec.rearrange("(p c) w -> p c w", c=SCOLS)
        partial_v = partial[0:SORTED, :].rearrange("(p c) w -> p (c w)", c=SCOLS)
        rows_s = [S["rows0"], S["rows1"]]
        res_s = [S["res0"], S["res1"]]
        ff = [S["ff0"], S["ff1"]]
        ost = [S["out0"], S["out1"]]
        WTS = 9

        def chunks(eng, step):
            outside = (NODES - GRAPH_NODES) // NT
            lo = GRAPH_NODES
            with eng.Fori(0, outside // 2) as i:
                for q in range(2):
                    step(2 * i + q, lo + (2 * i + q) * NT, q)
            k = outside
            step(k, NODES - NT, 0)
            step(k + 1, 0, 1)
            k += 2
            inside = GRAPH_NODES // NT - 1
            with eng.Fori(0, inside // 2) as i:
                for q in range(2):
                    step(k + 2 * i + q, (1 + 2 * i + q) * NT, q)
            step(k + inside - 1, inside * NT, 0)

        assert (NODES - GRAPH_NODES) // NT % 2 == 0 and (GRAPH_NODES // NT - 1) % 2 == 1
        TOTAL = (NODES - GRAPH_NODES) // NT + 1 + GRAPH_NODES // NT
        OUTSIDE = (NODES - GRAPH_NODES) // NT + 1

        @block.sync
        def _(sp):
            sp.dma_start(recs, sorted_v).then_inc(S["in0"], 16)
            sp.dma_start(seg[:, :], seg_scratch[1, :, :]).then_inc(S["in0"], 16)
            for dst, src in ((bgat[:, :], b_gat.partition_broadcast(P)), (gam[:, :], ln_gamma.partition_broadcast(P)),
                             (bet[:, :], ln_beta.partition_broadcast(P)), (fb2[:, :], b2.partition_broadcast(P)),
                             (w1[:, :, :], W1.rearrange("e c h -> c e h")), (w2[:, :, :], W2.rearrange("e h c -> h e c")),
                             (fb1[:, :], b1)):
                sp.dma_start(dst, src).then_inc(S["wts"], 16)

            def load_rows(k, q):
                sp.dma_start(rows[q][:, :, :].rearrange("p c w -> p (c w)"),
                             gathered[:, bass.ds(k * SC * TW, SC * TW)]).then_inc(rows_s[q], 16)

            load_rows(0, 0)
            load_rows(1, 1)

            def store_res(k, q):
                sp.wait_ge(S["scan_used"], k + 1)
                sp.sem_inc(S["waited"], 1)
                sp.dma_start(partial_v[:, bass.ds(k * SC * RW, SC * RW)],
                             res[q][:, :, :].rearrange("p c w -> p (c w)")).then_inc(res_s[q], 16)

            with sp.Fori(0, SCHUNKS // 2 - 1) as i:
                for q in range(2):
                    store_res(2 * i + q, q)
                    load_rows(2 * i + q + 2, q)
            for q in range(2):
                store_res(SCHUNKS - 2 + q, q)

            for n, g0 in enumerate(GATE_BATCHES):
                if n:
                    sp.wait_ge(S["gt_st"], 16 * n)
                sp.dma_start(th[:, 0:GK, :], table[g0:g0 + P * GK, 0:HE].rearrange("(p k) w -> p k w", k=GK))\
                    .then_inc(S["th_in"], 16)
                sp.wait_ge(S["gt_ready"], n + 1)
                sp.dma_start(gates[g0:g0 + P * GK, :].rearrange("(p k) w -> p k w", k=GK), g1[:, 0:GK, :])\
                    .then_inc(S["gt_st"], 16)
            sp.wait_ge(S["gt_st"], 16 * len(GATE_BATCHES))

            def load_ff(k, n0, q):
                sp.dma_start(xf[q][:, :], xnT[:, bass.ds(n0, NT)]).then_inc(ff[q], 16)
                sp.dma_start(hr[q][:, :, :], h_tok[bass.ds(n0, NT), :].rearrange("(p j) c -> p j c", j=FF))\
                    .then_inc(ff[q], 16)
                sp.dma_start(gf[q][:, :, :], gates[bass.ds(n0, NT), :].rearrange("(p j) c -> p j c", j=FF))\
                    .then_inc(ff[q], 16)

            def store_ff(k, n0, q):
                sp.wait_ge(S["yo_done"], k + 1)
                sp.sem_inc(S["waited"], 1)
                sp.dma_start(out[bass.ds(n0, NT), :].rearrange("(p j) c -> p j c", j=FF), yo[q][:, :, :])\
                    .then_inc(ost[q], 16)

            def node0(k):
                return (GRAPH_NODES + k * NT if k < OUTSIDE - 1 else
                        NODES - NT if k == OUTSIDE - 1 else (k - OUTSIDE) * NT)

            load_ff(0, node0(0), 0)
            load_ff(1, node0(1), 1)
            with sp.Fori(0, (OUTSIDE - 3) // 2) as i:
                for q in range(2):
                    store_ff(2 * i + q, GRAPH_NODES + (2 * i + q) * NT, q)
                    load_ff(2 * i + q + 2, GRAPH_NODES + (2 * i + q + 2) * NT, q)
            for k in range(OUTSIDE - 3, OUTSIDE + 1):
                if k == OUTSIDE - 1:
                    for z in range(2):
                        sp.wait_ge(ost[z], 16 * (OUTSIDE // 2))
                store_ff(k, node0(k), k % 2)
                if k == OUTSIDE - 2:
                    sp.wait_ge(S["gt_ready"], len(GATE_BATCHES) + 1)
                    sp.dma_start(gates[0:GRAPH_NODES, :].rearrange("(p k) w -> p k w", k=P), g1[:, :, :])\
                        .then_inc(S["gt_st"], 16)
                    sp.wait_ge(S["gt_st"], 16 * (len(GATE_BATCHES) + 1))
                load_ff(k + 2, node0(k + 2), k % 2)
            with sp.Fori(0, (TOTAL - OUTSIDE - 4) // 2) as i:
                for z in range(2):
                    m = 2 * i + z + 1
                    store_ff(OUTSIDE + m, m * NT, z)
                    load_ff(OUTSIDE + m + 2, (m + 2) * NT, z)
            for k in range(TOTAL - 3, TOTAL):
                store_ff(k, node0(k), k % 2)
                if k + 2 < TOTAL:
                    load_ff(k + 2, node0(k + 2), k % 2)
            sp.wait_ge(ost[0], 16 * ((TOTAL + 1) // 2))
            sp.wait_ge(ost[1], 16 * (TOTAL // 2))

        @block.gpsimd
        def _(pool):
            g = nc.gpsimd
            g.memset(ident[:, :], 0.0)
            g.memset(eps2[:, :], EPS)
            g.iota(cols, pattern=[[1, SCOLS]], base=0, channel_multiplier=0)
            g.iota(part[:, :], pattern=[[1, 1]], base=0, channel_multiplier=1)
            g.drain()
            g.affine_select(out=ident[:, :], in_=ident[:, :], compare_op=ALU.not_equal, fill=1.0, base=0,
                            pattern=[[-1, P]], channel_multiplier=1)
            g.drain()
            g.nop().then_inc(S["consts"], 1)
            off = bass.IndirectOffsetOnAxis
            pool.wait_ge(S["idx_ready"], 1)
            g.indirect_dma_start(out=arow[:, :], out_offset=None, in_=table[0:GRAPH_NODES, :],
                                 in_offset=off(ap=idx[:, 0:1], axis=0)).then_inc(S["arow_in"], 16)
            for q in range(2):
                pool.wait_ge(res_s[q], 16 * SCHUNKS // 2)
            g.indirect_dma_start(out=fix[:, :], out_offset=None, in_=partial[0:SORTED, :],
                                 in_offset=off(ap=idx[:, 1:2], axis=0)).then_inc(S["fix_in"], 16)
            pool.wait_ge(S["fixed_ready"], 1)
            g.indirect_dma_start(out=partial, out_offset=off(ap=idx[:, 2:3], axis=0), in_=fixed[:, :],
                                 in_offset=None).then_inc(S["fixed_st"], 16)
            pool.wait_ge(S["fixed_st"], 16)
            with pool.Fori(0, SROUNDS) as i:
                for h in range(2):
                    g.tensor_copy(nidx[h][:, :], seg[:, bass.ds((2 * i + h) * HALF, HALF)])
                g.drain()
                for h in range(2):
                    for j in range(HALF):
                        g.indirect_dma_start(out=nrow[h][:, j, :], out_offset=None, in_=partial[0:SORTED, :],
                                             in_offset=off(ap=nidx[h][:, j:j + 1], axis=0))\
                            .then_inc([S["ngath0"], S["ngath1"]][h], 16)
                for h in range(2):
                    pool.wait_ge([S["ngath0"], S["ngath1"]][h], 16 * HALF * (i + 1))
                    g.tensor_copy(node[:, bass.ds((2 * i + h) * HALF, HALF), :], nrow[h][:, :, :])
                g.drain()
            g.nop().then_inc(S["node_ready"], 1)

        @block.tensor
        def _(pe):
            mm = nc.tensor.matmul
            pe.wait_ge(S["ends_ready"], 1)
            for n in range(3):
                m = mm(tp[0:VW, n * P:(n + 1) * P], ends[:, n, :], ident[:, :], start=True, stop=True)
            m.then_inc(S["endsT_done"], 1)
            pe.wait_ge(S["cin_ready"], 1)
            mm(tp[:, 0:VW], mcT[:, 0:P], ident[0:VW, 0:VW], start=True, stop=True)
            mm(tp[:, VW:2 * VW], vcT[:, 0:P], ident[0:VW, 0:VW], start=True, stop=True).then_inc(S["cin_done"], 1)
            pe.wait_ge(S["wts"], 16 * 7)

            def step(k, n0, q):
                pe.wait_ge(ff[q], 24 * (k - q) + 48)
                for ee in range(EXPERTS):
                    if ee >= 2:
                        pe.wait_ge(S["hh_done"], EXPERTS * k + ee - 1)
                    mm(hid[ee % 2][:, :], w1[:, ee, :], xf[q][:, :], start=True, stop=True).then_inc(S["hid_done"], 1)
                pe.wait_ge(S["hh_done"], EXPERTS * k + EXPERTS)
                pe.wait_ge(S["ybank_free"], k + 1)
                for j in range(FF):
                    for ee in range(EXPERTS):
                        o = (j * EXPERTS + ee) * CH
                        m = mm(ybank[q][:, o:o + CH], hh[q][:, ee, j:NT:FF], w2[:, ee, :], start=True, stop=True)
                m.then_inc(S["y_done"], 1)

            chunks(pe, step)

        @block.scalar
        def _(act):
            a = nc.scalar.activation
            with act.Fori(0, SCHUNKS) as k:
                act.wait_ge(S["ex_in"], k + 1)
                a(ex[:, :, :, :], ex[:, :, :, :], ACT.Exp).then_inc(S["ex_done"], 1)
            act.wait_ge(S["exT_in"], 1)
            a(exT[:, :, :], exT[:, :, :], ACT.Exp).then_inc(S["exT_done"], 1)
            act.wait_ge(S["fix_ex"], 1)
            a(fm[:, 0:2, :], fm[:, 0:2, :], ACT.Exp).then_inc(S["fix_exd"], 1)

            def gate_fn(n, K):
                act.wait_ge(S["g_sq"], n + 1)
                a(r1[:, 0:K], r1[:, 0:K], ACT.Sqrt, scale=1.0 / HE, bias=eps2[:, :]).then_inc(S["g_std"], 1)
                act.wait_ge(S["g_e"], n + 1)
                a(g1[:, 0:K, :], g1[:, 0:K, :], ACT.Exp).then_inc(S["g_ex"], 1)

            for n in range(len(GATE_BATCHES)):
                gate_fn(n, GK)

            act.wait_ge(S["wts"], 16 * 7)

            def step(k, n0, q):
                if isinstance(k, int) and k == OUTSIDE:
                    gate_fn(len(GATE_BATCHES), P)
                for ee in range(EXPERTS):
                    act.wait_ge(S["hid_done"], EXPERTS * k + ee + 1)
                    a(hh[q][:, ee, :], hid[ee % 2][:, :], ACT.Gelu, bias=fb1[:, ee:ee + 1]).then_inc(S["hh_done"], 1)

            chunks(act, step)

        @block.vector
        def _(dve):
            v = nc.vector

            def seq(*ops):
                for op in ops:
                    op()
                    v.drain()

            dve.wait_ge(S["consts"], 1)
            v.nop().then_inc(S["ybank_free"], 2)
            dve.wait_ge(S["in0"], 32)
            seq(lambda: v.tensor_copy(key[:, :], recs[:, :, 1]),
                lambda: v.tensor_scalar(st[:, :], key[:, :], float(FLAG), None, ALU.is_ge))
            v.tensor_scalar(ns[:, :], st[:, :], -1.0, 1.0, ALU.mult, ALU.add)
            v.tensor_scalar(nb[:, :], st[:, :], -BIG, None, ALU.mult)
            v.scalar_tensor_tensor(out=idx[:, 0:1], in0=st[:, 0:1], scalar=-float(FLAG), in1=key[:, 0:1],
                                   op0=ALU.mult, op1=ALU.add)
            v.tensor_copy(partf[:, :], part[:, :])
            v.tensor_reduce(hs[:, :], st[:, :], AX.X, ALU.max)
            v.drain()
            v.nop().then_inc(S["idx_ready"], 1)
            seq(lambda: v.tensor_copy(key[:, :], cols),
                lambda: v.scalar_tensor_tensor(out=key[:, :], in0=ns[:, :], scalar=float(SCOLS), in1=key[:, :],
                                               op0=ALU.mult, op1=ALU.add),
                lambda: v.tensor_reduce(fs[:, :], key[:, :], AX.X, ALU.min),
                lambda: v.tensor_scalar(idxf[:, 3:4], fs[:, :], 0.0, None, ALU.is_equal),
                lambda: v.scalar_tensor_tensor(out=idxf[:, 0:1], in0=partf[:, :], scalar=float(SCOLS), in1=fs[:, :],
                                               op0=ALU.mult, op1=ALU.add),
                lambda: v.tensor_tensor(idxf[:, 1:2], idxf[:, 0:1], idxf[:, 3:4], ALU.add),
                lambda: v.tensor_scalar(idxf[:, 1:2], idxf[:, 1:2], -1.0, None, ALU.add),
                lambda: v.tensor_scalar(idxf[:, 2:3], partf[:, :], float(SORTED), None, ALU.add),
                lambda: v.tensor_tensor(idxf[:, 2:3], idxf[:, 2:3], idxf[:, 1:2], ALU.subtract),
                lambda: v.scalar_tensor_tensor(out=idxf[:, 2:3], in0=idxf[:, 2:3], scalar=idxf[:, 3:4],
                                               in1=idxf[:, 1:2], op0=ALU.mult, op1=ALU.add),
                lambda: v.tensor_copy(idx[:, 1:3], idxf[:, 1:3]),
                lambda: v.memset(car[:, :], 0.0),
                lambda: v.memset(car[:, 0:HEADS], -BIG))
            dve.wait_ge(S["arow_in"], 16)
            seq(lambda: v.tensor_copy(cad[:, :], arow[:, HE + HEADS:TW]))

            with dve.Fori(0, SCHUNKS // 2) as i:
                for q in range(2):
                    k = 2 * i + q
                    dve.wait_ge(rows_s[q], 16 * (i + 1))
                    rv = rows[q][:, :, :].rearrange("p c w -> p w c")
                    ov = res[q][:, :, :].rearrange("p c w -> p w c")
                    cs = bass.ds(k * SC, SC)

                    def flag(t, n=HEADS):
                        return t[:, cs].unsqueeze(1).broadcast_to([P, n, SC])

                    seq(lambda: v.tensor_tensor(sd[:, :, :], rv[:, HE + HEADS:TW, :], flag(st), ALU.mult))
                    for h in range(HEADS):
                        v.tensor_tensor_scan(ad[:, h, :], ns[:, cs], sd[:, h, :], cad[:, h:h + 1], ALU.mult, ALU.add)
                    v.tensor_copy(mx[:, :, 0], car[:, 0:HEADS])
                    v.drain()
                    v.tensor_copy(cad[:, :], ad[:, :, SC - 1])
                    seq(lambda: v.tensor_tensor(e[:, :, :], rv[:, HE:HE + HEADS, :], ad[:, :, :], ALU.add),
                        lambda: v.scalar_tensor_tensor(out=e[:, :, :], in0=e[:, :, :], scalar=0.2, in1=e[:, :, :],
                                                       op0=ALU.mult, op1=ALU.max))
                    for h in range(HEADS):
                        v.tensor_tensor_scan(mx[:, h, 1:SC + 1], nb[:, cs], e[:, h, :], car[:, h:h + 1],
                                             ALU.add, ALU.max)
                    v.drain()
                    v.tensor_tensor(ex[:, 0, :, :], mx[:, :, 0:SC], mx[:, :, 1:SC + 1], ALU.subtract)
                    v.tensor_tensor(ex[:, 1, :, :], e[:, :, :], mx[:, :, 1:SC + 1], ALU.subtract)
                    v.drain()
                    v.tensor_scalar(ex[:, 0, :, :], ex[:, 0, :, :], 0.0, None, ALU.min).then_inc(S["ex_in"], 1)
                    dve.wait_ge(S["ex_done"], k + 1)
                    v.tensor_tensor(ex[:, 0, :, :], ex[:, 0, :, :], flag(ns), ALU.mult)
                    for h in range(HEADS):
                        v.tensor_tensor(msg[:, h * EXPERTS:(h + 1) * EXPERTS, :],
                                        rv[:, h * EXPERTS:(h + 1) * EXPERTS, :],
                                        ex[:, 1, h, :].unsqueeze(1).broadcast_to([P, EXPERTS, SC]), ALU.mult)
                    v.drain()
                    dve.wait_ge(res_s[q], 16 * i)
                    v.tensor_copy(ov[:, 0:HEADS, :], mx[:, :, 1:SC + 1])
                    for h in range(HEADS):
                        v.tensor_tensor_scan(ov[:, HEADS + h, :], ex[:, 0, h, :], ex[:, 1, h, :],
                                             car[:, HEADS + h:HEADS + h + 1], ALU.mult, ALU.add)
                        for x_ in range(EXPERTS):
                            w = h * EXPERTS + x_
                            v.tensor_tensor_scan(ov[:, 2 * HEADS + w, :], ex[:, 0, h, :], msg[:, w, :],
                                                 car[:, 2 * HEADS + w:2 * HEADS + w + 1], ALU.mult, ALU.add)
                    v.drain()
                    v.tensor_copy(car[:, :], res[q][:, SC - 1, :])
                    v.drain()
                    v.nop().then_inc(S["scan_used"], 1)

            v.tensor_copy(ends[:, 0, 0:HEADS], car[:, 0:HEADS])
            v.tensor_copy(ends[:, 0, HEADS:VW].rearrange("p (h x) -> p h x", x=EXPERTS),
                          car[:, 0:HEADS].unsqueeze(2).broadcast_to([P, HEADS, EXPERTS]))
            v.tensor_copy(ends[:, 1, :], car[:, HEADS:RW])
            v.tensor_scalar(ends[:, 2, :], hs[:, 0:1].broadcast_to([P, VW]), -1.0, 1.0, ALU.mult, ALU.add)
            v.drain()
            v.nop().then_inc(S["ends_ready"], 1)
            dve.wait_ge(S["endsT_done"], 1)
            v.tensor_copy(endsT[:, :, :].rearrange("p a b -> p (a b)"), tp[0:VW, 0:3 * P])
            v.memset(mcT[:, 0:1], -BIG)
            v.memset(vcT[:, 0:1], 0.0)
            v.drain()
            seq(lambda: v.tensor_scalar(nbT[:, :], endsT[:, 2, :], 1.0, BIG, ALU.subtract, ALU.mult),
                lambda: v.tensor_tensor_scan(mcT[:, 1:P + 1], nbT[:, :], endsT[:, 0, :], -BIG, ALU.add, ALU.max),
                lambda: v.tensor_tensor(exT[:, 0, :], mcT[:, 0:P], mcT[:, 1:P + 1], ALU.subtract),
                lambda: v.tensor_scalar(exT[:, 0, :], exT[:, 0, :], 0.0, None, ALU.min),
                lambda: v.tensor_tensor(exT[:, 1, :], endsT[:, 0, :], mcT[:, 1:P + 1], ALU.subtract))
            v.nop().then_inc(S["exT_in"], 1)
            dve.wait_ge(S["exT_done"], 1)
            seq(lambda: v.tensor_tensor(exT[:, 0, :], exT[:, 0, :], endsT[:, 2, :], ALU.mult),
                lambda: v.tensor_tensor(endsT[:, 1, :], exT[:, 1, :], endsT[:, 1, :], ALU.mult),
                lambda: v.tensor_tensor_scan(vcT[:, 1:P + 1], exT[:, 0, :], endsT[:, 1, :], 0.0, ALU.mult, ALU.add))
            v.nop().then_inc(S["cin_ready"], 1)
            dve.wait_ge(S["cin_done"], 1)
            seq(lambda: v.tensor_copy(cin[:, :, :].rearrange("p a b -> p (a b)"), tp[:, 0:2 * VW]))
            dve.wait_ge(S["fix_in"], 16)
            v.tensor_copy(fm[:, 0, 0:HEADS], fix[:, 0:HEADS])
            v.tensor_copy(fm[:, 0, HEADS:VW].rearrange("p (h x) -> p h x", x=EXPERTS),
                          fix[:, 0:HEADS].unsqueeze(2).broadcast_to([P, HEADS, EXPERTS]))
            v.drain()
            seq(lambda: v.tensor_tensor(fm[:, 2, :], fm[:, 0, :], cin[:, 0, :], ALU.max),
                lambda: v.tensor_copy(fixed[:, 0:HEADS], fm[:, 2, 0:HEADS]),
                lambda: v.tensor_tensor(fm[:, 0, :], fm[:, 0, :], fm[:, 2, :], ALU.subtract),
                lambda: v.tensor_tensor(fm[:, 1, :], cin[:, 0, :], fm[:, 2, :], ALU.subtract))
            v.nop().then_inc(S["fix_ex"], 1)
            dve.wait_ge(S["fix_exd"], 1)
            seq(lambda: v.tensor_tensor(fm[:, 0, :], fm[:, 0, :], fix[:, HEADS:RW], ALU.mult),
                lambda: v.tensor_tensor(fm[:, 1, :], fm[:, 1, :], cin[:, 1, :], ALU.mult),
                lambda: v.tensor_tensor(fixed[:, HEADS:RW], fm[:, 0, :], fm[:, 1, :], ALU.add))
            v.nop().then_inc(S["fixed_ready"], 1)

            def bc(t, K):
                return t[:, :].unsqueeze(1).broadcast_to([P, K, HE])

            def gate_fn(n, K):
                T = th[:, 0:K, :]
                G = gt[:, 0:K, :]
                R = r1[:, 0:K]
                W = r2[:, 0:K]
                A1, A2, A3 = g1[:, 0:K, :], g2[:, 0:K, :], g3[:, 0:K, :]
                seq(lambda: v.tensor_tensor(T, T, bc(bgat, K), ALU.add),
                    lambda: v.tensor_reduce(R, T, AX.X, ALU.add),
                    lambda: v.tensor_scalar(R, R, 1.0 / HE, None, ALU.mult),
                    lambda: v.tensor_tensor(T, T, R.unsqueeze(2).broadcast_to([P, K, HE]), ALU.subtract),
                    lambda: v.tensor_tensor(G, T, T, ALU.mult),
                    lambda: v.tensor_reduce(R, G, AX.X, ALU.add))
                v.nop().then_inc(S["g_sq"], 1)
                dve.wait_ge(S["g_std"], n + 1)
                seq(lambda: v.reciprocal(R, R),
                    lambda: v.tensor_tensor(T, T, R.unsqueeze(2).broadcast_to([P, K, HE]), ALU.mult),
                    lambda: v.tensor_tensor(T, T, bc(gam, K), ALU.mult),
                    lambda: v.tensor_tensor(T, T, bc(bet, K), ALU.add),
                    lambda: v.tensor_tensor(A2, T[:, :, 0:4], T[:, :, 4:8], ALU.add),
                    lambda: v.tensor_tensor(A2, A2, T[:, :, 8:12], ALU.add),
                    lambda: v.tensor_tensor(A2, A2, T[:, :, 12:16], ALU.add),
                    lambda: v.tensor_scalar(A2, A2, 1.0 / HEADS, None, ALU.mult),
                    lambda: v.memset(A3, 0.0))
                for i in range(EXPERTS):
                    for j in range(i + 1, EXPERTS):
                        seq(lambda: v.tensor_tensor(W, A2[:, :, i], A2[:, :, j], ALU.is_ge),
                            lambda: v.tensor_tensor(A3[:, :, j], A3[:, :, j], W, ALU.add),
                            lambda: v.tensor_scalar(W, W, -1.0, 1.0, ALU.mult, ALU.add),
                            lambda: v.tensor_tensor(A3[:, :, i], A3[:, :, i], W, ALU.add))
                seq(lambda: v.tensor_scalar(A3, A3, 2.0, None, ALU.is_lt),
                    lambda: v.tensor_reduce(R, A2, AX.X, ALU.max))
                if n:
                    dve.wait_ge(S["gt_st"], 16 * n)
                seq(lambda: v.tensor_tensor(A1, A2, R.unsqueeze(2).broadcast_to([P, K, EXPERTS]), ALU.subtract))
                v.nop().then_inc(S["g_e"], 1)
                dve.wait_ge(S["g_ex"], n + 1)
                seq(lambda: v.tensor_tensor(A1, A1, A3, ALU.mult),
                    lambda: v.tensor_reduce(R, A1, AX.X, ALU.add),
                    lambda: v.reciprocal(R, R),
                    lambda: v.tensor_tensor(A1, A1, R.unsqueeze(2).broadcast_to([P, K, EXPERTS]), ALU.mult))
                v.nop().then_inc(S["gt_ready"], 1)

            dve.wait_ge(S["wts"], 16 * 7)
            for n in range(len(GATE_BATCHES)):
                dve.wait_ge(S["th_in"], 16 * (n + 1))
                gate_fn(n, GK)

            def step(k, n0, q):
                if isinstance(k, int) and k == OUTSIDE:
                    dve.wait_ge(S["node_ready"], 1)
                    seq(lambda: v.tensor_scalar(g2[:, :, :], node[:, :, HEADS:2 * HEADS], DENOM_EPS, None, ALU.add),
                        lambda: v.reciprocal(g2[:, :, :], g2[:, :, :]))
                    for h in range(HEADS):
                        v.tensor_tensor(th[:, :, h * EXPERTS:(h + 1) * EXPERTS],
                                        node[:, :, 2 * HEADS + h * EXPERTS:2 * HEADS + (h + 1) * EXPERTS],
                                        g2[:, :, h:h + 1].broadcast_to([P, P, EXPERTS]), ALU.mult)
                    v.drain()
                    gate_fn(len(GATE_BATCHES), P)
                dve.wait_ge(S["y_done"], k + 1)
                dve.wait_ge(ff[q], 24 * (k - q) + 48)
                Y = yb[:, :, :, :].rearrange("p j e c -> p j (e c)")
                v.tensor_tensor(Y, ybank[q][:, :].rearrange("p (j n) -> p j n", j=FF),
                                fb2[:, :].unsqueeze(1).broadcast_to([P, FF, EXPERTS * CH]), ALU.add)\
                    .then_inc(S["ybank_free"], 1)
                v.drain()
                v.tensor_tensor(yb[:, :, :, :].rearrange("p j e c -> p (j e) c"),
                                yb[:, :, :, :].rearrange("p j e c -> p (j e) c"),
                                gf[q][:, :, :].rearrange("p j e -> p (j e)").unsqueeze(2)
                                .broadcast_to([P, FF * EXPERTS, CH]), ALU.mult)
                v.drain()
                v.tensor_tensor(yc[:, :, :, :], yb[:, :, 0:2, :], yb[:, :, 2:4, :], ALU.add)
                v.drain()
                v.tensor_tensor(yc[:, :, 0, :], yc[:, :, 0, :], yc[:, :, 1, :], ALU.add)
                v.drain()
                dve.wait_ge(ost[q], 8 * (k - q))
                v.tensor_tensor(yo[q][:, :, :], yc[:, :, 0, :], hr[q][:, :, :], ALU.add).then_inc(S["yo_done"], 1)

            chunks(dve, step)


_TAP_ORDER = [t for ts in TAP_TILES for t in ts]


def kernel(**inputs):
    import numpy as np
    import concourse.bacc as bacc
    from concourse.bass_utils import run_bass_kernel_spmd

    g = {k: np.asarray(v) for k, v in inputs.items()}

    def by_tap(w):
        r = w.reshape(CH, TAPS, -1).transpose(1, 0, 2)[_TAP_ORDER]
        return np.ascontiguousarray(r.reshape(TAPS * CH, -1))

    col = lambda a: np.ascontiguousarray(a.reshape(-1, 1))
    row = lambda a: np.ascontiguousarray(a.reshape(1, -1))
    arrays = {
        "x": g["x"], "cls_tok": col(g["cls_tok"]),
        "tok_W1": by_tap(g["L0_tok_W1"]), "tok_b1": col(g["L0_tok_b1"]),
        "tok_W2": np.ascontiguousarray(by_tap(np.ascontiguousarray(g["L0_tok_W2"].T)).T),
        "tok_b2": by_tap(col(g["L0_tok_b2"])),
        "tok_W3": by_tap(g["L0_tok_W3"]), "tok_b3": col(g["L0_tok_b3"]),
        "A_diag": col(g["L0_attn_A_diag"]),
        "B": np.ascontiguousarray(g["L0_attn_B"].transpose(1, 2, 0).reshape(CH, 2 * CH)),
        "C": np.ascontiguousarray(g["L0_attn_C"].transpose(2, 1, 0).reshape(2 * CH, CH)),
        "D": col(g["L0_attn_D"]), "dt": col(g["L0_attn_dt"]),
        "W_gat": g["L0_ffn_W_gat"], "att_src": row(g["L0_ffn_att_src"]), "att_dst": row(g["L0_ffn_att_dst"]),
        "b_gat": row(g["L0_ffn_b_gat"]), "ln_gamma": row(g["L0_ffn_ln_gamma"]),
        "ln_beta": row(g["L0_ffn_ln_beta"]), "W1": g["L0_ffn_W1"],
        "b1": np.ascontiguousarray(g["L0_ffn_b1"].T), "W2": g["L0_ffn_W2"], "b2": row(g["L0_ffn_b2"]),
        "edges": g["L0_ffn_edge_index"],
    }
    nc = bacc.Bacc("TRN2", target_bir_lowering=False, num_devices=1)
    args = [nc.dram_tensor("in_" + k, a.shape, mybir.dt.from_np(a.dtype), kind="ExternalInput").ap()
            for k, a in arrays.items()]
    args.append(nc.dram_tensor("out", [NODES, CH], f32, kind="ExternalOutput").ap())
    build(nc, *args)
    r = run_bass_kernel_spmd(nc, [{"in_" + k: a for k, a in arrays.items()}], core_ids=[0])
    return r.results[0]["out"].reshape(IMAGES, SEQ, CH)
```

```python
import concourse.bass as bass
from concourse import mybir
from contextlib import ExitStack

f32 = mybir.dt.float32
i32 = mybir.dt.int32
bf16 = mybir.dt.bfloat16
ALU = mybir.AluOpType
ACT = mybir.ActivationFunctionType
AX = mybir.AxisListType

IMAGES, CH, SIDE = 16, 64, 56
TOKENS = SIDE * SIDE
SEQ = TOKENS + 1
NODES = IMAGES * SEQ
ROWS = 8
CHUNK = ROWS * SIDE
CHUNKS = TOKENS // CHUNK
STEPS = CHUNK + 1
PAD = SIDE + 2
TAPS = 9
TAP_TILES = [(0, 1), (3, 4), (6, 7), (2, 5), (8,)]
FOLD = 4
FP = CHUNK // FOLD
HEADS, EXPERTS = 4, 4
HE = HEADS * EXPERTS
HIDDEN = 128
TW = HE + 2 * HEADS
GRAPH_NODES = 16 * 1024
EDGES = 262144
P = 128
LO = P
ETILES = EDGES // P
SORTED = EDGES + GRAPH_NODES
SCOLS = SORTED // P
HALF = 16
RING = 64
BLOCKS = SCOLS // RING
FRONT_BLOCKS = 18
EROUNDS = ETILES // (2 * HALF)
SROUNDS = LO // (2 * HALF)
GROUP = 4
GROUPS = ETILES // GROUP
RG = 2 * HALF // GROUP
FLAG = 65536
FAR = 1024.0
BIG = 1.0e30
EPS = 1e-5
DENOM_EPS = 1e-16
GRAPH_IMAGES = -(-GRAPH_NODES // SEQ)
NT = 512


def wait(eng, sem, value):
    if not (isinstance(value, int) and value <= 0):
        eng.wait_ge(sem, value)


def build(nc, x, cls_tok, tokW1, tokb1, tokW2, tokb2, tokW3, tokb3, A_diag, Bmat, Cmat, Dvec, dtv,
          W_gat, att_src, att_dst, b_gat, ln_gamma, ln_beta, W1, b1, W2, b2, edges, out):
    sorted_rec = nc.dram_tensor("sorted_rec", [SORTED, 2], i32, kind="Internal").ap()
    gathered = nc.dram_tensor("gathered", [P, SCOLS * TW], f32, kind="Internal").ap()
    table = nc.dram_tensor("table", [NODES, TW], f32, kind="Internal").ap()
    h_tok = nc.dram_tensor("h_tok", [NODES, CH], f32, kind="Internal").ap()
    xnT = nc.dram_tensor("xnT", [CH, NODES], f32, kind="Internal").ap()
    seg_scratch = nc.dram_tensor("seg_scratch", [2, P, P], i32, kind="Internal").ap()

    with ExitStack() as ctx:
        pick = [ctx.enter_context(nc.sbuf_tensor(f"pick{n}", [P, RING, 2], i32)) for n in range(2)]
        ring = [ctx.enter_context(nc.sbuf_tensor(f"ring{n}", [P, RING, TW], f32)) for n in range(2)]
        front(nc, pick, ring, x, cls_tok, tokW1, tokb1, tokW2, tokb2, tokW3, tokb3, A_diag, Bmat, Cmat, Dvec, dtv,
              W_gat, att_src, att_dst, edges, sorted_rec, gathered, table, h_tok, xnT, seg_scratch)
        back(nc, pick, ring, table, gathered, sorted_rec, seg_scratch, h_tok, xnT, b_gat, ln_gamma, ln_beta,
             W1, b1, W2, b2, out)


def gather_blocks(nc, pool, pick, ring, table, sorted_rec, gathered, sems, waited, first, count):
    g = nc.gpsimd
    pick_in, gath, ring_st = sems
    sorted_v = sorted_rec.rearrange("(p c) w -> p c w", c=SCOLS)

    def load_pick(k, h):
        g.dma_start(pick[h][:, :, :], sorted_v[:, bass.ds((first + k) * RING, RING), :]).then_inc(pick_in[h], 16)

    def store_block(k, h):
        g.dma_start(gathered[:, bass.ds((first + k) * RING * TW, RING * TW)],
                    ring[h][:, :, :].rearrange("p a b -> p (a b)")).then_inc(ring_st[h], 16)

    def gather_block(i, h, start=False, last=False):
        k = 2 * i + h
        pool.wait_ge(pick_in[h], 16 * (i + 1))
        wait(pool, ring_st[h], 16 * i)
        pool.sem_inc(waited, 1)
        for j in range(RING):
            if j == 8 and not start:
                pool.wait_ge(gath[1 - h], 16 * RING * (i + h))
                store_block(k - 1, 1 - h)
                if not last:
                    load_pick(k + 1, 1 - h)
            g.indirect_dma_start(
                out=ring[h][:, j, :], out_offset=None, in_=table[0:GRAPH_NODES, :],
                in_offset=bass.IndirectOffsetOnAxis(ap=pick[h][:, j, 0:1], axis=0)).then_inc(gath[h], 16)

    load_pick(0, 0)
    load_pick(1, 1)
    gather_block(0, 0, start=True)
    gather_block(0, 1)
    with pool.Fori(1, count // 2 - 1) as i:
        for h in range(2):
            gather_block(i, h)
    gather_block(count // 2 - 1, 0)
    gather_block(count // 2 - 1, 1, last=True)
    pool.wait_ge(gath[1], 16 * RING * (count // 2))
    store_block(count - 1, 1)
    for h in range(2):
        pool.wait_ge(ring_st[h], 16 * (count // 2))


def front(nc, pick, ring, x, cls_tok, tokW1, tokb1, tokW2, tokb2, tokW3, tokb3, A_diag, Bmat, Cmat, Dvec, dtv,
          W_gat, att_src, att_dst, edges, sorted_rec, gathered, table, h_tok, xnT, seg_scratch):
    ctx = ExitStack()
    with ctx:
        def sb(name, shape, dt=f32):
            return ctx.enter_context(nc.sbuf_tensor(name, shape, dt))

        def pb(name, shape, dt=f32):
            return ctx.enter_context(nc.psum_tensor(name, shape, dt))

        def sem(name):
            return ctx.enter_context(nc.semaphore(name))

        ident = sb("ident", [P, P])
        ident_b = sb("ident_b", [P, P], bf16)
        not_after = sb("not_after", [P, P])
        neg_ident_b = sb("neg_ident_b", [P, P], bf16)
        not_after_b = sb("not_after_b", [P, P], bf16)
        above = sb("above", [P, P])
        iota_i = sb("iota_i", [P, P], i32)
        iota_f = sb("iota_f", [P, P])
        part_i = sb("part_i", [P, 1], i32)
        part_f = sb("part_f", [P, 1])
        zero_b = sb("zero_b", [P, NT], bf16)
        zero_f = sb("zero_f", [P, P])
        center = sb("center", [CH, CH])
        mean = sb("mean", [CH, CH])
        eps_c = sb("eps_c", [P, 1])

        src_i = sb("src_i", [P, ETILES], i32)[:, :]
        dst_f = sb("dst_f", [P, ETILES])[:, :]
        pos_all = sb("pos_all", [P, ETILES], i32)
        arena = sb("arena", [P, ETILES * 5 // 2 + 2 * GROUP])
        at = [0]

        def carve(n, dt=f32):
            words = n if dt != bf16 else n // 2
            v = arena[:, at[0]:at[0] + words]
            at[0] += words
            return v if dt == f32 else v.bitcast(dt)

        IDS = ETILES + 2 * GROUP
        lo_f = carve(ETILES)
        lo_b = carve(IDS, bf16)
        hi_b = carve(IDS, bf16)
        hi128_b = carve(ETILES, bf16)
        tabs = [arena[:, n * STEPS:(n + 1) * STEPS] for n in range(4)]
        tab_a, tab_b, tab_k, tab_c = tabs

        xa = [sb(f"xa{n}", [P, PAD * PAD]) for n in range(2)]
        xb = [sb(f"xb{n}", [P, PAD * PAD]) for n in range(2)]
        dst_i = xa[0][:, 0:ETILES].bitcast(i32)
        tmp_i = xb[0][:, 0:ETILES].bitcast(i32)
        oh_hi = [sb(f"oh_hi{n}", [P, P, GROUP], bf16) for n in range(2)]
        oh_lo = [sb(f"oh_lo{n}", [P, P, GROUP], bf16) for n in range(2)]
        iota_g = sb("iota_g", [P, P, GROUP], bf16)
        hiT = [sb(f"hiT{n}", [P, GROUP * P]) for n in range(2)]
        place = [sb(f"place{n}", [P, HALF]) for n in range(2)]
        neg_part = sb("neg_part", [P, 1])
        spare = [t[:, :, :].rearrange("p a b -> p (a b)") for t in ring]
        W = GROUP * P
        hist = [spare[0][:, 0:W], spare[1][:, 0:W]]
        apart = spare[0][:, W:2 * W]
        earlier = [spare[1][:, W + n * W // 2:W + (n + 1) * W // 2].bitcast(bf16) for n in range(2)]
        pos = [sb(f"pos{n}", [P, HALF], i32) for n in range(2)]
        rec = [sb(f"rec{n}", [P, HALF, 2], i32) for n in range(2)]
        counts = sb("counts", [P, GROUP * P])
        deg = sb("deg", [P, P])
        incl = sb("incl", [P, P])
        base = sb("base", [P, P])
        rowbase = sb("rowbase", [P, 1])
        seg_i = sb("seg_i", [P, 2, P], i32)
        node_f = sb("node_f", [P, P])
        node_flag = sb("node_flag", [P, P])
        base_i = seg_i[:, 0, :]

        NTT = len(TAP_TILES)
        w1 = sb("w1", [P, NTT, CH])
        w2 = sb("w2", [CH, TAPS * CH])
        w3 = sb("w3", [P, NTT, CH])
        tb1 = sb("tb1", [CH, 1])
        tb2 = sb("tb2", [P, NTT])
        tb3 = sb("tb3", [CH, 1])
        b_sb = sb("b_sb", [CH, 2 * CH])
        c_sb = sb("c_sb", [2 * CH, CH])
        d_sb = sb("d_sb", [CH, 1])
        cls_c = sb("cls_c", [CH, 1])
        adiag = sb("adiag", [P, 1])
        dts = sb("dts", [P, 1])
        wproj = sb("wproj", [CH, TW])
        att_bc = sb("att_bc", [CH, 2, HE])
        wtmp = sb("wtmp", [CH, 2, HE])
        par = sb("par", [P, 16])

        h1 = sb("h1", [CH, CHUNK])
        gate = [sb(f"gate{n}", [P, CHUNK]) for n in range(2)]
        prod = sb("prod", [P, NTT, CHUNK])
        hT = [sb(f"hT{n}", [CH, TOKENS]) for n in range(2)]
        sq = [sb(f"sq{n}", [CH, CHUNK]) for n in range(2)]
        std = [sb(f"std{n}", [CH, CHUNK]) for n in range(2)]
        u = [sb(f"u{n}", [CH, CHUNK]) for n in range(2)]
        fin = [sb(f"fin{n}", [P, CHUNK]) for n in range(2)]
        wst = [sb(f"wst{n}", [P, CHUNK]) for n in range(2)]
        first_junk = [t[:, 0:P] for t in (*fin, *wst)]
        y = sb("y", [P, CHUNK])
        carry = sb("carry", [P, 2])
        start = sb("start", [P, 2])
        h2 = [sb(f"h2{n}", [CH, CHUNK]) for n in range(2)]
        xn = [sb(f"xn{n}", [CH, CHUNK]) for n in range(2)]
        t_out = [sb(f"t_out{n}", [P, FOLD, TW]) for n in range(2)]
        h_out = [sb(f"h_out{n}", [P, FOLD, CH]) for n in range(2)]

        bank = [pb(f"bank{n}", [P, 512]) for n in range(8)]
        p_hi, p_later, p_first, p_hist = bank[0:2], bank[2:4], bank[4:6], bank[6:8]

        names = """consts weights_in edges_in ids_ready groups_oh hist_added counts_done totals_ready
            rowbase_done base_ready ids_bcast hiT_ready earlier_ready hist_ready first_done
            group_pos pos_ready staged scat0 scat1 tabs_ready pads_zero
            x_in conv_done h1_done s_ps gate_done prod_done tok_done hT_done cent_done sq_done
            var_done std_done u_done bu_done y_done co_done h2_done cent2_done sq2_done var2_done
            std2_done xn_done tm_done tm_copied fin_read
            tm_st0 tm_st1 pick0 pick1 gath0 gath1 ring_st0 ring_st1 seg_st cls_in cls_ps cls_sb
            cls_st wp1 par_act par_dve waited""".split()
        S = {n: sem(n) for n in names}
        scat = [S["scat0"], S["scat1"]]
        pick_in = [S["pick0"], S["pick1"]]
        gath = [S["gath0"], S["gath1"]]
        ring_st = [S["ring_st0"], S["ring_st1"]]
        tm_st = [S["tm_st0"], S["tm_st1"]]

        src_v = edges[0, :].rearrange("(p t) -> p t", t=ETILES)
        dst_v = edges[1, :].rearrange("(p t) -> p t", t=ETILES)
        sorted_v = sorted_rec.rearrange("(p c) w -> p c w", c=SCOLS)

        def tile_rows(t):
            return CH * len(TAP_TILES[t])

        def taps_view(buf, c, t):
            src = xa if t < 3 else xb
            row, col = [(0, 0), (1, 0), (2, 0), (0, 2), (2, 2)][t]
            v = src[buf][0:tile_rows(t), :].rearrange("p (r q) -> p r q", q=PAD)
            return v[:, ROWS * c + row:ROWS * c + row + ROWS, col:col + SIDE]

        def r3(ap):
            return ap.rearrange("p (r q) -> p r q", q=SIDE)

        WEIGHT_LOADS = 3 * NTT + 14

        def slots(ba):
            return range(CHUNKS + 2 if isinstance(ba, int) and ba == IMAGES - 1 else CHUNKS)

        def active(bt, ba, c):
            first = isinstance(ba, int) and ba == 0
            att = ba is not None
            return (bt is not None and c < CHUNKS, att and c < CHUNKS, att and (not first or c >= 1)
                    and c <= CHUNKS, att and (not first or c >= 2))

        def steps(eng, step, last_apart=False):
            step(0, 0, None, None)
            step(1, 1, 0, 0)
            with eng.Fori(1, IMAGES // 2 - last_apart) as i:
                step(2 * i, 0, 2 * i - 1, 1)
                step(2 * i + 1, 1, 2 * i, 0)
            if last_apart:
                step(IMAGES - 2, 0, IMAGES - 3, 1)
                step(IMAGES - 1, 1, IMAGES - 2, 0)
            step(None, None, IMAGES - 1, 1)

        block = ctx.enter_context(nc.Block())

        @block.sync
        def _(sp):
            sp.dma_start(dst_i, dst_v).then_inc(S["edges_in"], 16)
            sp.dma_start(src_i, src_v).then_inc(S["edges_in"], 16)
            n = [0]

            def w(dst, src):
                n[0] += 1
                sp.dma_start(dst, src).then_inc(S["weights_in"], 16)

            row = 0
            for t in range(NTT):
                k = tile_rows(t)
                w(w1[0:k, t, :], tokW1[row:row + k, :])
                w(w3[0:k, t, :], tokW3[row:row + k, :])
                row += k
            w(w2[:, :], tokW2)
            w(tb1[:, :], tokb1)
            for t in range(NTT):
                w(tb2[0:tile_rows(t), t:t + 1], tokb2[t * P:t * P + tile_rows(t), :])
            w(tb3[:, :], tokb3)
            w(b_sb[:, :], Bmat)
            w(c_sb[:, :], Cmat)
            w(d_sb[:, :], Dvec)
            for g in range(2):
                w(adiag[g * CH:(g + 1) * CH, :], A_diag)
                w(dts[g * CH:(g + 1) * CH, :], dtv)
            w(wproj[:, 0:HE], W_gat)
            w(att_bc[:, 0, :], att_src.partition_broadcast(CH))
            w(att_bc[:, 1, :], att_dst.partition_broadcast(CH))
            w(cls_c[:, :], cls_tok)
            assert n[0] == WEIGHT_LOADS

            sp.wait_ge(S["base_ready"], 1)
            sp.dma_start(seg_scratch.rearrange("a p q -> p a q"), seg_i[:, :, :]).then_inc(S["seg_st"], 16)
            sp.wait_ge(S["cls_sb"], 8)
            for dst, s in ((table.rearrange("(b s) w -> b s w", s=SEQ)[:, 0, :], t_out[0][0:IMAGES, 0, :]),
                           (h_tok.rearrange("(b s) w -> b s w", s=SEQ)[:, 0, :], h_out[0][0:IMAGES, 0, :]),
                           (xnT.rearrange("c (b s) -> c b s", s=SEQ)[:, :, 0:1], xn[0][:, 0:IMAGES].unsqueeze(2))):
                sp.dma_start(dst, s, allow_slow_non_contiguous=True).then_inc(S["cls_st"], 16)
            sp.wait_ge(S["cls_st"], 48)

            def load_image(b, buf):
                src = x[b, :, :, :]
                va = xa[buf][:, :].rearrange("p (r q) -> p r q", q=PAD)
                vb = xb[buf][:, :].rearrange("p (r q) -> p r q", q=PAD)
                sp.dma_start(va[0:CH, 1:1 + SIDE, 1:1 + SIDE], src).then_inc(S["x_in"], 16)
                sp.dma_start(va[CH:P, 1:1 + SIDE, 0:SIDE], src).then_inc(S["x_in"], 16)
                sp.dma_start(vb[0:CH, 1:1 + SIDE, 1:1 + SIDE], src).then_inc(S["x_in"], 16)
                sp.dma_start(vb[CH:P, 0:SIDE, 1:1 + SIDE], src).then_inc(S["x_in"], 16)

            def store_chunk(b, c, q):
                sp.wait_ge(S["tm_copied"], 2 * (b * CHUNKS + c) + 2)
                sp.sem_inc(S["waited"], 1)
                node = b * SEQ + 1 + c * CHUNK
                sp.dma_start(table[bass.ds(node, CHUNK), :].rearrange("(p j) w -> p j w", j=FOLD),
                             t_out[q][0:FP, :, :]).then_inc(tm_st[q], 16)
                sp.dma_start(h_tok[bass.ds(node, CHUNK), :].rearrange("(p j) w -> p j w", j=FOLD),
                             h_out[q][0:FP, :, :]).then_inc(tm_st[q], 16)
                sp.dma_start(xnT[:, bass.ds(node, CHUNK)], xn[q][:, :]).then_inc(tm_st[q], 16)

            sp.wait_ge(S["pads_zero"], 1)
            load_image(0, 0)

            def loads_and_stores(b_tok, tok_par, b_att, att_par):
                if b_tok is not None and not (isinstance(b_tok, int) and b_tok == IMAGES - 1):
                    sp.wait_ge(S["x_in"], 64 * (b_tok + 1))
                    sp.sem_inc(S["waited"], 1)
                    if not (isinstance(b_tok, int) and b_tok == 0):
                        sp.wait_ge(S["prod_done"], 5 * CHUNKS * b_tok)
                        sp.sem_inc(S["waited"], 1)
                        sp.wait_ge(S["conv_done"], CHUNKS * b_tok)
                    sp.sem_inc(S["waited"], 1)
                    load_image(b_tok + 1, 1 - tok_par)
                for c in slots(b_att):
                    if active(b_tok, b_att, c)[3]:
                        q = (att_par * CHUNKS + c) % 2
                        if c >= 2:
                            store_chunk(b_att, c - 2, q)
                        else:
                            store_chunk(b_att - 1, c + CHUNKS - 2, q)

            steps(sp, loads_and_stores, last_apart=True)
            sp.wait_ge(S["seg_st"], 16)
            for q in range(2):
                sp.wait_ge(tm_st[q], 48 * CHUNKS * IMAGES // 2)

        @block.gpsimd
        def _(pool):
            g = nc.gpsimd
            g.memset(ident[:, :], 0.0)
            g.memset(not_after[:, :], FAR)
            g.memset(above[:, :], 1.0)
            g.memset(zero_f[:, :], 0.0)
            g.memset(zero_b[:, :], 0.0)
            g.memset(mean[:, :], 1.0 / CH)
            g.memset(center[:, :], -1.0 / CH)
            g.memset(eps_c[:, :], EPS)
            g.iota(iota_i[:, :], pattern=[[1, P]], base=0, channel_multiplier=0)
            g.iota(part_i[:, :], pattern=[[1, 1]], base=0, channel_multiplier=1)
            g.drain()
            g.affine_select(out=ident[:, :], in_=ident[:, :], compare_op=ALU.not_equal, fill=1.0, base=0,
                            pattern=[[-1, P]], channel_multiplier=1)
            g.affine_select(out=not_after[:, :], in_=not_after[:, :], compare_op=ALU.is_ge, fill=0.0, base=0,
                            pattern=[[-1, P]], channel_multiplier=1)
            g.affine_select(out=above[:, :], in_=above[:, :], compare_op=ALU.is_gt, fill=0.0, base=0,
                            pattern=[[1, P]], channel_multiplier=-1)
            g.affine_select(out=center[:, :], in_=center[:, :], compare_op=ALU.not_equal,
                            fill=1.0 - 1.0 / CH, base=0, pattern=[[-1, CH]], channel_multiplier=1)
            g.drain()
            g.nop().then_inc(S["consts"], 1)

            pool.wait_ge(S["ids_ready"], 1)
            for t in (*xa, *xb):
                g.memset(t[:, :], 0.0)
            g.drain()
            g.nop().then_inc(S["pads_zero"], 1)

            def scatter_half(k, h, places, sources, targets):
                g.tensor_copy(pos[h][:, :], places)
                g.tensor_copy(rec[h][:, :, 0], sources)
                g.tensor_copy(rec[h][:, :, 1], targets).then_inc(S["staged"], 1)
                pool.wait_ge(S["staged"], k + 1)
                pool.sem_inc(S["waited"], 1)
                for j in range(HALF):
                    g.indirect_dma_start(
                        out=sorted_rec, out_offset=bass.IndirectOffsetOnAxis(ap=pos[h][:, j:j + 1], axis=0),
                        in_=rec[h][:, j, :], in_offset=None).then_inc(scat[h], 16)

            def scatter_edges(i):
                for h in range(2):
                    cols = bass.ds((2 * i + h) * HALF, HALF)
                    pool.wait_ge(S["pos_ready"], 2 * i + h + 1)
                    wait(pool, scat[h], 16 * HALF * i)
                    pool.sem_inc(S["waited"], 1)
                    scatter_half(2 * i + h, h, pos_all[:, cols], src_i[:, cols], dst_f[:, cols])

            scatter_edges(0)
            with pool.Fori(1, EROUNDS) as i:
                scatter_edges(i)
            for i in range(SROUNDS):
                for h in range(2):
                    cols = slice((2 * i + h) * HALF, (2 * i + h + 1) * HALF)
                    pool.wait_ge(scat[h], 16 * HALF * (EROUNDS + i))
                    scatter_half(2 * (EROUNDS + i) + h, h, base_i[:, cols], node_f[:, cols], node_flag[:, cols])
            for h in range(2):
                pool.wait_ge(scat[h], 16 * HALF * (EROUNDS + SROUNDS))
            pool.wait_ge(S["cls_st"], 48)
            for q in range(2):
                pool.wait_ge(tm_st[q], 48 * CHUNKS * GRAPH_IMAGES // 2)

            gather_blocks(nc, pool, pick, ring, table, sorted_rec, gathered, (pick_in, gath, ring_st),
                          S["waited"], 0, FRONT_BLOCKS)

        @block.tensor
        def _(pe):
            mm = nc.tensor.matmul
            pe.wait_ge(S["ids_ready"], 1)
            mm(p_hist[0][:, :], zero_b[:, 0:P], zero_b[:, :], start=True, stop=False)

            def count(o, buf, start, stop):
                for j in range(GROUP):
                    m = mm(o[:, j * P:(j + 1) * P], oh_hi[buf][:, :, j], oh_lo[buf][:, :, j],
                           start=start, stop=stop)
                m.then_inc(S["hist_added"], 1)

            def count_pair(q):
                for n in range(2):
                    pe.wait_ge(S["groups_oh"], q + n + 1)
                    count(p_hist[0], n, False, False)

            count_pair(0)
            with pe.Fori(1, GROUPS // 2) as i:
                count_pair(2 * i)
            mm(p_hist[0][:, :], zero_b[:, 0:P], zero_b[:, :], start=False, stop=True).then_inc(S["counts_done"], 1)
            pe.wait_ge(S["totals_ready"], 1)
            mm(p_hi[0][:, 0:1], above[:, :], incl[:, P - 1:P], start=True, stop=True).then_inc(S["rowbase_done"], 1)
            pe.wait_ge(S["base_ready"], 1)

            def broadcast_ids(q, t0, b):
                wait(pe, S["hiT_ready"], q - 1)
                wait(pe, S["earlier_ready"], q - 1)
                for j in range(GROUP):
                    mm(p_hi[b][:, j * P:(j + 1) * P], hi_b[:, bass.ds(t0 + j, 1)].broadcast_to([P, P]),
                       ident_b[:, :], start=True, stop=True)
                for j in range(GROUP):
                    o = p_later[b][:, j * P:(j + 1) * P]
                    mm(o, hi_b[:, bass.ds(t0 + j, 1)].broadcast_to([P, P]), ident_b[:, :],
                       start=True, stop=False)
                    mm(o, ident_b[:, :], not_after_b[:, :], start=False, stop=False)
                    m = mm(o, neg_ident_b[:, :], hi_b[:, bass.ds(t0 + j, 1)].broadcast_to([P, P]),
                           start=False, stop=True)
                m.then_inc(S["ids_bcast"], 1)

            def sort_round(i):
                for gi in range(RG):
                    q = i * RG + gi
                    b = gi % 2
                    broadcast_ids(q + 1, (i * RG + gi + 1) * GROUP, 1 - b)
                    pe.wait_ge(S["groups_oh"], GROUPS + q + 1)
                    wait(pe, S["hist_ready"], q - 1)
                    count(p_hist[b], b, True, True)
                    pe.wait_ge(S["hiT_ready"], q + 1)
                    wait(pe, S["hist_ready"], q)
                    wait(pe, S["group_pos"], q - 1)
                    pe.wait_ge(S["earlier_ready"], q + 1)
                    for j in range(GROUP):
                        mm(p_first[b][:, j * P:(j + 1) * P], hiT[b][:, j * P:(j + 1) * P],
                           hist[b][:, j * P:(j + 1) * P], start=True, stop=False)
                        m = mm(p_first[b][:, j * P:(j + 1) * P], earlier[b][:, j * P:(j + 1) * P],
                               oh_lo[b][:, :, j], start=False, stop=True)
                    m.then_inc(S["first_done"], 1)

            broadcast_ids(0, 0, 0)
            sort_round(0)
            with pe.Fori(1, EROUNDS) as i:
                sort_round(i)

            pe.wait_ge(S["wp1"], 1)
            pe.wait_ge(S["tabs_ready"], 1)
            N = IMAGES
            mm(bank[4][0:CH, 0:N], center[:, :], hT[0][:, 0:N], start=True, stop=True).then_inc(S["cls_ps"], 1)
            pe.wait_ge(S["cls_sb"], 1)
            mm(bank[5][0:CH, 0:N], mean[:, :], sq[0][:, 0:N], start=True, stop=True).then_inc(S["cls_ps"], 1)
            pe.wait_ge(S["cls_sb"], 2)
            mm(bank[6][:, 0:N], b_sb[:, :], u[0][:, 0:N], start=True, stop=True).then_inc(S["cls_ps"], 1)
            pe.wait_ge(S["cls_sb"], 3)
            mm(bank[7][0:CH, 0:N], c_sb[:, :], y[:, 0:N], start=True, stop=True).then_inc(S["cls_ps"], 1)
            pe.wait_ge(S["cls_sb"], 4)
            mm(bank[4][0:CH, 0:N], center[:, :], h2[0][:, 0:N], start=True, stop=True).then_inc(S["cls_ps"], 1)
            pe.wait_ge(S["cls_sb"], 5)
            mm(bank[5][0:CH, 0:N], mean[:, :], sq[1][:, 0:N], start=True, stop=True).then_inc(S["cls_ps"], 1)
            pe.wait_ge(S["cls_sb"], 6)
            mm(bank[6][0:N, 0:TW], xn[0][:, 0:N], wproj[:, :], start=True, stop=True)
            mm(bank[6][0:N, 128:128 + CH], h2[0][:, 0:N], ident[0:CH, 0:CH], start=True, stop=True)\
                .then_inc(S["cls_ps"], 1)
            pe.wait_ge(S["cls_sb"], 8)

            def step(bt, tp, ba, ap):
                nt = bt * CHUNKS if bt is not None else None
                na = ba * CHUNKS if ba is not None else None
                zero = isinstance(bt, int) and bt == 0
                zero_a = isinstance(ba, int) and ba == 0

                def conv(c):
                    k = nt + c
                    if c == 0:
                        pe.wait_ge(S["x_in"], 64 * (bt + 1))
                    if not (zero and c == 0):
                        pe.wait_ge(S["h1_done"], k)
                    for t in range(NTT):
                        n = tile_rows(t)
                        m = mm(bank[0][0:CH, 0:CHUNK], w1[0:n, t, :], taps_view(tp, c, t),
                               start=t == 0, stop=t == NTT - 1)
                    m.then_inc(S["conv_done"], 1)

                def gates(c, t):
                    k = 5 * (nt + c) + t
                    if t == 0:
                        pe.wait_ge(S["h1_done"], nt + c + 1)
                    if not (zero and c == 0 and t < 2):
                        pe.wait_ge(S["gate_done"], k - 1)
                        if t == NTT - 1:
                            pe.sem_inc(S["waited"], 1)
                    n = tile_rows(t)
                    o = (5 * (tp * CHUNKS + c) + t) % 2
                    mm(bank[1 + o][0:n, 0:CHUNK], w2[:, 128 * t:128 * t + n], h1[:, :],
                       start=True, stop=True).then_inc(S["s_ps"], 1)

                def project(c, t):
                    k = 5 * (nt + c) + t
                    n = tile_rows(t)
                    pe.wait_ge(S["prod_done"], k + 1)
                    if t == 0 and not (zero and c == 0):
                        pe.wait_ge(S["hT_done"], nt + c)
                    pe.sem_inc(S["waited"], 1)
                    m = mm(bank[3][0:CH, 0:CHUNK], w3[0:n, t, :], prod[0:n, t, :], start=t == 0, stop=t == NTT - 1)
                    if t == NTT - 1:
                        m.then_inc(S["tok_done"], 1)

                tok = bt is not None
                att = ba is not None
                if tok:
                    conv(0)
                for c in slots(ba):
                    tc, a0, a1, a2 = active(bt, ba, c)
                    if a0:
                        pe.wait_ge(S["hT_done"], na + CHUNKS)
                        if not (zero_a and c == 0):
                            pe.wait_ge(S["u_done"], na + c)
                        pe.sem_inc(S["waited"], 1)
                        mm(bank[4][0:CH, 0:CHUNK], center[:, :], hT[ap][:, c * CHUNK:(c + 1) * CHUNK],
                           start=True, stop=True).then_inc(S["cent_done"], 1)
                    if tc:
                        gates(c, 0)
                    if a2:
                        q = (ap * CHUNKS + c - 2) % 2
                        pe.wait_ge(S["xn_done"], na + c - 1)
                        pe.wait_ge(S["fin_read"], na + min(c, CHUNKS))
                        for j in range(FOLD):
                            mm(bank[6][0:FP, j * P:j * P + TW], xn[q][:, j:CHUNK:FOLD], wproj[:, :],
                               start=True, stop=True)
                            m = mm(bank[6][0:FP, j * P + 32:j * P + 32 + CH], h2[q][:, j:CHUNK:FOLD],
                                   ident[0:CH, 0:CH], start=True, stop=True)
                        m.then_inc(S["tm_done"], 1)
                    if tc:
                        gates(c, 1)
                    if a1:
                        pe.wait_ge(S["y_done"], na + c)
                        if c > 1 or not zero_a:
                            pe.wait_ge(S["xn_done"], na + c - 1)
                        mm(bank[7][0:CH, 0:CHUNK], c_sb[:, :], y[:, :], start=True, stop=True)\
                            .then_inc(S["co_done"], 1)
                    if tc:
                        gates(c, 2)
                    if a0:
                        pe.wait_ge(S["sq_done"], na + c + 1)
                        pe.sem_inc(S["waited"], 1)
                        mm(bank[5][0:CH, 0:CHUNK], mean[:, :], sq[0][:, :], start=True, stop=True)\
                            .then_inc(S["var_done"], 1)
                    if tc:
                        gates(c, 3)
                    if a1:
                        pe.wait_ge(S["h2_done"], na + c)
                        pe.sem_inc(S["waited"], 1)
                        mm(bank[7][0:CH, 0:CHUNK], center[:, :], h2[(ap * CHUNKS + c - 1) % 2][:, :],
                           start=True, stop=True).then_inc(S["cent2_done"], 1)
                    if tc:
                        gates(c, 4)
                        project(c, 0)
                    if a1:
                        pe.wait_ge(S["sq2_done"], na + c)
                        if a2:
                            pe.wait_ge(S["tm_copied"], 2 * (na + c - 1))
                        pe.sem_inc(S["waited"], 1)
                        mm(bank[6][0:CH, 0:CHUNK], mean[:, :], sq[1][:, :], start=True, stop=True)\
                            .then_inc(S["var2_done"], 1)
                    if tc:
                        if c + 1 < CHUNKS:
                            conv(c + 1)
                        project(c, 1)
                    if a0:
                        pe.wait_ge(S["u_done"], na + c + 1)
                        if a1:
                            pe.wait_ge(S["std2_done"], na + c)
                        elif not zero_a:
                            pe.wait_ge(S["tm_copied"], 2 * na)
                        mm(bank[6][:, 0:CHUNK], b_sb[:, :], u[(ap * CHUNKS + c) % 2][:, :], start=True, stop=True)\
                            .then_inc(S["bu_done"], 1)
                    if tc:
                        project(c, 2)
                        project(c, 3)
                        project(c, 4)

            steps(pe, step)

        @block.scalar
        def _(act):
            a = nc.scalar.activation
            act.wait_ge(S["base_ready"], 1)

            def hi_one_hot(q, b):
                act.wait_ge(S["ids_bcast"], q + 1)
                wait(act, S["first_done"], q - 1)
                a(hiT[b][:, :], p_hi[b][:, :], ACT.Abs, bias=neg_part[:, :])
                nc.scalar.drain()
                a(hiT[b][:, :], hiT[b][:, :], ACT.Relu, scale=-1.0, bias=1.0).then_inc(S["hiT_ready"], 1)

            def earlier_edges(b):
                a(apart[:, :], p_later[b][:, :], ACT.Abs)
                nc.scalar.drain()
                a(earlier[b][:, :], apart[:, :], ACT.Relu, scale=-1.0, bias=1.0).then_inc(S["earlier_ready"], 1)

            def sort_round(i):
                for gi in range(RG):
                    q = i * RG + gi
                    earlier_edges(gi % 2)
                    hi_one_hot(q + 1, 1 - gi % 2)

            hi_one_hot(0, 0)
            sort_round(0)
            with act.Fori(1, EROUNDS) as i:
                sort_round(i)

            act.wait_ge(S["weights_in"], 16 * WEIGHT_LOADS)
            a(par[:, 0:1], dts[:, :], ACT.Sigmoid).then_inc(S["par_act"], 1)
            act.wait_ge(S["par_dve"], 1)
            a(par[:, 3:4], par[:, 2:3], ACT.Sqrt).then_inc(S["par_act"], 1)

            N = IMAGES
            act.wait_ge(S["cls_ps"], 1)
            a(sq[0][:, 0:N], bank[4][0:CH, 0:N], ACT.Square).then_inc(S["cls_sb"], 1)
            act.wait_ge(S["cls_ps"], 2)
            a(std[0][:, 0:N], bank[5][0:CH, 0:N], ACT.Sqrt, bias=eps_c[0:CH, :]).then_inc(S["cls_in"], 1)
            act.wait_ge(S["cls_ps"], 5)
            a(sq[1][:, 0:N], bank[4][0:CH, 0:N], ACT.Square).then_inc(S["cls_sb"], 1)
            act.wait_ge(S["cls_ps"], 6)
            a(std[1][:, 0:N], bank[5][0:CH, 0:N], ACT.Sqrt, bias=eps_c[0:CH, :]).then_inc(S["cls_in"], 1)
            act.wait_ge(S["cls_ps"], 7)
            a(t_out[0][0:N, 0, :], bank[6][0:N, 0:TW], ACT.Copy).then_inc(S["cls_sb"], 1)
            a(h_out[0][0:N, 0, :], bank[6][0:N, 128:128 + CH], ACT.Copy).then_inc(S["cls_sb"], 1)

            def step(bt, tp, ba, ap):
                nt = bt * CHUNKS if bt is not None else None
                na = ba * CHUNKS if ba is not None else None
                tok = bt is not None
                att = ba is not None
                zero = isinstance(bt, int) and bt == 0
                zero_a = isinstance(ba, int) and ba == 0

                def relu(c):
                    act.wait_ge(S["conv_done"], nt + c + 1)
                    if not (zero and c == 0):
                        act.wait_ge(S["s_ps"], 5 * (nt + c))
                    a(h1[:, :], bank[0][0:CH, 0:CHUNK], ACT.Relu, bias=tb1[:, :]).then_inc(S["h1_done"], 1)

                def gate_(c, t):
                    k = 5 * (nt + c) + t
                    o = (5 * (tp * CHUNKS + c) + t) % 2
                    n = tile_rows(t)
                    act.wait_ge(S["s_ps"], k + 1)
                    if not (zero and c == 0 and t < 2):
                        act.wait_ge(S["prod_done"], k - 1)
                    a(gate[o][0:n, :], bank[1 + o][0:n, 0:CHUNK], ACT.Sigmoid, bias=tb2[0:n, t:t + 1])\
                        .then_inc(S["gate_done"], 1)

                if tok:
                    relu(0)
                for c in slots(ba):
                    tc, a0, a1, a2 = active(bt, ba, c)
                    if a0:
                        act.wait_ge(S["cent_done"], na + c + 1)
                        if not (zero_a and c == 0):
                            act.wait_ge(S["var_done"], na + c)
                        a(sq[0][:, :], bank[4][0:CH, 0:CHUNK], ACT.Square).then_inc(S["sq_done"], 1)
                    if tc:
                        gate_(c, 0)
                    if a2:
                        q = (ap * CHUNKS + c - 2) % 2
                        act.wait_ge(S["tm_done"], na + c - 1)
                        if not (zero_a and c - 2 < 2):
                            act.wait_ge(tm_st[q], 24 * (na + c - 2 - q))
                        v = bank[6][0:FP, :].rearrange("p (j w) -> p j w", w=P)
                        a(t_out[q][0:FP, :, :], v[:, :, 0:TW], ACT.Copy).then_inc(S["tm_copied"], 1)
                        a(h_out[q][0:FP, :, :], v[:, :, 32:32 + CH], ACT.Copy).then_inc(S["tm_copied"], 1)
                    if tc:
                        gate_(c, 1)
                        gate_(c, 2)
                        gate_(c, 3)
                    if a1:
                        act.wait_ge(S["cent2_done"], na + c)
                        if not (zero_a and c == 1):
                            act.wait_ge(S["var2_done"], na + c - 1)
                        a(sq[1][:, :], bank[7][0:CH, 0:CHUNK], ACT.Square).then_inc(S["sq2_done"], 1)
                    if tc:
                        gate_(c, 4)
                    if a0 or a1:
                        nc.scalar.preload_act_table_set("natural_log_exp_and_others")
                    if a0:
                        act.wait_ge(S["var_done"], na + c + 1)
                        wait(act, S["u_done"], na + c)
                        a(std[0][:, :], bank[5][0:CH, 0:CHUNK], ACT.Ln, bias=eps_c[0:CH, :])
                    if a1:
                        act.wait_ge(S["var2_done"], na + c)
                        wait(act, S["xn_done"], na + c - 1)
                        a(std[1][:, :], bank[6][0:CH, 0:CHUNK], ACT.Ln, bias=eps_c[0:CH, :])
                    if a0 or a1:
                        nc.scalar.drain()
                    if a0:
                        a(std[0][:, :], std[0][:, :], ACT.Exp, scale=-0.5).then_inc(S["std_done"], 1)
                    if a1:
                        a(std[1][:, :], std[1][:, :], ACT.Exp, scale=-0.5).then_inc(S["std2_done"], 1)
                    if tc:
                        if c + 1 < CHUNKS:
                            relu(c + 1)
                        act.wait_ge(S["tok_done"], nt + c + 1)
                        if att and not zero_a:
                            act.wait_ge(S["h2_done"], na - CHUNKS + c + 1)
                        a(hT[tp][:, c * CHUNK:(c + 1) * CHUNK], bank[3][0:CH, 0:CHUNK], ACT.Identity,
                          bias=tb3[:, :]).then_inc(S["hT_done"], 1)

            steps(act, step)

        @block.vector
        def _(dve):
            v = nc.vector
            dve.wait_ge(S["consts"], 1)
            dve.wait_ge(S["edges_in"], 32)
            v.tensor_copy(ident_b[:, :], ident[:, :])
            v.tensor_copy(iota_f[:, :], iota_i[:, :])
            v.tensor_copy(not_after_b[:, :], not_after[:, :])
            v.tensor_scalar(neg_ident_b[:, :], ident[:, :], -1.0, None, ALU.mult)
            v.tensor_copy(iota_g[:, :, :], iota_i[:, :].unsqueeze(2).broadcast_to([P, P, GROUP]))
            v.memset(lo_b[:, ETILES:IDS], 0.0)
            v.memset(hi_b[:, ETILES:IDS], 0.0)
            v.tensor_copy(part_f[:, :], part_i[:, :])
            v.tensor_single_scalar(tmp_i, dst_i, 7, ALU.arith_shift_right)
            v.tensor_copy(dst_f, dst_i)
            v.drain()
            v.tensor_copy(hi_b[:, 0:ETILES], tmp_i)
            v.tensor_scalar(neg_part[:, :], part_f[:, :], -1.0, None, ALU.mult)
            v.tensor_scalar(hi128_b[:, 0:ETILES], tmp_i, float(LO), None, ALU.mult)
            v.tensor_scalar(node_f[:, :], part_f[:, 0:1].broadcast_to([P, P]), float(LO), None, ALU.mult)
            v.drain()
            v.tensor_tensor(lo_f, dst_f, hi128_b[:, 0:ETILES], ALU.subtract)
            v.tensor_tensor(node_f[:, :], node_f[:, :], iota_f[:, :], ALU.add)
            v.drain()
            v.tensor_copy(lo_b[:, 0:ETILES], lo_f)
            v.tensor_scalar(node_flag[:, :], node_f[:, :], float(FLAG), None, ALU.add)
            v.drain()
            v.nop().then_inc(S["ids_ready"], 1)

            def one_hots(t0, b):
                for o, ids in ((oh_hi, hi_b), (oh_lo, lo_b)):
                    last = v.tensor_tensor(o[b][:, :, :], ids[:, bass.ds(t0, GROUP)].unsqueeze(1)
                                           .broadcast_to([P, P, GROUP]), iota_g[:, :, :], ALU.is_equal)
                last.then_inc(S["groups_oh"], 1)

            def count_pair(q):
                for n in range(2):
                    wait(dve, S["hist_added"], q + n - 1)
                    one_hots((q + n) * GROUP, n)

            count_pair(0)
            with dve.Fori(1, GROUPS // 2) as i:
                count_pair(2 * i)
            dve.wait_ge(S["counts_done"], 1)
            v.tensor_copy(counts[:, :], p_hist[0][:, :])
            v.drain()
            v.tensor_tensor(deg[:, :], counts[:, 0:P], counts[:, P:2 * P], ALU.add)
            v.drain()
            for j in (2, 3):
                v.tensor_tensor(deg[:, :], deg[:, :], counts[:, j * P:(j + 1) * P], ALU.add)
                v.drain()
            v.tensor_scalar(deg[:, :], deg[:, :], 1.0, None, ALU.add)
            v.drain()
            v.tensor_tensor_scan(incl[:, :], deg[:, :], zero_f[:, :], 0.0, ALU.add, ALU.add)
            v.drain()
            v.nop().then_inc(S["totals_ready"], 1)
            dve.wait_ge(S["rowbase_done"], 1)
            v.tensor_copy(rowbase[:, :], p_hi[0][:, 0:1])
            v.tensor_tensor(base[:, :], incl[:, :], deg[:, :], ALU.subtract)
            v.drain()
            v.tensor_scalar(base[:, :], base[:, :], rowbase[:, 0:1], None, ALU.add)
            v.drain()
            v.tensor_copy(seg_i[:, 0, :], base[:, :])
            v.tensor_tensor(incl[:, :], base[:, :], deg[:, :], ALU.add)
            v.drain()
            v.tensor_scalar(seg_i[:, 1, :], incl[:, :], -1.0, None, ALU.add)
            v.tensor_scalar(hist[0][:, 0:P], base[:, :], 1.0, None, ALU.add)
            v.drain()
            for j in (1, 2, 3):
                v.tensor_tensor(hist[0][:, j * P:(j + 1) * P], hist[0][:, (j - 1) * P:j * P],
                                counts[:, (j - 1) * P:j * P], ALU.add)
                v.drain()
            v.nop().then_inc(S["base_ready"], 1)

            def sort_round(i):
                for h in range(2):
                    for g in range(RG // 2):
                        gi = h * (RG // 2) + g
                        q = i * RG + gi
                        b = gi % 2
                        t0 = (i * RG + gi) * GROUP
                        v.drain()
                        dve.wait_ge(S["hist_added"], GROUPS + q + 1)
                        v.tensor_tensor(hist[1 - b][:, :], hist[b][:, :], p_hist[b][:, :], ALU.add)\
                            .then_inc(S["hist_ready"], 1)
                        dve.wait_ge(S["first_done"], q + 1)
                        for j in range(GROUP):
                            last = v.scalar_tensor_tensor(
                                out=first_junk[j], in0=iota_f[:, :],
                                scalar=lo_f[:, bass.ds(t0 + j, 1)], in1=p_first[b][:, j * P:(j + 1) * P],
                                op0=ALU.is_equal, op1=ALU.mult,
                                accum_out=place[h][:, g * GROUP + j:g * GROUP + j + 1])
                        last.then_inc(S["group_pos"], 1)
                        one_hots(t0 + 2 * GROUP, b)
                    v.drain()
                    v.tensor_copy(pos_all[:, bass.ds((2 * i + h) * HALF, HALF)], place[h][:, :])\
                        .then_inc(S["pos_ready"], 1)

            one_hots(0, 0)
            one_hots(GROUP, 1)
            sort_round(0)
            with dve.Fori(1, EROUNDS) as i:
                sort_round(i)
            dve.wait_ge(S["weights_in"], 16 * WEIGHT_LOADS)
            wh = wproj[:, 0:HE].unsqueeze(1).broadcast_to([CH, 2, HE])
            v.tensor_tensor(wtmp[:, :, :], wh, att_bc[:, :, :], ALU.mult)
            v.drain()
            v.tensor_reduce(wproj[:, HE:TW], wtmp[:, :, :].rearrange("p a (h e) -> p (a h) e", e=EXPERTS),
                            AX.X, ALU.add)
            v.tensor_scalar(c_sb[CH:P, :], c_sb[CH:P, :], -1.0, None, ALU.mult)
            v.tensor_copy(hT[0][:, 0:IMAGES], cls_c[:, 0:1].broadcast_to([CH, IMAGES]))
            v.drain()
            v.nop().then_inc(S["wp1"], 1)

            def p_(n):
                return par[:, n:n + 1]

            def seq(*ops):
                for op in ops:
                    op()
                    v.drain()

            dve.wait_ge(S["par_act"], 1)
            seq(lambda: v.tensor_scalar(p_(1), adiag[:, :], 0.0, None, ALU.max),
                lambda: v.tensor_tensor(p_(7), p_(0), p_(0), ALU.mult),
                lambda: v.tensor_tensor(p_(7), p_(7), p_(1), ALU.mult),
                lambda: v.tensor_scalar(p_(7), p_(7), 1.0, None, ALU.add),
                lambda: v.reciprocal(p_(2), p_(7)))
            v.nop().then_inc(S["par_dve"], 1)
            dve.wait_ge(S["par_act"], 2)
            seq(lambda: v.reciprocal(p_(7), p_(3)),
                lambda: v.tensor_tensor(p_(7), p_(7), p_(2), ALU.mult),
                lambda: v.tensor_tensor(p_(7), p_(7), p_(3), ALU.add),
                lambda: v.tensor_scalar(p_(3), p_(7), 0.5, None, ALU.mult),
                lambda: v.reciprocal(p_(7), p_(3)),
                lambda: v.tensor_tensor(p_(4), p_(7), p_(2), ALU.mult),
                lambda: v.tensor_tensor(p_(5), p_(4), p_(0), ALU.mult))
            v.memset(tab_c[:, 0:1], 1.0)
            v.memset(tab_k[:, 0:1], 0.0)
            v.drain()
            n = 1
            while n < STEPS:
                m = min(2 * n, STEPS) - n
                seq(lambda: v.tensor_tensor(p_(6), p_(1), p_(5), ALU.mult),
                    lambda: v.tensor_scalar(p_(6), p_(6), -1.0, None, ALU.mult))
                v.tensor_scalar(tab_a[:, 0:m], tab_k[:, 0:m], p_(6), None, ALU.mult)
                v.tensor_scalar(tab_b[:, 0:m], tab_k[:, 0:m], p_(4), None, ALU.mult)
                v.drain()
                v.scalar_tensor_tensor(out=tab_c[:, n:n + m], in0=tab_c[:, 0:m], scalar=p_(4), in1=tab_a[:, 0:m],
                                       op0=ALU.mult, op1=ALU.add)
                v.scalar_tensor_tensor(out=tab_k[:, n:n + m], in0=tab_c[:, 0:m], scalar=p_(5), in1=tab_b[:, 0:m],
                                       op0=ALU.mult, op1=ALU.add)
                v.drain()
                seq(lambda: v.tensor_tensor(p_(6), p_(6), p_(5), ALU.mult),
                    lambda: v.tensor_tensor(p_(5), p_(5), p_(4), ALU.mult),
                    lambda: v.tensor_scalar(p_(5), p_(5), 2.0, None, ALU.mult),
                    lambda: v.tensor_tensor(p_(4), p_(4), p_(4), ALU.mult),
                    lambda: v.tensor_tensor(p_(4), p_(4), p_(6), ALU.add))
                n *= 2
            seq(lambda: v.tensor_tensor(p_(8), p_(1), tab_k[:, CHUNK:STEPS], ALU.mult),
                lambda: v.tensor_scalar(p_(8), p_(8), -1.0, None, ALU.mult))
            seq(lambda: v.tensor_tensor(p_(6), p_(1), p_(0), ALU.mult),
                lambda: v.tensor_tensor(p_(7), p_(2), p_(0), ALU.mult),
                lambda: v.scalar_tensor_tensor(out=tab_a, in0=tab_k, scalar=p_(6), in1=tab_c, op0=ALU.mult, op1=ALU.add),
                lambda: v.tensor_scalar(tab_a, tab_a, p_(7), None, ALU.mult),
                lambda: v.scalar_tensor_tensor(out=tab_b, in0=tab_c, scalar=p_(0), in1=tab_k, op0=ALU.mult, op1=ALU.subtract),
                lambda: v.tensor_scalar(tab_b, tab_b, p_(7), None, ALU.mult))
            v.nop().then_inc(S["tabs_ready"], 1)

            N = IMAGES
            dve.wait_ge(S["cls_in"], 1)
            seq(lambda: v.reciprocal(std[0][:, 0:N], std[0][:, 0:N]))
            v.tensor_tensor(u[0][:, 0:N], bank[4][0:CH, 0:N], std[0][:, 0:N], ALU.mult).then_inc(S["cls_sb"], 1)
            dve.wait_ge(S["cls_ps"], 3)
            v.tensor_tensor(start[:, 0:1], bank[6][:, 0:1], tab_a[:, 0:1], ALU.mult)
            v.tensor_tensor(start[:, 1:2], bank[6][:, 0:1], tab_b[:, 0:1], ALU.mult)
            v.tensor_scalar(y[:, 0:N], bank[6][:, 0:N], tab_b[:, 0:1], None, ALU.mult).then_inc(S["cls_sb"], 1)
            dve.wait_ge(S["cls_ps"], 4)
            v.scalar_tensor_tensor(out=h2[0][:, 0:N], in0=u[0][:, 0:N], scalar=d_sb[:, :],
                                   in1=bank[7][0:CH, 0:N], op0=ALU.mult, op1=ALU.add)
            v.drain()
            v.tensor_tensor(h2[0][:, 0:N], h2[0][:, 0:N], hT[0][:, 0:N], ALU.add).then_inc(S["cls_sb"], 1)
            dve.wait_ge(S["cls_in"], 2)
            seq(lambda: v.reciprocal(std[1][:, 0:N], std[1][:, 0:N]))
            v.tensor_tensor(xn[0][:, 0:N], bank[4][0:CH, 0:N], std[1][:, 0:N], ALU.mult).then_inc(S["cls_sb"], 1)
            dve.wait_ge(S["cls_st"], 48)

            def step(bt, tp, ba, ap):
                nt = bt * CHUNKS if bt is not None else None
                na = ba * CHUNKS if ba is not None else None
                tok = bt is not None
                att = ba is not None
                zero = isinstance(bt, int) and bt == 0
                zero_a = isinstance(ba, int) and ba == 0
                for c in slots(ba):
                    tc, a0, a1, _ = active(bt, ba, c)
                    q = (ap * CHUNKS + c) % 2 if att else 0

                    def gated(*tiles):
                        for t in tiles:
                            k = 5 * (nt + c) + t
                            o = (5 * (tp * CHUNKS + c) + t) % 2
                            n = tile_rows(t)
                            dve.wait_ge(S["gate_done"], k + 1)
                            v.tensor_tensor(r3(prod[0:n, t, :]), taps_view(tp, c, t), r3(gate[o][0:n, :]),
                                            ALU.mult).then_inc(S["prod_done"], 1)

                    if tc:
                        if not (zero and c == 0):
                            dve.wait_ge(S["tok_done"], nt + c)
                        gated(0, 1)
                    if a1:
                        dve.wait_ge(S["co_done"], na + c)
                        wait(dve, S["tm_done"], na + c - 2)
                        v.scalar_tensor_tensor(out=h2[1 - q][:, :], in0=u[1 - q][:, :], scalar=d_sb[:, :],
                                               in1=bank[7][0:CH, 0:CHUNK], op0=ALU.mult, op1=ALU.add)
                        v.drain()
                        before_c = (hT[ap][:, (c - 1) * CHUNK:c * CHUNK] if c else
                                    hT[1 - ap][:, (CHUNKS - 1) * CHUNK:CHUNKS * CHUNK])
                        v.tensor_tensor(h2[1 - q][:, :], h2[1 - q][:, :], before_c, ALU.add)\
                            .then_inc(S["h2_done"], 1)
                    if tc:
                        gated(2, 3, 4)
                    if a0:
                        dve.wait_ge(S["std_done"], na + c + 1)
                        v.tensor_tensor(u[q][:, :], bank[4][0:CH, 0:CHUNK], std[0][:, :], ALU.mult)\
                            .then_inc(S["u_done"], 1)
                    if a1:
                        dve.wait_ge(S["std2_done"], na + c)
                        if not (zero_a and c - 1 < 2):
                            dve.wait_ge(tm_st[1 - q], 24 * (na + c - 1 - (1 - q)))
                        v.tensor_tensor(xn[1 - q][:, :], bank[7][0:CH, 0:CHUNK], std[1][:, :], ALU.mult)\
                            .then_inc(S["xn_done"], 1)
                    if a0:
                        dve.wait_ge(S["bu_done"], na + c + 1)
                        tt = slice(1, STEPS)
                        v.tensor_tensor(fin[0][:, :], bank[6][:, 0:CHUNK], tab_a[:, tt], ALU.mult)
                        v.tensor_tensor(fin[1][:, :], bank[6][:, 0:CHUNK], tab_b[:, tt], ALU.mult)
                        v.drain()
                        v.nop().then_inc(S["fin_read"], 1)
                        init = carry if c else start
                        for n in range(2):
                            v.tensor_tensor_scan(wst[n][:, :], p_(3).broadcast_to([P, CHUNK]), fin[n][:, :],
                                                 init[:, n:n + 1], ALU.mult, ALU.add)
                        v.drain()
                        v.tensor_tensor(fin[0][:, :], wst[0][:, :], tab_k[:, tt], ALU.mult)
                        v.tensor_tensor(fin[1][:, :], wst[1][:, :], tab_c[:, tt], ALU.mult)
                        v.drain()
                        if not (zero_a and c == 0):
                            dve.wait_ge(S["co_done"], na + c)
                        v.tensor_tensor(y[:, :], fin[0][:, :], fin[1][:, :], ALU.add).then_inc(S["y_done"], 1)
                        last = slice(CHUNK - 1, CHUNK)
                        v.tensor_scalar(carry[:, 1:2], wst[0][:, last], tab_c[:, CHUNK:STEPS], None, ALU.mult)
                        v.drain()
                        v.scalar_tensor_tensor(out=carry[:, 0:1], in0=wst[1][:, last], scalar=p_(8),
                                               in1=carry[:, 1:2], op0=ALU.mult, op1=ALU.add)
                        v.drain()
                        v.tensor_copy(carry[:, 1:2], y[:, last])

            steps(dve, step)


SC = 136
SCHUNKS = SCOLS // SC
RW = 2 * HEADS + HE
VW = HEADS + HE
GK = 89
GATE_BATCHES = [GRAPH_NODES, GRAPH_NODES + P * GK, NODES - P * GK]
FF = NT // P


def back(nc, pick, ring, table, gathered, sorted_rec, seg_scratch, h_tok, xnT, b_gat, ln_gamma, ln_beta,
         W1, b1, W2, b2, out):
    partial = nc.dram_tensor("partial", [SORTED + P, RW], f32, kind="Internal").ap()
    outputs_d = nc.dram_tensor("outputs_d", [GRAPH_NODES // NT * P, FF * HE // HEADS * CH], f32, kind="Internal").ap()
    gates = nc.dram_tensor("gates", [NODES, EXPERTS], f32, kind="Internal").ap()
    ctx = ExitStack()
    with ctx:
        def sb(name, shape, dt=f32):
            return ctx.enter_context(nc.sbuf_tensor(name, shape, dt))

        def pb(name, shape, dt=f32):
            return ctx.enter_context(nc.psum_tensor(name, shape, dt))

        def sem(name):
            return ctx.enter_context(nc.semaphore(name))

        ident = sb("ident2", [P, P])
        big = sb("big", [P, 2 * SCOLS])
        recs = big[:, :].bitcast(i32).rearrange("p (c w) -> p c w", w=2)
        st = sb("st", [P, SCOLS])
        ns = sb("ns", [P, SCOLS])
        nb = sb("nb", [P, SCOLS])
        rows = [sb(f"rows{n}", [P, SC, TW]) for n in range(2)]
        res = [sb(f"res{n}", [P, SC, RW]) for n in range(2)]
        sd = sb("sd", [P, HEADS, SC])
        ad = sb("ad", [P, HEADS, SC])
        e = sb("e", [P, HEADS, SC])
        mx = sb("mx", [P, HEADS, SC + 1])
        ex = sb("ex", [P, 2, HEADS, SC])
        msg = sb("msg", [P, HE, SC])
        cad = sb("cad", [P, HEADS])
        car = sb("car", [P, RW])
        key = sb("key", [P, SCOLS])
        cols = msg[:, :, :].rearrange("p a c -> p (a c)").bitcast(i32)
        fs = sb("fs", [P, 1])
        hs = sb("hs", [P, 1])
        partf = sb("partf", [P, 1])
        part = sb("part", [P, 1], i32)
        idx = sb("idx", [P, 4], i32)
        idxf = sb("idxf", [P, 4])
        arow = sb("arow", [P, TW])
        ends = sb("ends", [P, 3, VW])
        endsT = sb("endsT", [VW, 3, P])
        nbT = sb("nbT", [VW, P])
        mcT = sb("mcT", [VW, P + 1])
        vcT = sb("vcT", [VW, P + 1])
        exT = sb("exT", [VW, 2, P])
        cin = sb("cin", [P, 2, VW])
        fix = sb("fix", [P, RW])
        fm = sb("fm", [P, 3, VW])
        fixed = sb("fixed", [P, RW])
        seg = sb("seg", [P, P], i32)
        nidx = [sb(f"nidx{n}", [P, HALF], i32) for n in range(2)]
        nrow = [sb(f"nrow{n}", [P, HALF, RW]) for n in range(2)]
        node = rows[0][:, :, :].rearrange("p c w -> p (c w)")[:, 0:P * RW].rearrange("p (k w) -> p k w", w=RW)
        th = sb("th", [P, P, HE])
        gt = sb("gt", [P, P, HE])
        g1 = sb("g1", [P, P, HEADS])
        g2 = sb("g2", [P, P, HEADS])
        g3 = sb("g3", [P, P, HEADS])
        r1 = sb("r1", [P, P])
        r2 = sb("r2", [P, P])
        bgat = sb("bgat", [P, HE])
        gam = sb("gam", [P, HE])
        bet = sb("bet", [P, HE])
        eps2 = sb("eps2", [P, 1])
        w1 = sb("fw1", [CH, EXPERTS, HIDDEN])
        w2 = sb("fw2", [HIDDEN, EXPERTS, CH])
        fb1 = sb("fb1", [HIDDEN, EXPERTS])
        fb2 = sb("fb2", [P, EXPERTS * CH])
        xf = [sb(f"xf{n}", [CH, NT]) for n in range(2)]
        hr = [sb(f"hr{n}", [P, FF, CH]) for n in range(2)]
        gf = [sb(f"gf{n}", [P, FF, EXPERTS]) for n in range(2)]
        hh = [sb(f"hh{n}", [P, EXPERTS, NT]) for n in range(2)]
        yb = sb("yb", [P, FF, EXPERTS, CH])
        YW = FF * EXPERTS * CH
        ycopy = [key[:, n * YW:(n + 1) * YW] for n in range(2)]
        yback = [t[:, :, :].rearrange("p c w -> p (c w)")[:, 0:YW] for t in res]
        yc = sb("yc", [P, FF, 2, CH])
        yo = [sb(f"yo{n}", [P, FF, CH]) for n in range(2)]

        hid = [pb(f"hid{n}", [P, 512]) for n in range(2)]
        ybank = [pb(f"ybank{n}", [P, 1024]) for n in range(2)]
        tp = pb("tp", [P, 512])

        names = """consts in0 wts idx_ready arow_in rows0 rows1 res0 res1 ex_in ex_done ends_ready endsT_done
            cin_ready exT_in exT_done cin_done fix_in fix_ex fix_exd fixed_ready fixed_st
            ngath0 ngath1 ybank_free node_ready th_in g_sq g_std g_e g_ex gt_ready gt_st ff0 ff1 ffx0 ffx1 hid_done hh_done y_done
            yo_done out0 out1 scan_used waited
            all_gathered y_copied yst0 yst1 yin0 yin1 pick0 pick1 gath0 gath1 ring_st0 ring_st1""".split()
        S = {n: sem("b_" + n) for n in names}
        block = ctx.enter_context(nc.Block())
        sorted_v = sorted_rec.rearrange("(p c) w -> p c w", c=SCOLS)
        partial_v = partial[0:SORTED, :].rearrange("(p c) w -> p (c w)", c=SCOLS)
        rows_s = [S["rows0"], S["rows1"]]
        res_s = [S["res0"], S["res1"]]
        ff = [S["ff0"], S["ff1"]]
        ffx = [S["ffx0"], S["ffx1"]]
        ost = [S["out0"], S["out1"]]
        yst = [S["yst0"], S["yst1"]]
        yin = [S["yin0"], S["yin1"]]

        def outside_chunks(eng, step):
            with eng.Fori(0, (OUTSIDE - 1) // 2) as i:
                for q in range(2):
                    step(2 * i + q, q)
            step(OUTSIDE - 1, 0)

        def later_graph_chunks(eng, step):
            with eng.Fori(SCHUNKS // 2, GRAPH_CHUNKS // 2 - 1) as i:
                for z in range(2):
                    step(2 * i + z, z)
            for m in range(GRAPH_CHUNKS - 2, GRAPH_CHUNKS):
                step(m, m % 2)

        GRAPH_CHUNKS = GRAPH_NODES // NT
        assert (NODES - GRAPH_NODES) // NT % 2 == 0 and GRAPH_CHUNKS % 2 == 0 and GRAPH_CHUNKS > SCHUNKS
        TOTAL = (NODES - GRAPH_NODES) // NT + 1 + GRAPH_NODES // NT
        OUTSIDE = (NODES - GRAPH_NODES) // NT + 1

        @block.sync
        def _(sp):
            sp.dma_start(recs, sorted_v).then_inc(S["in0"], 16)
            sp.dma_start(seg[:, :], seg_scratch[1, :, :]).then_inc(S["in0"], 16)
            for dst, src in ((bgat[:, :], b_gat.partition_broadcast(P)), (gam[:, :], ln_gamma.partition_broadcast(P)),
                             (bet[:, :], ln_beta.partition_broadcast(P)), (fb2[:, :], b2.partition_broadcast(P)),
                             (w1[:, :, :], W1.rearrange("e c h -> c e h")), (w2[:, :, :], W2.rearrange("e h c -> h e c")),
                             (fb1[:, :], b1)):
                sp.dma_start(dst, src).then_inc(S["wts"], 16)

            for n, g0 in enumerate(GATE_BATCHES):
                if n:
                    sp.wait_ge(S["gt_st"], 16 * n)
                sp.dma_start(th[:, 0:GK, :], table[g0:g0 + P * GK, 0:HE].rearrange("(p k) w -> p k w", k=GK))\
                    .then_inc(S["th_in"], 16)
                sp.wait_ge(S["gt_ready"], n + 1)
                sp.dma_start(gates[g0:g0 + P * GK, :].rearrange("(p k) w -> p k w", k=GK), g1[:, 0:GK, :])\
                    .then_inc(S["gt_st"], 16)
            sp.wait_ge(S["gt_st"], 16 * len(GATE_BATCHES))

            def node0(k):
                return (GRAPH_NODES + k * NT if k < OUTSIDE - 1 else
                        NODES - NT if k == OUTSIDE - 1 else (k - OUTSIDE) * NT)

            def load_x(n0, q):
                sp.dma_start(xf[q][:, :], xnT[:, bass.ds(n0, NT)]).then_inc(ffx[q], 16)

            def load_h(n0, q):
                sp.dma_start(hr[q][:, :, :], h_tok[bass.ds(n0, NT), :].rearrange("(p j) c -> p j c", j=FF))\
                    .then_inc(ff[q], 16)
                sp.dma_start(gf[q][:, :, :], gates[bass.ds(n0, NT), :].rearrange("(p j) c -> p j c", j=FF))\
                    .then_inc(ff[q], 16)

            def store_ff(n0, q):
                sp.dma_start(out[bass.ds(n0, NT), :].rearrange("(p j) c -> p j c", j=FF), yo[q][:, :, :])\
                    .then_inc(ost[q], 16)

            def transfers(k, n0, q):
                sp.wait_ge(S["hid_done"], EXPERTS * k + EXPERTS)
                sp.sem_inc(S["waited"], 1)
                load_x(n0(2), q)
                sp.wait_ge(S["yo_done"], k)
                sp.sem_inc(S["waited"], 1)
                store_ff(n0(-1), 1 - q)
                load_h(n0(1), 1 - q)

            def transfer_pairs(k0, k1, first_node):
                with sp.Fori(0, (k1 - k0) // 2) as i:
                    for z in range(2):
                        transfers(2 * i + z + k0, lambda d: first_node + (2 * i + (z + k0 + d)) * NT, (z + k0) % 2)

            load_x(node0(0), 0)
            load_x(node0(1), 1)
            load_h(node0(0), 0)
            load_h(node0(1), 1)
            sp.wait_ge(S["hid_done"], EXPERTS)
            load_x(node0(2), 0)
            end = 1 + (OUTSIDE - 4) // 2 * 2
            transfer_pairs(1, end, GRAPH_NODES)
            for k in range(end, OUTSIDE + 1):
                sp.wait_ge(S["hid_done"], EXPERTS * k + EXPERTS)
                load_x(node0(k + 2), k % 2)
                sp.wait_ge(S["yo_done"], k)
                if k == OUTSIDE:
                    for z in range(2):
                        sp.wait_ge(ost[z], 16 + 16 * (OUTSIDE // 2))
                store_ff(node0(k - 1), (k - 1) % 2)
                if k + 1 < OUTSIDE:
                    load_h(node0(k + 1), (k + 1) % 2)

            def graph_transfers(m, z):
                sp.wait_ge(S["y_copied"], m + 3)
                sp.sem_inc(S["waited"], 1)
                sp.dma_start(outputs_d[bass.ds(m * P, P), :], ycopy[z]).then_inc(yst[z], 16)
                if not (isinstance(m, int) and m + 3 >= GRAPH_CHUNKS):
                    sp.wait_ge(S["hid_done"], EXPERTS * (OUTSIDE + m + 2))
                    sp.sem_inc(S["waited"], 1)
                    load_x((m + 3) * NT, z)

            sp.wait_ge(S["all_gathered"], 1)
            def load_rows(k, q):
                sp.dma_start(rows[q][:, :, :].rearrange("p c w -> p (c w)"),
                             gathered[:, bass.ds(k * SC * TW, SC * TW)]).then_inc(rows_s[q], 16)

            load_rows(0, 0)
            load_rows(1, 1)

            def store_res(k, q):
                sp.wait_ge(S["scan_used"], k + 1)
                sp.sem_inc(S["waited"], 1)
                sp.dma_start(partial_v[:, bass.ds(k * SC * RW, SC * RW)],
                             res[q][:, :, :].rearrange("p c w -> p (c w)")).then_inc(res_s[q], 16)

            with sp.Fori(0, SCHUNKS // 2 - 1) as i:
                for q in range(2):
                    graph_transfers(2 * i + q, q)
                    store_res(2 * i + q, q)
                    load_rows(2 * i + q + 2, q)
            for q in range(2):
                graph_transfers(SCHUNKS - 2 + q, q)
                store_res(SCHUNKS - 2 + q, q)

            with sp.Fori(SCHUNKS // 2, GRAPH_CHUNKS // 2 - 2) as i:
                for z in range(2):
                    graph_transfers(2 * i + z, z)
            for m in range(GRAPH_CHUNKS - 4, GRAPH_CHUNKS):
                graph_transfers(m, m % 2)
            for q in range(2):
                sp.wait_ge(yst[q], 16 + 8 * GRAPH_CHUNKS)
                sp.wait_ge(res_s[q], 16 + 16 * SCHUNKS // 2)

            sp.wait_ge(S["gt_ready"], len(GATE_BATCHES) + 1)
            sp.dma_start(gates[0:GRAPH_NODES, :].rearrange("(p k) w -> p k w", k=P), g1[:, :, :])\
                .then_inc(S["gt_st"], 16)
            sp.wait_ge(S["gt_st"], 16 * (len(GATE_BATCHES) + 1))

            def load_graph(m, z):
                sp.dma_start(yback[z], outputs_d[bass.ds(m * P, P), :]).then_inc(yin[z], 16)
                load_h(m * NT, 1 - z)

            def store_graph(m, z):
                sp.wait_ge(S["yo_done"], OUTSIDE + m + 1)
                sp.sem_inc(S["waited"], 1)
                store_ff(m * NT, 1 - z)

            load_graph(0, 0)
            load_graph(1, 1)
            with sp.Fori(0, GRAPH_CHUNKS // 2 - 1) as i:
                for z in range(2):
                    store_graph(2 * i + z, z)
                    load_graph(2 * i + z + 2, z)
            for z in range(2):
                store_graph(GRAPH_CHUNKS - 2 + z, z)
            sp.wait_ge(ost[0], 16 + 16 * ((TOTAL + 1) // 2))
            sp.wait_ge(ost[1], 16 + 16 * (TOTAL // 2))

        @block.gpsimd
        def _(pool):
            g = nc.gpsimd
            g.memset(ident[:, :], 0.0)
            g.memset(eps2[:, :], EPS)
            g.iota(cols, pattern=[[1, SCOLS]], base=0, channel_multiplier=0)
            g.iota(part[:, :], pattern=[[1, 1]], base=0, channel_multiplier=1)
            g.drain()
            g.affine_select(out=ident[:, :], in_=ident[:, :], compare_op=ALU.not_equal, fill=1.0, base=0,
                            pattern=[[-1, P]], channel_multiplier=1)
            g.drain()
            g.nop().then_inc(S["consts"], 1)
            off = bass.IndirectOffsetOnAxis
            gather_blocks(nc, pool, pick, ring, table, sorted_rec, gathered,
                          ([S["pick0"], S["pick1"]], [S["gath0"], S["gath1"]], [S["ring_st0"], S["ring_st1"]]),
                          S["waited"], FRONT_BLOCKS, BLOCKS - FRONT_BLOCKS)
            g.nop().then_inc(S["all_gathered"], 1)
            pool.wait_ge(S["idx_ready"], 1)
            g.indirect_dma_start(out=arow[:, :], out_offset=None, in_=table[0:GRAPH_NODES, :],
                                 in_offset=off(ap=idx[:, 0:1], axis=0)).then_inc(S["arow_in"], 16)
            for q in range(2):
                pool.wait_ge(res_s[q], 16 + 16 * SCHUNKS // 2)
            g.indirect_dma_start(out=fix[:, :], out_offset=None, in_=partial[0:SORTED, :],
                                 in_offset=off(ap=idx[:, 1:2], axis=0)).then_inc(S["fix_in"], 16)
            pool.wait_ge(S["fixed_ready"], 1)
            g.indirect_dma_start(out=partial, out_offset=off(ap=idx[:, 2:3], axis=0), in_=fixed[:, :],
                                 in_offset=None).then_inc(S["fixed_st"], 16)
            pool.wait_ge(S["fixed_st"], 16)
            with pool.Fori(0, SROUNDS) as i:
                for h in range(2):
                    g.tensor_copy(nidx[h][:, :], seg[:, bass.ds((2 * i + h) * HALF, HALF)])
                g.drain()
                for h in range(2):
                    for j in range(HALF):
                        g.indirect_dma_start(out=nrow[h][:, j, :], out_offset=None, in_=partial[0:SORTED, :],
                                             in_offset=off(ap=nidx[h][:, j:j + 1], axis=0))\
                            .then_inc([S["ngath0"], S["ngath1"]][h], 16)
                for h in range(2):
                    pool.wait_ge([S["ngath0"], S["ngath1"]][h], 16 * HALF * (i + 1))
                    g.tensor_copy(node[:, bass.ds((2 * i + h) * HALF, HALF), :], nrow[h][:, :, :])
                g.drain()
            g.nop().then_inc(S["node_ready"], 1)

        @block.tensor
        def _(pe):
            mm = nc.tensor.matmul
            pe.wait_ge(S["wts"], 16 * 7)

            def hidden(k, ee, q):
                if ee == 0:
                    pe.wait_ge(ffx[q], 8 * (k - q) + 16)
                wait(pe, S["hh_done"], EXPERTS * k + ee - 1)
                mm(hid[ee % 2][:, :], w1[:, ee, :], xf[q][:, :], start=True, stop=True).then_inc(S["hid_done"], 1)

            def outputs(k, j, q, m):
                if j == 0:
                    pe.wait_ge(S["hh_done"], EXPERTS * k + EXPERTS)
                    if m is None:
                        pe.wait_ge(S["ybank_free"], k + 1)
                    else:
                        pe.wait_ge(S["ybank_free"], OUTSIDE + 2)
                        pe.wait_ge(S["y_copied"], m + 1)
                for ee in range(EXPERTS):
                    o = (j * EXPERTS + ee) * CH
                    last = mm(ybank[q][:, o:o + CH], hh[q][:, ee, j:NT:FF], w2[:, ee, :], start=True, stop=True)
                if j == FF - 1:
                    last.then_inc(S["y_done"], 1)

            def step(k, q, m=None):
                for j in range(FF):
                    if not (isinstance(k, int) and k == TOTAL - 1):
                        hidden(k + 1, j, 1 - q)
                    outputs(k, j, q, m)

            def graph_step(m, z):
                step(OUTSIDE + m, 1 - z, m)

            for ee in range(EXPERTS):
                hidden(0, ee, 0)
            outside_chunks(pe, step)
            with pe.Fori(0, SCHUNKS // 2) as i:
                for z in range(2):
                    graph_step(2 * i + z, z)

            pe.wait_ge(S["ends_ready"], 1)
            for n in range(3):
                m = mm(tp[0:VW, n * P:(n + 1) * P], ends[:, n, :], ident[:, :], start=True, stop=True)
            m.then_inc(S["endsT_done"], 1)
            pe.wait_ge(S["cin_ready"], 1)
            mm(tp[:, 0:VW], mcT[:, 0:P], ident[0:VW, 0:VW], start=True, stop=True)
            mm(tp[:, VW:2 * VW], vcT[:, 0:P], ident[0:VW, 0:VW], start=True, stop=True).then_inc(S["cin_done"], 1)

            later_graph_chunks(pe, graph_step)

        @block.scalar
        def _(act):
            a = nc.scalar.activation

            def gate_fn(n, K):
                act.wait_ge(S["g_sq"], n + 1)
                a(r1[:, 0:K], r1[:, 0:K], ACT.Sqrt, scale=1.0 / HE, bias=eps2[:, :]).then_inc(S["g_std"], 1)
                act.wait_ge(S["g_e"], n + 1)
                a(g1[:, 0:K, :], g1[:, 0:K, :], ACT.Exp).then_inc(S["g_ex"], 1)

            for n in range(len(GATE_BATCHES)):
                gate_fn(n, GK)
            act.wait_ge(S["wts"], 16 * 7)

            def gelu(k, q):
                for ee in range(EXPERTS):
                    act.wait_ge(S["hid_done"], EXPERTS * k + ee + 1)
                    a(hh[q][:, ee, :], hid[ee % 2][:, :], ACT.Gelu, bias=fb1[:, ee:ee + 1]).then_inc(S["hh_done"], 1)

            def step(k, q):
                gelu(k + 1, 1 - q)

            def graph_step(m, z):
                if not (isinstance(m, int) and m == GRAPH_CHUNKS - 1):
                    gelu(OUTSIDE + m + 1, z)
                act.wait_ge(S["y_done"], OUTSIDE + m + 1)
                act.wait_ge(yst[z], 8 * (m - z) + 16)
                a(ycopy[z], ybank[1 - z][:, :], ACT.Copy).then_inc(S["y_copied"], 1)

            gelu(0, 0)
            outside_chunks(act, step)

            with act.Fori(0, SCHUNKS // 2) as i:
                for z in range(2):
                    act.wait_ge(S["ex_in"], 2 * i + z + 1)
                    a(ex[:, :, :, :], ex[:, :, :, :], ACT.Exp).then_inc(S["ex_done"], 1)
                    graph_step(2 * i + z, z)
            act.wait_ge(S["exT_in"], 1)
            a(exT[:, :, :], exT[:, :, :], ACT.Exp).then_inc(S["exT_done"], 1)
            act.wait_ge(S["fix_ex"], 1)
            a(fm[:, 0:2, :], fm[:, 0:2, :], ACT.Exp).then_inc(S["fix_exd"], 1)

            later_graph_chunks(act, graph_step)
            gate_fn(len(GATE_BATCHES), P)

        @block.vector
        def _(dve):
            v = nc.vector

            def seq(*ops):
                for op in ops:
                    op()
                    v.drain()

            dve.wait_ge(S["consts"], 1)
            v.nop().then_inc(S["ybank_free"], 2)
            for q in range(2):
                v.nop().then_inc(res_s[q], 16)
                v.nop().then_inc(ost[q], 16)
                v.nop().then_inc(yst[q], 16)
                v.nop().then_inc(S["y_copied"], 1)
            dve.wait_ge(S["in0"], 32)
            seq(lambda: v.tensor_copy(key[:, :], recs[:, :, 1]),
                lambda: v.tensor_scalar(st[:, :], key[:, :], float(FLAG), None, ALU.is_ge))
            v.tensor_scalar(ns[:, :], st[:, :], -1.0, 1.0, ALU.mult, ALU.add)
            v.tensor_scalar(nb[:, :], st[:, :], -BIG, None, ALU.mult)
            v.scalar_tensor_tensor(out=idx[:, 0:1], in0=st[:, 0:1], scalar=-float(FLAG), in1=key[:, 0:1],
                                   op0=ALU.mult, op1=ALU.add)
            v.tensor_copy(partf[:, :], part[:, :])
            v.tensor_reduce(hs[:, :], st[:, :], AX.X, ALU.max)
            v.drain()
            v.nop().then_inc(S["idx_ready"], 1)
            seq(lambda: v.tensor_copy(key[:, :], cols),
                lambda: v.scalar_tensor_tensor(out=key[:, :], in0=ns[:, :], scalar=float(SCOLS), in1=key[:, :],
                                               op0=ALU.mult, op1=ALU.add),
                lambda: v.tensor_reduce(fs[:, :], key[:, :], AX.X, ALU.min),
                lambda: v.tensor_scalar(idxf[:, 3:4], fs[:, :], 0.0, None, ALU.is_equal),
                lambda: v.scalar_tensor_tensor(out=idxf[:, 0:1], in0=partf[:, :], scalar=float(SCOLS), in1=fs[:, :],
                                               op0=ALU.mult, op1=ALU.add),
                lambda: v.tensor_tensor(idxf[:, 1:2], idxf[:, 0:1], idxf[:, 3:4], ALU.add),
                lambda: v.tensor_scalar(idxf[:, 1:2], idxf[:, 1:2], -1.0, None, ALU.add),
                lambda: v.tensor_scalar(idxf[:, 2:3], partf[:, :], float(SORTED), None, ALU.add),
                lambda: v.tensor_tensor(idxf[:, 2:3], idxf[:, 2:3], idxf[:, 1:2], ALU.subtract),
                lambda: v.scalar_tensor_tensor(out=idxf[:, 2:3], in0=idxf[:, 2:3], scalar=idxf[:, 3:4],
                                               in1=idxf[:, 1:2], op0=ALU.mult, op1=ALU.add),
                lambda: v.tensor_copy(idx[:, 1:3], idxf[:, 1:3]),
                lambda: v.memset(car[:, :], 0.0),
                lambda: v.memset(car[:, 0:HEADS], -BIG))
            def bc(t, K):
                return t[:, :].unsqueeze(1).broadcast_to([P, K, HE])

            def gate_fn(n, K):
                T = th[:, 0:K, :]
                G = gt[:, 0:K, :]
                R = r1[:, 0:K]
                W = r2[:, 0:K]
                A1, A2, A3 = g1[:, 0:K, :], g2[:, 0:K, :], g3[:, 0:K, :]
                seq(lambda: v.tensor_tensor(T, T, bc(bgat, K), ALU.add),
                    lambda: v.tensor_reduce(R, T, AX.X, ALU.add),
                    lambda: v.tensor_scalar(R, R, 1.0 / HE, None, ALU.mult),
                    lambda: v.tensor_tensor(T, T, R.unsqueeze(2).broadcast_to([P, K, HE]), ALU.subtract),
                    lambda: v.tensor_tensor(G, T, T, ALU.mult),
                    lambda: v.tensor_reduce(R, G, AX.X, ALU.add))
                v.nop().then_inc(S["g_sq"], 1)
                dve.wait_ge(S["g_std"], n + 1)
                seq(lambda: v.reciprocal(R, R),
                    lambda: v.tensor_tensor(T, T, R.unsqueeze(2).broadcast_to([P, K, HE]), ALU.mult),
                    lambda: v.tensor_tensor(T, T, bc(gam, K), ALU.mult),
                    lambda: v.tensor_tensor(T, T, bc(bet, K), ALU.add),
                    lambda: v.tensor_tensor(A2, T[:, :, 0:4], T[:, :, 4:8], ALU.add),
                    lambda: v.tensor_tensor(A2, A2, T[:, :, 8:12], ALU.add),
                    lambda: v.tensor_tensor(A2, A2, T[:, :, 12:16], ALU.add),
                    lambda: v.tensor_scalar(A2, A2, 1.0 / HEADS, None, ALU.mult),
                    lambda: v.memset(A3, 0.0))
                for i in range(EXPERTS):
                    for j in range(i + 1, EXPERTS):
                        seq(lambda: v.tensor_tensor(W, A2[:, :, i], A2[:, :, j], ALU.is_ge),
                            lambda: v.tensor_tensor(A3[:, :, j], A3[:, :, j], W, ALU.add),
                            lambda: v.tensor_scalar(W, W, -1.0, 1.0, ALU.mult, ALU.add),
                            lambda: v.tensor_tensor(A3[:, :, i], A3[:, :, i], W, ALU.add))
                seq(lambda: v.tensor_scalar(A3, A3, 2.0, None, ALU.is_lt),
                    lambda: v.tensor_reduce(R, A2, AX.X, ALU.max))
                if n:
                    dve.wait_ge(S["gt_st"], 16 * n)
                seq(lambda: v.tensor_tensor(A1, A2, R.unsqueeze(2).broadcast_to([P, K, EXPERTS]), ALU.subtract))
                v.nop().then_inc(S["g_e"], 1)
                dve.wait_ge(S["g_ex"], n + 1)
                seq(lambda: v.tensor_tensor(A1, A1, A3, ALU.mult),
                    lambda: v.tensor_reduce(R, A1, AX.X, ALU.add),
                    lambda: v.reciprocal(R, R),
                    lambda: v.tensor_tensor(A1, A1, R.unsqueeze(2).broadcast_to([P, K, EXPERTS]), ALU.mult))
                v.nop().then_inc(S["gt_ready"], 1)

            dve.wait_ge(S["wts"], 16 * 7)
            for n in range(len(GATE_BATCHES)):
                dve.wait_ge(S["th_in"], 16 * (n + 1))
                gate_fn(n, GK)

            def combine(k, q, y):
                Y = yb[:, :, :, :].rearrange("p j e c -> p j (e c)")
                v.tensor_tensor(Y, y.rearrange("p (j n) -> p j n", j=FF),
                                       fb2[:, :].unsqueeze(1).broadcast_to([P, FF, EXPERTS * CH]), ALU.add).then_inc(S["ybank_free"], 1)
                v.drain()
                dve.wait_ge(ff[q], 16 * (k - q) + 32)
                v.tensor_tensor(yb[:, :, :, :].rearrange("p j e c -> p (j e) c"),
                                yb[:, :, :, :].rearrange("p j e c -> p (j e) c"),
                                gf[q][:, :, :].rearrange("p j e -> p (j e)").unsqueeze(2)
                                .broadcast_to([P, FF * EXPERTS, CH]), ALU.mult)
                v.drain()
                v.tensor_tensor(yc[:, :, :, :], yb[:, :, 0:2, :], yb[:, :, 2:4, :], ALU.add)
                v.drain()
                v.tensor_tensor(yc[:, :, 0, :], yc[:, :, 0, :], yc[:, :, 1, :], ALU.add)
                v.drain()
                dve.wait_ge(ost[q], 8 * (k - q) + 16)
                v.tensor_tensor(yo[q][:, :, :], yc[:, :, 0, :], hr[q][:, :, :], ALU.add).then_inc(S["yo_done"], 1)

            def step(k, q):
                dve.wait_ge(S["y_done"], k + 1)
                combine(k, q, ybank[q][:, :])

            outside_chunks(dve, step)

            dve.wait_ge(S["arow_in"], 16)
            seq(lambda: v.tensor_copy(cad[:, :], arow[:, HE + HEADS:TW]))

            with dve.Fori(0, SCHUNKS // 2) as i:
                for q in range(2):
                    k = 2 * i + q
                    dve.wait_ge(rows_s[q], 16 * (i + 1))
                    rv = rows[q][:, :, :].rearrange("p c w -> p w c")
                    ov = res[q][:, :, :].rearrange("p c w -> p w c")
                    cs = bass.ds(k * SC, SC)

                    def flag(t, n=HEADS):
                        return t[:, cs].unsqueeze(1).broadcast_to([P, n, SC])

                    seq(lambda: v.tensor_tensor(sd[:, :, :], rv[:, HE + HEADS:TW, :], flag(st), ALU.mult))
                    for h in range(HEADS):
                        v.tensor_tensor_scan(ad[:, h, :], ns[:, cs], sd[:, h, :], cad[:, h:h + 1], ALU.mult, ALU.add)
                    v.tensor_copy(mx[:, :, 0], car[:, 0:HEADS])
                    v.drain()
                    v.tensor_copy(cad[:, :], ad[:, :, SC - 1])
                    seq(lambda: v.tensor_tensor(e[:, :, :], rv[:, HE:HE + HEADS, :], ad[:, :, :], ALU.add),
                        lambda: v.scalar_tensor_tensor(out=e[:, :, :], in0=e[:, :, :], scalar=0.2, in1=e[:, :, :],
                                                       op0=ALU.mult, op1=ALU.max))
                    for h in range(HEADS):
                        v.tensor_tensor_scan(mx[:, h, 1:SC + 1], nb[:, cs], e[:, h, :], car[:, h:h + 1],
                                             ALU.add, ALU.max)
                    v.drain()
                    v.tensor_tensor(ex[:, 0, :, :], mx[:, :, 0:SC], mx[:, :, 1:SC + 1], ALU.subtract)
                    v.tensor_tensor(ex[:, 1, :, :], e[:, :, :], mx[:, :, 1:SC + 1], ALU.subtract)
                    v.drain()
                    v.tensor_scalar(ex[:, 0, :, :], ex[:, 0, :, :], 0.0, None, ALU.min).then_inc(S["ex_in"], 1)
                    dve.wait_ge(S["ex_done"], k + 1)
                    v.tensor_tensor(ex[:, 0, :, :], ex[:, 0, :, :], flag(ns), ALU.mult)
                    for h in range(HEADS):
                        v.tensor_tensor(msg[:, h * EXPERTS:(h + 1) * EXPERTS, :],
                                        rv[:, h * EXPERTS:(h + 1) * EXPERTS, :],
                                        ex[:, 1, h, :].unsqueeze(1).broadcast_to([P, EXPERTS, SC]), ALU.mult)
                    v.drain()
                    dve.wait_ge(res_s[q], 16 * i + 16)
                    v.tensor_copy(ov[:, 0:HEADS, :], mx[:, :, 1:SC + 1])
                    for h in range(HEADS):
                        v.tensor_tensor_scan(ov[:, HEADS + h, :], ex[:, 0, h, :], ex[:, 1, h, :],
                                             car[:, HEADS + h:HEADS + h + 1], ALU.mult, ALU.add)
                        for x_ in range(EXPERTS):
                            w = h * EXPERTS + x_
                            v.tensor_tensor_scan(ov[:, 2 * HEADS + w, :], ex[:, 0, h, :], msg[:, w, :],
                                                 car[:, 2 * HEADS + w:2 * HEADS + w + 1], ALU.mult, ALU.add)
                    v.drain()
                    v.tensor_copy(car[:, :], res[q][:, SC - 1, :])
                    v.drain()
                    v.nop().then_inc(S["scan_used"], 1)

            v.tensor_copy(ends[:, 0, 0:HEADS], car[:, 0:HEADS])
            v.tensor_copy(ends[:, 0, HEADS:VW].rearrange("p (h x) -> p h x", x=EXPERTS),
                          car[:, 0:HEADS].unsqueeze(2).broadcast_to([P, HEADS, EXPERTS]))
            v.tensor_copy(ends[:, 1, :], car[:, HEADS:RW])
            v.tensor_scalar(ends[:, 2, :], hs[:, 0:1].broadcast_to([P, VW]), -1.0, 1.0, ALU.mult, ALU.add)
            v.drain()
            v.nop().then_inc(S["ends_ready"], 1)
            dve.wait_ge(S["endsT_done"], 1)
            v.tensor_copy(endsT[:, :, :].rearrange("p a b -> p (a b)"), tp[0:VW, 0:3 * P])
            v.memset(mcT[:, 0:1], -BIG)
            v.memset(vcT[:, 0:1], 0.0)
            v.drain()
            seq(lambda: v.tensor_scalar(nbT[:, :], endsT[:, 2, :], 1.0, BIG, ALU.subtract, ALU.mult),
                lambda: v.tensor_tensor_scan(mcT[:, 1:P + 1], nbT[:, :], endsT[:, 0, :], -BIG, ALU.add, ALU.max),
                lambda: v.tensor_tensor(exT[:, 0, :], mcT[:, 0:P], mcT[:, 1:P + 1], ALU.subtract),
                lambda: v.tensor_scalar(exT[:, 0, :], exT[:, 0, :], 0.0, None, ALU.min),
                lambda: v.tensor_tensor(exT[:, 1, :], endsT[:, 0, :], mcT[:, 1:P + 1], ALU.subtract))
            v.nop().then_inc(S["exT_in"], 1)
            dve.wait_ge(S["exT_done"], 1)
            seq(lambda: v.tensor_tensor(exT[:, 0, :], exT[:, 0, :], endsT[:, 2, :], ALU.mult),
                lambda: v.tensor_tensor(endsT[:, 1, :], exT[:, 1, :], endsT[:, 1, :], ALU.mult),
                lambda: v.tensor_tensor_scan(vcT[:, 1:P + 1], exT[:, 0, :], endsT[:, 1, :], 0.0, ALU.mult, ALU.add))
            v.nop().then_inc(S["cin_ready"], 1)
            dve.wait_ge(S["cin_done"], 1)
            seq(lambda: v.tensor_copy(cin[:, :, :].rearrange("p a b -> p (a b)"), tp[:, 0:2 * VW]))
            dve.wait_ge(S["fix_in"], 16)
            v.tensor_copy(fm[:, 0, 0:HEADS], fix[:, 0:HEADS])
            v.tensor_copy(fm[:, 0, HEADS:VW].rearrange("p (h x) -> p h x", x=EXPERTS),
                          fix[:, 0:HEADS].unsqueeze(2).broadcast_to([P, HEADS, EXPERTS]))
            v.drain()
            seq(lambda: v.tensor_tensor(fm[:, 2, :], fm[:, 0, :], cin[:, 0, :], ALU.max),
                lambda: v.tensor_copy(fixed[:, 0:HEADS], fm[:, 2, 0:HEADS]),
                lambda: v.tensor_tensor(fm[:, 0, :], fm[:, 0, :], fm[:, 2, :], ALU.subtract),
                lambda: v.tensor_tensor(fm[:, 1, :], cin[:, 0, :], fm[:, 2, :], ALU.subtract))
            v.nop().then_inc(S["fix_ex"], 1)
            dve.wait_ge(S["fix_exd"], 1)
            seq(lambda: v.tensor_tensor(fm[:, 0, :], fm[:, 0, :], fix[:, HEADS:RW], ALU.mult),
                lambda: v.tensor_tensor(fm[:, 1, :], fm[:, 1, :], cin[:, 1, :], ALU.mult),
                lambda: v.tensor_tensor(fixed[:, HEADS:RW], fm[:, 0, :], fm[:, 1, :], ALU.add))
            v.nop().then_inc(S["fixed_ready"], 1)

            dve.wait_ge(S["node_ready"], 1)
            seq(lambda: v.tensor_scalar(g2[:, :, :], node[:, :, HEADS:2 * HEADS], DENOM_EPS, None, ALU.add),
                lambda: v.reciprocal(g2[:, :, :], g2[:, :, :]))
            for h in range(HEADS):
                v.tensor_tensor(th[:, :, h * EXPERTS:(h + 1) * EXPERTS],
                                node[:, :, 2 * HEADS + h * EXPERTS:2 * HEADS + (h + 1) * EXPERTS],
                                g2[:, :, h:h + 1].broadcast_to([P, P, EXPERTS]), ALU.mult)
            v.drain()
            gate_fn(len(GATE_BATCHES), P)
            with dve.Fori(0, GRAPH_CHUNKS // 2) as i:
                for z in range(2):
                    dve.wait_ge(yin[z], 16 * (i + 1))
                    combine(OUTSIDE + 2 * i + z, 1 - z, yback[z])


_TAP_ORDER = [t for ts in TAP_TILES for t in ts]


def kernel(**inputs):
    import numpy as np
    import concourse.bacc as bacc
    from concourse.bass_utils import run_bass_kernel_spmd

    g = {k: np.asarray(v) for k, v in inputs.items()}

    def by_tap(w):
        r = w.reshape(CH, TAPS, -1).transpose(1, 0, 2)[_TAP_ORDER]
        return np.ascontiguousarray(r.reshape(TAPS * CH, -1))

    col = lambda a: np.ascontiguousarray(a.reshape(-1, 1))
    row = lambda a: np.ascontiguousarray(a.reshape(1, -1))
    arrays = {
        "x": g["x"], "cls_tok": col(g["cls_tok"]),
        "tok_W1": by_tap(g["L0_tok_W1"]), "tok_b1": col(g["L0_tok_b1"]),
        "tok_W2": np.ascontiguousarray(by_tap(np.ascontiguousarray(g["L0_tok_W2"].T)).T),
        "tok_b2": by_tap(col(g["L0_tok_b2"])),
        "tok_W3": by_tap(g["L0_tok_W3"]), "tok_b3": col(g["L0_tok_b3"]),
        "A_diag": col(g["L0_attn_A_diag"]),
        "B": np.ascontiguousarray(g["L0_attn_B"].transpose(1, 2, 0).reshape(CH, 2 * CH)),
        "C": np.ascontiguousarray(g["L0_attn_C"].transpose(2, 1, 0).reshape(2 * CH, CH)),
        "D": col(g["L0_attn_D"]), "dt": col(g["L0_attn_dt"]),
        "W_gat": g["L0_ffn_W_gat"], "att_src": row(g["L0_ffn_att_src"]), "att_dst": row(g["L0_ffn_att_dst"]),
        "b_gat": row(g["L0_ffn_b_gat"]), "ln_gamma": row(g["L0_ffn_ln_gamma"]),
        "ln_beta": row(g["L0_ffn_ln_beta"]), "W1": g["L0_ffn_W1"],
        "b1": np.ascontiguousarray(g["L0_ffn_b1"].T), "W2": g["L0_ffn_W2"], "b2": row(g["L0_ffn_b2"]),
        "edges": g["L0_ffn_edge_index"],
    }
    nc = bacc.Bacc("TRN2", target_bir_lowering=False, num_devices=1)
    args = [nc.dram_tensor("in_" + k, a.shape, mybir.dt.from_np(a.dtype), kind="ExternalInput").ap()
            for k, a in arrays.items()]
    args.append(nc.dram_tensor("out", [NODES, CH], f32, kind="ExternalOutput").ap())
    build(nc, *args)
    r = run_bass_kernel_spmd(nc, [{"in_" + k: a for k, a in arrays.items()}], core_ids=[0])
    return r.results[0]["out"].reshape(IMAGES, SEQ, CH)
```
